# Optimizing a Trainium2 kernel written in Bass

```python
import numpy as np
import jax
import jax.numpy as jnp

def _softmax(x, axis=-1):
    return jax.nn.softmax(x, axis=axis)

def _gelu(x):
    return jax.nn.gelu(x, approximate=True)

def _silu(x):
    return jax.nn.silu(x)

def _sigmoid(x):
    return jax.nn.sigmoid(x)

def _layernorm(x, axis=-1, eps=1e-05):
    m = jnp.mean(x, axis=axis, keepdims=True)
    v = jnp.var(x, axis=axis, keepdims=True)
    return (x - m) / jnp.sqrt(v + eps)

def _scatter_add(tgt, idx, src, axis=0):
    return tgt.at[idx].add(src)

def _segment_sum(src, seg, n):
    return jax.ops.segment_sum(src, seg, n)
kernel_name = 'mk_pixart_resid_d4_seqx_r4_af641b'

def setup_inputs(seed: int=0):
    np.random.seed(seed)
    _w = jnp.asarray

    def _rec_inputs():
        import jax
        import jax.numpy as jnp
        _rk = jax.random.key(seed)
        x = -0.0002928 + 1 * jax.random.normal(jax.random.fold_in(_rk, 1), (32, 128, 256), jnp.float32)
        _lenS = 128 - jax.random.randint(jax.random.fold_in(_rk, 7), (32,), 0, max(1, 128 // 4) + 1, jnp.int32)
        _lenS2 = 128 - jax.random.randint(jax.random.fold_in(_rk, 8), (32,), 0, max(1, 128 // 4) + 1, jnp.int32)
        _ctx_1024P = jax.random.normal(jax.random.fold_in(_rk, 11), (32, 16, 256), jnp.float32)
        _ctx_1024c = jax.random.dirichlet(jax.random.fold_in(_rk, 511), 0.3 * jnp.ones((16,), jnp.float32), (32, 128))
        _ctx_1024t = jnp.einsum('bsk,bkd->bsd', _ctx_1024c, _ctx_1024P)
        _ctx_1024t = _ctx_1024t * jax.lax.rsqrt(jnp.mean(jnp.square(_ctx_1024t)) + 1e-12) * 0.953939
        ctx_1024 = -1.39393e-06 + 0.999914 * (_ctx_1024t + 0.3 * jax.random.normal(jax.random.fold_in(_rk, 611), (32, 128, 256), jnp.float32))
        condB_tau = jax.random.uniform(jax.random.fold_in(_rk, 12), (32,), jnp.float32, 0.0, 1.23395)
        fside_BxS2_0 = -0.00205293 + 0.99739 * jax.random.normal(jax.random.fold_in(_rk, 13), (32, 128), jnp.float32)
        condB_pt = jax.random.uniform(jax.random.fold_in(_rk, 15), (32,), jnp.float32, 0.0, 226.919)
        return (x, ctx_1024, condB_tau, fside_BxS2_0, condB_pt, _lenS2)
    x, ctx_1024, condB_tau, fside_BxS2_0, condB_pt, _lenS2 = _rec_inputs()

    def _L0_xcond_setup():
        import jax, jax.numpy as jnp
        import numpy as np
        B, S, D, H = (2, 512, 256, 16)
        DK = D // H

        def _split_heads(x):
            b, s, _ = x.shape
            return x.reshape(b, s, H, DK).transpose(0, 2, 1, 3)
        key = jax.random.key(seed)
        ks = jax.random.split(key, 14)
        inp = {'query': jax.random.normal(ks[0], (B, S, D), jnp.float32), 'key': jax.random.normal(ks[1], (B, S, D), jnp.float32), 'value': jax.random.normal(ks[2], (B, S, D), jnp.float32), 'tau': jax.random.uniform(ks[3], (B, 1), jnp.float32, 0.5, 1.5), 'delta': jax.random.normal(ks[4], (B, S), jnp.float32)}
        sc = 1.0 / np.sqrt(D)
        for i, name in enumerate(['q', 'k', 'v', 'o']):
            inp[f'W{name}'] = jax.random.normal(ks[5 + 2 * i], (D, D), jnp.float32) * sc
            inp[f'b{name}'] = jax.random.normal(ks[6 + 2 * i], (D,), jnp.float32) * 0.01
        return inp
    _L0_xcond_all = _L0_xcond_setup()
    _L0_xcond_in = {k: v for k, v in _L0_xcond_all.items() if k in ('Wq', 'bq', 'Wk', 'bk', 'Wv', 'bv', 'Wo', 'bo')}
    del _L0_xcond_all

    def _L0_ffn_setup():
        import jax, jax.numpy as jnp
        import numpy as np
        NUM_EXPERTS = 8
        CAP_FACTOR = 1.0
        MIN_CAP = 8
        key = jax.random.key(seed)
        ks = jax.random.split(key, 10)
        G, S, D, H, E = (4, 1024, 256, 1024, NUM_EXPERTS)
        s = 0.02
        return {'x': jax.random.normal(ks[0], (G, S, D), dtype=jnp.float32), 'gate': jax.random.normal(ks[1], (D, E), dtype=jnp.float32) * s, 'W1': jax.random.normal(ks[2], (E, D, H), dtype=jnp.float32) * s, 'b1': jnp.zeros((E, H), dtype=jnp.float32), 'W2': jax.random.normal(ks[3], (E, H, D), dtype=jnp.float32) * s, 'b2': jnp.zeros((E, D), dtype=jnp.float32), 'Ws1': jax.random.normal(ks[4], (D, H), dtype=jnp.float32) * s, 'bs1': jnp.zeros((H,), dtype=jnp.float32), 'Ws2': jax.random.normal(ks[5], (H, D), dtype=jnp.float32) * s, 'bs2': jnp.zeros((D,), dtype=jnp.float32)}
    _L0_ffn_all = _L0_ffn_setup()
    _L0_ffn_in = {k: v for k, v in _L0_ffn_all.items() if k in ('gate', 'W1', 'b1', 'W2', 'b2', 'Ws1', 'bs1', 'Ws2', 'bs2')}
    del _L0_ffn_all

    def _L1_xcond_setup():
        import jax, jax.numpy as jnp
        import numpy as np
        D_MODEL = 256
        N_HEADS = 16
        key = jax.random.key(seed)
        ks = jax.random.split(key, 16)
        B, L, S, D = (4, 512, 512, D_MODEL)
        inp = {'q': jax.random.normal(ks[0], (B, L, D), jnp.float32), 'k': jax.random.normal(ks[1], (B, S, D), jnp.float32), 'v': jax.random.normal(ks[2], (B, S, D), jnp.float32), 'tau': jax.random.uniform(ks[3], (B, 1), jnp.float32, 0.5, 1.5), 'delta': jax.random.normal(ks[4], (B, S), jnp.float32)}
        s = 1.0 / np.sqrt(D)
        inp['Wq'] = jax.random.normal(ks[5], (D, D), jnp.float32) * s
        inp['bq'] = jnp.zeros((D,), jnp.float32)
        inp['Wk'] = jax.random.normal(ks[6], (D, D), jnp.float32) * s
        inp['bk'] = jnp.zeros((D,), jnp.float32)
        inp['Wv'] = jax.random.normal(ks[7], (D, D), jnp.float32) * s
        inp['bv'] = jnp.zeros((D,), jnp.float32)
        inp['Wo'] = jax.random.normal(ks[8], (D, D), jnp.float32) * s
        inp['bo'] = jnp.zeros((D,), jnp.float32)
        return inp
    _L1_xcond_all = _L1_xcond_setup()
    _L1_xcond_in = {k: v for k, v in _L1_xcond_all.items() if k in ('Wq', 'bq', 'Wk', 'bk', 'Wv', 'bv', 'Wo', 'bo')}
    del _L1_xcond_all

    def _L1_ffn_setup():
        import jax, jax.numpy as jnp
        import numpy as np
        HIDDEN = 256
        INNER = 1024

        def _weight_quant(w):
            scale = 1.0 / jnp.clip(jnp.mean(jnp.abs(w)), 1e-05)
            wq = jnp.clip(jnp.round(w * scale), -1.0, 1.0) / scale
            return w + jax.lax.stop_gradient(wq - w)

        def _act_quant(x):
            scale = 127.0 / jnp.clip(jnp.max(jnp.abs(x), axis=-1, keepdims=True), 1e-05)
            xq = jnp.clip(jnp.round(x * scale), -128.0, 127.0) / scale
            return x + jax.lax.stop_gradient(xq - x)

        def _bitlinear(x, w):
            return jnp.einsum('bsi,oi->bso', _act_quant(x), _weight_quant(w))
        key = jax.random.key(seed)
        k0, k1, k2, k3 = jax.random.split(key, 4)
        x = jax.random.normal(k0, (4, 512, HIDDEN), dtype=jnp.float32)
        w_gate = jax.random.normal(k1, (INNER, HIDDEN), dtype=jnp.float32) / np.sqrt(HIDDEN)
        w_up = jax.random.normal(k2, (INNER, HIDDEN), dtype=jnp.float32) / np.sqrt(HIDDEN)
        w_down = jax.random.normal(k3, (HIDDEN, INNER), dtype=jnp.float32) / np.sqrt(INNER)
        return {'x': x, 'w_gate': w_gate, 'w_up': w_up, 'w_down': w_down}
    _L1_ffn_all = _L1_ffn_setup()
    _L1_ffn_in = {k: v for k, v in _L1_ffn_all.items() if k in ('w_gate', 'w_up', 'w_down')}
    del _L1_ffn_all

    def _L2_xcond_setup():
        import jax, jax.numpy as jnp
        import numpy as np
        N, L, H, Q = (64, 258, 256, 64)
        WINDOW = 16.0
        DEV_POW = 128.0
        key = jax.random.key(seed)
        k1, k2, k3, k4, k5, k6 = jax.random.split(key, 6)
        encoder_outputs = jax.random.normal(k1, (N, L, H), dtype=jnp.float32)
        decoder_h_t = jax.random.normal(k2, (N, Q, H), dtype=jnp.float32)
        src_len = jax.random.randint(k3, (N,), 32, L + 1).astype(jnp.int32)
        p_t = jax.random.uniform(k4, (N,), dtype=jnp.float32) * (src_len.astype(jnp.float32) - 1.0)
        W_a = jax.random.normal(k5, (H, H), dtype=jnp.float32) * (1.0 / np.sqrt(H))
        W_c = jax.random.normal(k6, (H, 2 * H), dtype=jnp.float32) * (1.0 / np.sqrt(2 * H))
        return {'encoder_outputs': encoder_outputs, 'decoder_h_t': decoder_h_t, 'src_len': src_len, 'p_t': p_t, 'W_a': W_a, 'W_c': W_c}
    _L2_xcond_all = _L2_xcond_setup()
    _L2_xcond_in = {k: v for k, v in _L2_xcond_all.items() if k in ('W_a', 'W_c')}
    del _L2_xcond_all

    def _L2_ffn_setup():
        import jax, jax.numpy as jnp
        import numpy as np
        B, S, H = (2, 256, 256)
        KD, NH, K = (128, 8, 8)
        NE = 16384
        NK = 64
        EPS = 1e-05
        key = jax.random.key(seed)
        ks = jax.random.split(key, 5)
        inputs = jax.random.normal(ks[0], (B, S, H), jnp.float32)
        bn_gamma = jnp.ones((H,), jnp.float32)
        bn_beta = jnp.zeros((H,), jnp.float32)
        w_q = jax.random.normal(ks[1], (2 * NH * KD, H), jnp.float32) * (1.0 / np.sqrt(H))
        keys_p = jax.random.normal(ks[2], (NH, NK, 2, KD), jnp.float32) * 0.02
        lim = float(np.sqrt(6.0 / (NE + H)))
        down = jax.random.uniform(ks[3], (NE, H), jnp.float32, -lim, lim)
        up = jax.random.uniform(ks[4], (NE, H), jnp.float32, -lim, lim)
        return {'inputs': inputs, 'bn_gamma': bn_gamma, 'bn_beta': bn_beta, 'w_q': w_q, 'keys_p': keys_p, 'down': down, 'up': up}
    _L2_ffn_all = _L2_ffn_setup()
    _L2_ffn_in = {k: v for k, v in _L2_ffn_all.items() if k in ('bn_gamma', 'bn_beta', 'w_q', 'keys_p', 'down', 'up')}
    del _L2_ffn_all

    def _L3_xcond_setup():
        import jax, jax.numpy as jnp
        import numpy as np
        D_MODEL = 256
        N_HEADS = 16
        key = jax.random.key(seed)
        ks = jax.random.split(key, 16)
        B, L, S, D = (4, 512, 512, D_MODEL)
        inp = {'q': jax.random.normal(ks[0], (B, L, D), jnp.float32), 'k': jax.random.normal(ks[1], (B, S, D), jnp.float32), 'v': jax.random.normal(ks[2], (B, S, D), jnp.float32), 'tau': jax.random.uniform(ks[3], (B, 1), jnp.float32, 0.5, 1.5), 'delta': jax.random.normal(ks[4], (B, S), jnp.float32)}
        s = 1.0 / np.sqrt(D)
        inp['Wq'] = jax.random.normal(ks[5], (D, D), jnp.float32) * s
        inp['bq'] = jnp.zeros((D,), jnp.float32)
        inp['Wk'] = jax.random.normal(ks[6], (D, D), jnp.float32) * s
        inp['bk'] = jnp.zeros((D,), jnp.float32)
        inp['Wv'] = jax.random.normal(ks[7], (D, D), jnp.float32) * s
        inp['bv'] = jnp.zeros((D,), jnp.float32)
        inp['Wo'] = jax.random.normal(ks[8], (D, D), jnp.float32) * s
        inp['bo'] = jnp.zeros((D,), jnp.float32)
        return inp
    _L3_xcond_all = _L3_xcond_setup()
    _L3_xcond_in = {k: v for k, v in _L3_xcond_all.items() if k in ('Wq', 'bq', 'Wk', 'bk', 'Wv', 'bv', 'Wo', 'bo')}
    del _L3_xcond_all

    def _L3_ffn_setup():
        import jax, jax.numpy as jnp
        import numpy as np
        NUM_EXPERTS = 8
        TOP_K = 2
        N_EMBD = 256
        B, T = (4, 512)
        key = jax.random.key(seed)
        k_x, k_g, k_e = jax.random.split(key, 3)
        x = jax.random.normal(k_x, (B, T, N_EMBD), dtype=jnp.float32)
        scale = 1.0 / np.sqrt(N_EMBD)
        gate_w = jax.random.uniform(k_g, (NUM_EXPERTS, N_EMBD), dtype=jnp.float32, minval=-scale, maxval=scale)
        expert_w = jax.random.uniform(k_e, (NUM_EXPERTS, N_EMBD, N_EMBD), dtype=jnp.float32, minval=-scale, maxval=scale)
        return {'x': x, 'gate_w': gate_w, 'expert_w': expert_w}
    _L3_ffn_all = _L3_ffn_setup()
    _L3_ffn_in = {k: v for k, v in _L3_ffn_all.items() if k in ('gate_w', 'expert_w')}
    del _L3_ffn_all
    return {'x': x, 'ctx_1024': ctx_1024, 'condB_tau': condB_tau, 'fside_BxS2_0': fside_BxS2_0, 'condB_pt': condB_pt, '_lenS2': _lenS2, 'L0_xcond_Wq': _L0_xcond_in['Wq'], 'L0_xcond_bq': _L0_xcond_in['bq'], 'L0_xcond_Wk': _L0_xcond_in['Wk'], 'L0_xcond_bk': _L0_xcond_in['bk'], 'L0_xcond_Wv': _L0_xcond_in['Wv'], 'L0_xcond_bv': _L0_xcond_in['bv'], 'L0_xcond_Wo': _L0_xcond_in['Wo'], 'L0_xcond_bo': _L0_xcond_in['bo'], 'L0_ffn_gate': _L0_ffn_in['gate'], 'L0_ffn_W1': _L0_ffn_in['W1'], 'L0_ffn_b1': _L0_ffn_in['b1'], 'L0_ffn_W2': _L0_ffn_in['W2'], 'L0_ffn_b2': _L0_ffn_in['b2'], 'L0_ffn_Ws1': _L0_ffn_in['Ws1'], 'L0_ffn_bs1': _L0_ffn_in['bs1'], 'L0_ffn_Ws2': _L0_ffn_in['Ws2'], 'L0_ffn_bs2': _L0_ffn_in['bs2'], 'L1_xcond_Wq': _L1_xcond_in['Wq'], 'L1_xcond_bq': _L1_xcond_in['bq'], 'L1_xcond_Wk': _L1_xcond_in['Wk'], 'L1_xcond_bk': _L1_xcond_in['bk'], 'L1_xcond_Wv': _L1_xcond_in['Wv'], 'L1_xcond_bv': _L1_xcond_in['bv'], 'L1_xcond_Wo': _L1_xcond_in['Wo'], 'L1_xcond_bo': _L1_xcond_in['bo'], 'L1_ffn_w_gate': _L1_ffn_in['w_gate'], 'L1_ffn_w_up': _L1_ffn_in['w_up'], 'L1_ffn_w_down': _L1_ffn_in['w_down'], 'L2_xcond_W_a': _L2_xcond_in['W_a'], 'L2_xcond_W_c': _L2_xcond_in['W_c'], 'L2_ffn_bn_gamma': _L2_ffn_in['bn_gamma'], 'L2_ffn_bn_beta': _L2_ffn_in['bn_beta'], 'L2_ffn_w_q': _L2_ffn_in['w_q'], 'L2_ffn_keys_p': _L2_ffn_in['keys_p'], 'L2_ffn_down': _L2_ffn_in['down'], 'L2_ffn_up': _L2_ffn_in['up'], 'L3_xcond_Wq': _L3_xcond_in['Wq'], 'L3_xcond_bq': _L3_xcond_in['bq'], 'L3_xcond_Wk': _L3_xcond_in['Wk'], 'L3_xcond_bk': _L3_xcond_in['bk'], 'L3_xcond_Wv': _L3_xcond_in['Wv'], 'L3_xcond_bv': _L3_xcond_in['bv'], 'L3_xcond_Wo': _L3_xcond_in['Wo'], 'L3_xcond_bo': _L3_xcond_in['bo'], 'L3_ffn_gate_w': _L3_ffn_in['gate_w'], 'L3_ffn_expert_w': _L3_ffn_in['expert_w']}

def reference(x, ctx_1024, condB_tau, fside_BxS2_0, condB_pt, _lenS2, L0_xcond_Wq, L0_xcond_bq, L0_xcond_Wk, L0_xcond_bk, L0_xcond_Wv, L0_xcond_bv, L0_xcond_Wo, L0_xcond_bo, L0_ffn_gate, L0_ffn_W1, L0_ffn_b1, L0_ffn_W2, L0_ffn_b2, L0_ffn_Ws1, L0_ffn_bs1, L0_ffn_Ws2, L0_ffn_bs2, L1_xcond_Wq, L1_xcond_bq, L1_xcond_Wk, L1_xcond_bk, L1_xcond_Wv, L1_xcond_bv, L1_xcond_Wo, L1_xcond_bo, L1_ffn_w_gate, L1_ffn_w_up, L1_ffn_w_down, L2_xcond_W_a, L2_xcond_W_c, L2_ffn_bn_gamma, L2_ffn_bn_beta, L2_ffn_w_q, L2_ffn_keys_p, L2_ffn_down, L2_ffn_up, L3_xcond_Wq, L3_xcond_bq, L3_xcond_Wk, L3_xcond_bk, L3_xcond_Wv, L3_xcond_bv, L3_xcond_Wo, L3_xcond_bo, L3_ffn_gate_w, L3_ffn_expert_w):
    import jax
    import jax.numpy as jnp

    def _L0_xcond_ref(query, key, value, tau, delta, Wq, bq, Wk, bk, Wv, bv, Wo, bo):
        import jax, jax.numpy as jnp
        import numpy as np
        B, S, D, H = (2, 512, 256, 16)
        DK = D // H

        def _split_heads(x):
            b, s, _ = x.shape
            return x.reshape(b, s, H, DK).transpose(0, 2, 1, 3)
        q = _split_heads(query @ Wq.T + bq)
        k = _split_heads(key @ Wk.T + bk)
        v = _split_heads(value @ Wv.T + bv)
        scores = jnp.einsum('bhqd,bhkd->bhqk', q, k)
        scores = scores * tau[:, :, None, None] + delta[:, None, None, :]
        scores = scores / jnp.sqrt(jnp.asarray(DK, scores.dtype))
        p_attn = jax.nn.softmax(scores, axis=-1)
        x = jnp.einsum('bhqk,bhkd->bhqd', p_attn, v)
        x = x.transpose(0, 2, 1, 3).reshape(query.shape[0], -1, H * DK)
        return x @ Wo.T + bo

    def _L0_ffn_ref(x, gate, W1, b1, W2, b2, Ws1, bs1, Ws2, bs2):
        import jax, jax.numpy as jnp
        import numpy as np
        NUM_EXPERTS = 8
        CAP_FACTOR = 1.0
        MIN_CAP = 8
        G, S, D = x.shape
        E = gate.shape[1]
        T = G * S
        capacity = max(MIN_CAP, int(CAP_FACTOR * T / E))
        logits = jnp.einsum('gsd,de->gse', x, gate)
        probs = jax.nn.softmax(logits, axis=-1)
        flat_probs = probs.transpose(2, 0, 1).reshape(E, T)
        scores, token_idx = jax.lax.top_k(flat_probs, k=capacity)
        scores = jnp.where(scores > -100000000.0, scores, 0.0)
        flat_x = x.reshape(T, D)
        tok = flat_x[token_idx]
        h = jax.nn.gelu(jnp.einsum('ecd,edh->ech', tok, W1) + b1[:, None, :])
        out_tok = jnp.einsum('ech,ehd->ecd', h, W2) + b2[:, None, :]
        scaled = out_tok * scores[..., None]
        routed = jnp.zeros_like(flat_x).at[token_idx.reshape(-1)].add(scaled.reshape(E * capacity, D)).reshape(G, S, D)
        shared = jax.nn.gelu(jnp.einsum('gsd,dh->gsh', x, Ws1) + bs1)
        shared = jnp.einsum('gsh,hd->gsd', shared, Ws2) + bs2
        return routed + shared

    def _L1_xcond_ref(q, k, v, tau, delta, Wq, bq, Wk, bk, Wv, bv, Wo, bo):
        import jax, jax.numpy as jnp
        import numpy as np
        D_MODEL = 256
        N_HEADS = 16
        B, L, D = q.shape
        S = k.shape[1]
        H = N_HEADS
        E = D // H
        qh = (q @ Wq.T + bq).reshape(B, L, H, E)
        kh = (k @ Wk.T + bk).reshape(B, S, H, E)
        vh = (v @ Wv.T + bv).reshape(B, S, H, E)
        scale = 1.0 / np.sqrt(E).astype(np.float32)
        scores = jnp.einsum('blhe,bshe->bhls', qh, kh)
        scores = scores * tau[:, None, None, :] + delta[:, None, None, :]
        a = jax.nn.softmax(scale * scores, axis=-1)
        out = jnp.einsum('bhls,bshd->blhd', a, vh).reshape(B, L, D)
        return out @ Wo.T + bo

    def _L1_ffn_ref(x, w_gate, w_up, w_down):
        import jax, jax.numpy as jnp
        import numpy as np
        HIDDEN = 256
        INNER = 1024

        def _weight_quant(w):
            scale = 1.0 / jnp.clip(jnp.mean(jnp.abs(w)), 1e-05)
            wq = jnp.clip(jnp.round(w * scale), -1.0, 1.0) / scale
            return w + jax.lax.stop_gradient(wq - w)

        def _act_quant(x):
            scale = 127.0 / jnp.clip(jnp.max(jnp.abs(x), axis=-1, keepdims=True), 1e-05)
            xq = jnp.clip(jnp.round(x * scale), -128.0, 127.0) / scale
            return x + jax.lax.stop_gradient(xq - x)

        def _bitlinear(x, w):
            return jnp.einsum('bsi,oi->bso', _act_quant(x), _weight_quant(w))
        gate = jax.nn.silu(_bitlinear(x, w_gate))
        up = _bitlinear(x, w_up)
        return _bitlinear(gate * up, w_down)

    def _L2_xcond_ref(encoder_outputs, decoder_h_t, src_len, p_t, W_a, W_c):
        import jax, jax.numpy as jnp
        import numpy as np
        N, L, H, Q = (64, 258, 256, 64)
        WINDOW = 16.0
        DEV_POW = 128.0
        n, l, h = encoder_outputs.shape
        idx = jnp.arange(l, dtype=jnp.float32)
        src_end = src_len.astype(jnp.float32)
        attn_start = jnp.maximum(p_t - WINDOW, 0.0)
        attn_end = jnp.minimum(p_t + WINDOW, src_end)
        mask = (idx[None, :] < attn_start[:, None]) | (idx[None, :] > attn_end[:, None])
        score = jnp.einsum('nqh,hk,nlk->nql', decoder_h_t, W_a, encoder_outputs)
        score = jnp.where(mask[:, None, :], -1000000000.0, score)
        align = jax.nn.softmax(score, axis=2)
        gauss = jnp.exp(-(idx[None, :] - p_t[:, None]) ** 2 / DEV_POW)
        align = align * gauss[:, None, :]
        context = jnp.einsum('nql,nlh->nqh', align, encoder_outputs)
        cat = jnp.concatenate([context, decoder_h_t], axis=2)
        return jnp.tanh(cat @ W_c.T)

    def _L2_ffn_ref(inputs, bn_gamma, bn_beta, w_q, keys_p, down, up):
        import jax, jax.numpy as jnp
        import numpy as np
        B, S, H = (2, 256, 256)
        KD, NH, K = (128, 8, 8)
        NE = 16384
        NK = 64
        EPS = 1e-05
        b, s, d = inputs.shape
        x = inputs.reshape(b * s, d)
        mean = x.mean(axis=0)
        var = x.var(axis=0)
        xn = (x - mean) * jax.lax.rsqrt(var + EPS) * bn_gamma + bn_beta
        xn = xn.reshape(b, s, d)
        q = (xn @ w_q.T).reshape(b, s, 2, NH, KD).transpose(2, 0, 1, 3, 4)
        sim = jnp.einsum('pbnhd,hkpd->pbnhk', q, keys_p)
        scores, idx = jax.lax.top_k(sim, K)
        all_scores = (scores[0][..., :, None] + scores[1][..., None, :]).reshape(b, s, NH, K * K)
        all_idx = (idx[0][..., :, None] * NK + idx[1][..., None, :]).reshape(b, s, NH, K * K)
        sc, pk = jax.lax.top_k(all_scores, K)
        indices = jnp.take_along_axis(all_idx, pk, axis=-1)
        wd = down[indices]
        hmid = jnp.einsum('bnd,bnhkd->bnhk', inputs, wd)
        hmid = jax.nn.sigmoid(sc) * jax.nn.gelu(hmid, approximate=False)
        wu = up[indices]
        return jnp.einsum('bnhk,bnhkd->bnd', hmid, wu)

    def _L3_xcond_ref(q, k, v, tau, delta, Wq, bq, Wk, bk, Wv, bv, Wo, bo):
        import jax, jax.numpy as jnp
        import numpy as np
        D_MODEL = 256
        N_HEADS = 16
        B, L, D = q.shape
        S = k.shape[1]
        H = N_HEADS
        E = D // H
        qh = (q @ Wq.T + bq).reshape(B, L, H, E)
        kh = (k @ Wk.T + bk).reshape(B, S, H, E)
        vh = (v @ Wv.T + bv).reshape(B, S, H, E)
        scale = 1.0 / np.sqrt(E).astype(np.float32)
        scores = jnp.einsum('blhe,bshe->bhls', qh, kh)
        scores = scores * tau[:, None, None, :] + delta[:, None, None, :]
        a = jax.nn.softmax(scale * scores, axis=-1)
        out = jnp.einsum('bhls,bshd->blhd', a, vh).reshape(B, L, D)
        return out @ Wo.T + bo

    def _L3_ffn_ref(x, gate_w, expert_w):
        import jax, jax.numpy as jnp
        import numpy as np
        NUM_EXPERTS = 8
        TOP_K = 2
        N_EMBD = 256
        B, T = (4, 512)
        Bb, Tt, C = x.shape
        xf = x.reshape(Bb * Tt, C)
        logits = xf @ gate_w.T
        w, sel = jax.lax.top_k(logits, TOP_K)
        w = jax.nn.softmax(w.astype(jnp.float32), axis=1).astype(xf.dtype)
        n = xf.shape[0]
        w_full = jnp.zeros((n, NUM_EXPERTS), dtype=xf.dtype)
        w_full = w_full.at[jnp.arange(n)[:, None], sel].add(w)
        expert_out = jnp.einsum('nc,edc->ned', xf, expert_w)
        out = jnp.einsum('ne,ned->nd', w_full, expert_out)
        return out.reshape(Bb, Tt, C)
    x = x + _L0_xcond_ref(_layernorm(x, axis=-1), ctx_1024, ctx_1024, condB_tau[:, None], fside_BxS2_0, L0_xcond_Wq, L0_xcond_bq, L0_xcond_Wk, L0_xcond_bk, L0_xcond_Wv, L0_xcond_bv, L0_xcond_Wo, L0_xcond_bo)
    x = x + _L0_ffn_ref(_layernorm(x, axis=-1), L0_ffn_gate, L0_ffn_W1, L0_ffn_b1, L0_ffn_W2, L0_ffn_b2, L0_ffn_Ws1, L0_ffn_bs1, L0_ffn_Ws2, L0_ffn_bs2)
    x = x + _L1_xcond_ref(_layernorm(x, axis=-1), ctx_1024, ctx_1024, condB_tau[:, None], fside_BxS2_0, L1_xcond_Wq, L1_xcond_bq, L1_xcond_Wk, L1_xcond_bk, L1_xcond_Wv, L1_xcond_bv, L1_xcond_Wo, L1_xcond_bo)
    x = x + _L1_ffn_ref(_layernorm(x, axis=-1), L1_ffn_w_gate, L1_ffn_w_up, L1_ffn_w_down)
    x = x + _L2_xcond_ref(ctx_1024, _layernorm(x, axis=-1), _lenS2, condB_pt, L2_xcond_W_a, L2_xcond_W_c)
    x = x + _L2_ffn_ref(_layernorm(x, axis=-1), L2_ffn_bn_gamma, L2_ffn_bn_beta, L2_ffn_w_q, L2_ffn_keys_p, L2_ffn_down, L2_ffn_up)
    x = x + _L3_xcond_ref(_layernorm(x, axis=-1), ctx_1024, ctx_1024, condB_tau[:, None], fside_BxS2_0, L3_xcond_Wq, L3_xcond_bq, L3_xcond_Wk, L3_xcond_bk, L3_xcond_Wv, L3_xcond_bv, L3_xcond_Wo, L3_xcond_bo)
    x = x + _L3_ffn_ref(_layernorm(x, axis=-1), L3_ffn_gate_w, L3_ffn_expert_w)
    return x

_drawn_inputs = setup_inputs


def setup_inputs(seed=0):
    import zlib

    import numpy as np

    out = dict(_drawn_inputs(seed))
    spreads = {'L0_ffn_b1': (0.0, 0.491),
     'L0_ffn_b2': (0.0, 0.28),
     'L0_ffn_bs1': (0.0, 0.1),
     'L0_ffn_bs2': (0.0, 0.1),
     'L1_xcond_bq': (0.0, 0.336),
     'L1_xcond_bk': (0.0, 0.8),
     'L1_xcond_bv': (0.0, 0.1),
     'L1_xcond_bo': (0.0, 0.1),
     'L2_ffn_bn_gamma': (1.0, 0.6),
     'L2_ffn_bn_beta': (0.0, 0.8),
     'L3_xcond_bq': (0.0, 0.415),
     'L3_xcond_bk': (0.0, 0.8),
     'L3_xcond_bv': (0.0, 0.1),
     'L3_xcond_bo': (0.0, 0.1)}
    factors = {'L0_xcond_bq': 6.437,
     'L0_xcond_bk': 8.0,
     'L0_xcond_bv': 2.849,
     'L0_xcond_bo': 3.317,
     'L2_ffn_w_q': 5.744,
     'L2_ffn_keys_p': 5.235,
     'L2_ffn_down': 4.907,
     'L2_ffn_up': 4.692}
    for name, (base, spread) in spreads.items():
        noise = np.random.default_rng([zlib.crc32(name.encode()), seed]).standard_normal(out[name].shape)
        drawn = base * np.exp(spread * noise) if base else spread * noise
        out[name] = jnp.asarray(drawn.astype(out[name].dtype))
    for name, factor in factors.items():
        out[name] = (out[name] * factor).astype(out[name].dtype)
    return out
```

```python
from contextlib import ExitStack

import concourse.bass as bass
from concourse import mybir

ALU = mybir.AluOpType
ACT = mybir.ActivationFunctionType
F32 = mybir.dt.float32
BF16 = mybir.dt.bfloat16
F16 = mybir.dt.float16
I32 = mybir.dt.int32
U32 = mybir.dt.uint32
AX_X = mybir.AxisListType.X

P = 128
TILES = 32
D = 256
KC = D // P
HEADS = 16
DK = D // HEADS
HC = 4
G = 4
GT = G * P
GROUPS = TILES // G
LN_EPS = 1e-5


class Tally:

    def __init__(self, sem, turn, per):
        self.sem, self.base, self.per, self.n = sem, turn * per, per, 0

    def inc(self, ins):
        ins.then_inc(self.sem, 1)
        self.n += 1

    def wait(self, eng):
        eng.wait_ge(self.sem, self.base + self.n)

    def close(self):
        assert self.n == self.per, (self.sem, self.n, self.per)


def await_apart(eng, sem, value, passed):
    eng.wait_ge(sem, value)
    eng.sem_inc(passed, 1)


class Ring:

    def __init__(self, name, sem, banks, uses):
        assert len(uses) % len(banks) == 0
        self.banks, self.uses = banks, uses
        self.n_banks, self.per = len(banks), len(uses)
        self.full = sem(name + "_full")
        self.taken = [sem(f"{name}_taken{b}") for b in range(len(banks))]
        self.at = {u: n for n, u in enumerate(uses)}

    def bank(self, use):
        return self.banks[self.at[use] % self.n_banks]

    def start_empty(self, eng):
        for s in self.taken:
            eng.sem_inc(s, 1)

    def claim(self, pe, turn, use):
        n = self.at[use]
        pe.wait_ge(self.taken[n % self.n_banks], turn * (self.per // self.n_banks) + n // self.n_banks + 1)

    def wait_full(self, eng, turn, use):
        eng.wait_ge(self.full, turn * self.per + self.at[use] + 1)

    def filled(self, ins):
        ins.then_inc(self.full, 1)

    def take(self, ins, use):
        ins.then_inc(self.taken[self.at[use] % self.n_banks], 1)

    def wait_taken(self, eng, turn, use):
        n = self.at[use]
        eng.wait_ge(self.taken[n % self.n_banks], turn * (self.per // self.n_banks) + n // self.n_banks + 2)


def finish_rows(dve, keep, link, t, new, bst, mv):
    link.wait(dve)
    link.inc(dve.bn_stats(bst[:, :], new[:, :]))
    link.wait(dve)
    dve.tensor_scalar(keep["X"][:, bass.ds(t, 1), :], new[:, :].rearrange("p (a n) -> p a n", a=1), 1.0, None,
                      ALU.mult)
    link.inc(dve.bn_aggr(mv[:, :], bst[:, :]))
    link.wait(dve)
    dve.tensor_scalar(keep["MV"][:, bass.ds(t, 1), :], mv[:, :].rearrange("p (a n) -> p a n", a=1), 1.0, None,
                      ALU.mult)


def attention(nc, keep, tag, w, ctxT):
    with ExitStack() as ctx:
        def sb(name, shape, dt=F32):
            return ctx.enter_context(nc.sbuf_tensor(f"{tag}_{name}", shape, dt))

        def sem(name):
            return keep["semaphore"](f"{tag}_{name}")

        X, MV, ident = keep["X"], keep["MV"], keep["ident"]
        wq = sb("wq", [P, KC, HC * P])
        wk = sb("wk", [P, KC, HC * P])
        wv = sb("wv", [P, KC, D])
        wo = sb("wo", [P, KC, D])
        bq = sb("bq", [P, HC])
        bk = sb("bk", [P, HC])
        bv = sb("bv", [P, D])
        bo = sb("bo", [P, D])
        delta = sb("delta", [P, TILES * P])
        tau4 = sb("tau4", [P, TILES])
        rstd = sb("rstd", [P, TILES])
        rstd_tau = sb("rstd_tau", [P, TILES])
        bq_tau = sb("bq_tau", [P, HC, TILES])
        ctx_g = sb("ctx_g", [P, KC, GT])
        xn = sb("xn", [P, G, D])
        xnT = sb("xnT", [P, KC, GT])
        qT = sb("qT", [P, HC, GT])
        kT = sb("kT", [P, HC, GT])
        vaug = sb("vaug", [P, G, HEADS, DK + 1])
        probs = sb("probs", [P, 2, HEADS * P])
        probsT = sb("probsT", [P, 2, HEADS, P])
        mx = sb("mx", [P, HEADS])
        rden = sb("rden", [P, HEADS])
        on = sb("on", [P, 2, D])
        oT = sb("oT", [P, KC, P])
        tmp = sb("tmp", [P, D])
        new = sb("new", [P, D])
        bst = sb("bst", [P, 6])
        mv = sb("mv", [P, 2])

        ps_s = ctx.enter_context(nc.psum_tensor(f"{tag}_ps_s", [P, 4, HC, P], F32))
        ps_t = [ctx.enter_context(nc.psum_tensor(f"{tag}_ps_t{b}", [P, 4, P], F32)) for b in range(2)]
        ps_m = [ctx.enter_context(nc.psum_tensor(f"{tag}_ps_m{b}", [P, 512], F32)) for b in range(2)]
        uses = ["xt0", "xt1"] + [f"{a}{c}" for c in range(HC) for a in "qk"] + ["v0", "v1"]
        for u in range(G + 1):
            uses += ([f"ot{u - 1}"] if u else []) + ([f"pv{u}"] if u < G else []) + ([f"y{u - 1}"] if u else [])
        misc = Ring(f"{tag}_misc", sem, ps_m, uses)
        tr = Ring(f"{tag}_tr", sem, ps_t, [f"{u}_{j}" for u in range(G) for j in range(4)])

        w_loaded = sem("w_loaded")
        ctx_loaded = sem("ctx_loaded")
        rstd_sq = sem("rstd_sq")
        xn_ready = sem("xn_ready")
        s_ready = sem("s_ready")
        s_taken = sem("s_taken")
        p_ready = sem("p_ready")
        dve_link = sem("dve_link")
        setup_link = sem("setup_link")

        loads = [(wq[:, :, :], w["wq"].rearrange("(k p) n -> p k n", p=P)),
                 (wk[:, :, :], w["wk"].rearrange("(k p) n -> p k n", p=P)),
                 (wv[:, :, :], w["wv"].rearrange("(k p) n -> p k n", p=P)),
                 (wo[:, :, :], w["wo"].rearrange("(k p) n -> p k n", p=P)),
                 (delta[:, :], keep["delta_rows"]), (bq[:, :], w["bq"]), (bk[:, :], w["bk"]), (bv[:, :], w["bv"]), (bo[:, :], w["bo"])]
        ctx_v = ctxT.rearrange("(k p) n -> p k n", p=P)
        block = ctx.enter_context(nc.Block())

        @block.sync
        def _(sp):
            for dst, src in loads:
                sp.dma_start(dst, src).then_inc(w_loaded, 16)
            sp.dma_start(ctx_g[:, :, :], ctx_v[:, :, 0:GT]).then_inc(ctx_loaded, 16)
            with sp.Fori(1, GROUPS) as g:
                misc.wait_full(sp, g - 1, "v1")
                sp.dma_start(ctx_g[:, :, :], ctx_v[:, :, bass.ds(g * GT, GT)]).then_inc(ctx_loaded, 16)

        @block.scalar
        def _(act):
            act.activation(rstd[:, :], MV[:, :, 1], ACT.Sqrt, bias=keep["eps"][:, 0:1]).then_inc(rstd_sq, 1)
            act.wait_ge(setup_link, 5)
            with act.Fori(0, GROUPS) as g:
                for i in range(2):
                    misc.wait_full(act, g, f"xt{i}")
                    ins = act.activation(xnT[:, :, i * 256:(i + 1) * 256],
                                         misc.bank(f"xt{i}")[:, :].rearrange("p (k n) -> p k n", k=KC), ACT.Copy)
                    misc.take(ins, f"xt{i}")
                for c in range(HC):
                    misc.wait_full(act, g, f"q{c}")
                    for u in range(G):
                        ins = act.activation(qT[:, c, u * P:(u + 1) * P], misc.bank(f"q{c}")[:, u * P:(u + 1) * P],
                                             ACT.Identity, bias=bq_tau[:, c, bass.ds(g * G + u, 1)])
                    misc.take(ins, f"q{c}")

                def exps(u):
                    act.wait_ge(s_taken, g * G + u + 2)
                    act.activation(probs[:, u % 2, :], probs[:, u % 2, :], ACT.Exp).then_inc(p_ready, 1)

                exps(0)
                for u in range(G + 1):
                    if u < G:
                        for j in range(4):
                            tr.wait_full(act, g, f"{u}_{j}")
                            ins = act.activation(probsT[:, u % 2, 4 * j:4 * j + 4, :], tr.bank(f"{u}_{j}")[:, :, :],
                                                 ACT.Copy)
                            tr.take(ins, f"{u}_{j}")
                    if u + 1 < G:
                        exps(u + 1)
                    if u:
                        misc.wait_full(act, g, f"ot{u - 1}")
                        ins = act.activation(oT[:, :, :], misc.bank(f"ot{u - 1}")[:, 0:D].rearrange(
                            "p (k n) -> p k n", k=KC), ACT.Copy)
                        misc.take(ins, f"ot{u - 1}")

        @block.tensor
        def _(pe):
            misc.start_empty(pe)
            tr.start_empty(pe)
            pe.sem_inc(s_taken, 1)
            pe.wait_ge(w_loaded, 16 * len(loads))
            with pe.Fori(0, GROUPS) as g:
                for i in range(2):
                    misc.claim(pe, g, f"xt{i}")
                    for u in (2 * i, 2 * i + 1):
                        pe.wait_ge(xn_ready, g * G + u + 1)
                        for k in range(KC):
                            at = k * 256 + (u % 2) * P
                            ins = pe.transpose(misc.bank(f"xt{i}")[:, at:at + P], xn[:, u, k * P:(k + 1) * P],
                                               ident[:, :])
                    misc.filled(ins)
                for i in range(2):
                    misc.wait_taken(pe, g, f"xt{i}")
                pe.wait_ge(ctx_loaded, g * 16 + 16)
                for c in range(HC):
                    for a, wt, rhs in (("q", wq, xnT), ("k", wk, ctx_g)):
                        misc.claim(pe, g, f"{a}{c}")
                        for k in range(KC):
                            ins = pe.matmul(misc.bank(f"{a}{c}")[:, :], wt[:, k, c * P:(c + 1) * P], rhs[:, k, :],
                                            start=(k == 0), stop=(k == KC - 1))
                        misc.filled(ins)
                for i in range(2):
                    misc.claim(pe, g, f"v{i}")
                    for u in (2 * i, 2 * i + 1):
                        for k in range(KC):
                            ins = pe.matmul(misc.bank(f"v{i}")[:, (u % 2) * D:(u % 2 + 1) * D],
                                            ctx_g[:, k, u * P:(u + 1) * P], wv[:, k, :],
                                            start=(k == 0), stop=(k == KC - 1))
                    misc.filled(ins)
                misc.wait_taken(pe, g, f"q{HC - 1}")
                misc.wait_taken(pe, g, f"k{HC - 1}")

                def scores(u):
                    pe.wait_ge(s_taken, g * G + u + 1)
                    for c in range(HC):
                        for r in range(4):
                            ins = pe.matmul(ps_s[:, r, c, :], qT[32 * r:32 * r + 32, c, u * P:(u + 1) * P],
                                            kT[32 * r:32 * r + 32, c, u * P:(u + 1) * P], start=True, stop=True,
                                            skip_group_check=True)
                    ins.then_inc(s_ready, 1)

                scores(0)
                for u in range(G + 1):
                    if u + 1 < G:
                        scores(u + 1)
                    if u < G:
                        pe.wait_ge(p_ready, g * G + u + 1)
                        for j in range(4):
                            tr.claim(pe, g, f"{u}_{j}")
                            for c in range(4):
                                ins = pe.transpose(tr.bank(f"{u}_{j}")[:, c, :],
                                                   probs[:, u % 2, (4 * j + c) * P:(4 * j + c + 1) * P], ident[:, :])
                            tr.filled(ins)
                    if u:
                        misc.claim(pe, g, f"ot{u - 1}")
                        misc.wait_taken(pe, g, f"pv{u - 1}")
                        for k in range(KC):
                            ins = pe.transpose(misc.bank(f"ot{u - 1}")[:, k * P:(k + 1) * P],
                                               on[:, (u - 1) % 2, k * P:(k + 1) * P], ident[:, :])
                        misc.filled(ins)
                    if u < G:
                        misc.claim(pe, g, f"pv{u}")
                        if u == 0:
                            for i in range(2):
                                misc.wait_taken(pe, g, f"v{i}")
                        for j in range(4):
                            tr.wait_taken(pe, g, f"{u}_{j}")
                            for c in range(4):
                                h = 4 * c + j
                                ins = pe.matmul(misc.bank(f"pv{u}")[:, h * (DK + 1):(h + 1) * (DK + 1)],
                                                probsT[:, u % 2, 4 * j + c, :], vaug[:, u, h, :],
                                                start=True, stop=True, skip_group_check=True)
                        misc.filled(ins)
                    if u:
                        misc.claim(pe, g, f"y{u - 1}")
                        misc.wait_taken(pe, g, f"ot{u - 1}")
                        for k in range(KC):
                            ins = pe.matmul(misc.bank(f"y{u - 1}")[:, 0:D], oT[:, k, :], wo[:, k, :],
                                            start=(k == 0), stop=(k == KC - 1))
                        misc.filled(ins)

        @block.vector
        def _(dve):
            dve.memset(vaug[:, :, :, DK:DK + 1], 1.0).then_inc(setup_link, 1)
            dve.wait_ge(rstd_sq, 1)
            dve.reciprocal(rstd[:, :], rstd[:, :]).then_inc(setup_link, 1)
            dve.tensor_scalar(tau4[:, :], keep["tau"][:, :], 1.0 / DK ** 0.5, None, ALU.mult).then_inc(setup_link, 1)
            dve.wait_ge(setup_link, 3)
            dve.tensor_tensor(rstd_tau[:, :], rstd[:, :], tau4[:, :], ALU.mult).then_inc(setup_link, 1)
            dve.wait_ge(w_loaded, 16 * len(loads))
            for c in range(HC):
                ins = dve.tensor_scalar(bq_tau[:, c, :], tau4[:, :], bq[:, c:c + 1], keep["quarter"][:, 0:1],
                                        ALU.mult, ALU.add)
            ins.then_inc(setup_link, 1)
            dve.wait_ge(setup_link, 5)
            with dve.Fori(0, GROUPS) as g:
                link = Tally(dve_link, g, G * 5)
                for u in range(G):
                    t = g * G + u
                    dve.tensor_scalar(xn[:, u, :], X[:, bass.ds(t, 1), :], MV[:, bass.ds(t, 1), 0],
                                      rstd_tau[:, bass.ds(t, 1)], ALU.subtract, ALU.mult).then_inc(xn_ready, 1)
                for c in range(HC):
                    misc.wait_full(dve, g, f"k{c}")
                    ins = dve.scalar_tensor_tensor(kT[:, c, :], misc.bank(f"k{c}")[:, :], bk[:, c:c + 1],
                                                   delta[:, bass.ds(g * GT, GT)], ALU.add, ALU.add)
                    misc.take(ins, f"k{c}")
                for i in range(2):
                    misc.wait_full(dve, g, f"v{i}")
                    ins = dve.tensor_tensor(vaug[:, 2 * i:2 * i + 2, :, 0:DK],
                                            misc.bank(f"v{i}")[:, :].rearrange("p (u h d) -> p u h d", u=2, h=HEADS),
                                            bv[:, :].rearrange("p (a h d) -> p a h d", a=1, h=HEADS).broadcast_to(
                                                [P, 2, HEADS, DK]), ALU.add)
                    misc.take(ins, f"v{i}")

                def shift(u):
                    dve.wait_ge(s_ready, g * G + u + 1)
                    sv = ps_s[:, :, :, :].rearrange("p r c n -> p (r c) n")
                    link.inc(dve.tensor_reduce(mx[:, :], sv, AX_X, ALU.max))
                    link.wait(dve)
                    if u >= 2:
                        pass
                    dve.tensor_tensor(probs[:, u % 2, :].rearrange("p (h n) -> p h n", h=HEADS), sv,
                                      mx[:, :].rearrange("p (h a) -> p h a", a=1).broadcast_to([P, HEADS, P]),
                                      ALU.subtract).then_inc(s_taken, 1)

                shift(0)
                for u in range(G + 1):
                    if u + 1 < G:
                        if u >= 1:
                            tr.wait_full(dve, g, f"{u - 1}_3")
                        shift(u + 1)
                    if u < G:
                        b = misc.bank(f"pv{u}")[:, 0:HEADS * (DK + 1)].rearrange("p (h d) -> p h d", h=HEADS)
                        misc.wait_full(dve, g, f"pv{u}")
                        link.inc(dve.reciprocal(rden[:, :], b[:, :, DK]))
                        link.wait(dve)
                        ins = dve.tensor_tensor(on[:, u % 2, :].rearrange("p (h d) -> p h d", h=HEADS), b[:, :, 0:DK],
                                                rden[:, :].rearrange("p (h a) -> p h a", a=1).broadcast_to(
                                                    [P, HEADS, DK]), ALU.mult)
                        misc.take(ins, f"pv{u}")
                    if u:
                        t = g * G + u - 1
                        misc.wait_full(dve, g, f"y{u - 1}")
                        ins = dve.tensor_tensor(tmp[:, :], misc.bank(f"y{u - 1}")[:, 0:D], bo[:, :], ALU.add)
                        misc.take(ins, f"y{u - 1}")
                        misc.wait_taken(dve, g, f"y{u - 1}")
                        link.inc(dve.tensor_tensor(new[:, :].rearrange("p (a n) -> p a n", a=1),
                                                   X[:, bass.ds(t, 1), :],
                                                   tmp[:, :].rearrange("p (a n) -> p a n", a=1), ALU.add))
                        finish_rows(dve, keep, link, t, new, bst, mv)
                link.close()


TOKENS = TILES * P
EXPERTS = 8
CAPACITY = TOKENS // EXPERTS
SLOTS = CAPACITY // P
HID = 1024
HCH = HID // P
ROW = D + EXPERTS


def layer_norm_scale(act, dve, keep, rstd, sq, done):
    if act is not None:
        act.activation(rstd[:, :], keep["MV"][:, :, 1], ACT.Sqrt, bias=keep["eps"][:, 0:1]).then_inc(sq, 1)
    if dve is not None:
        dve.wait_ge(sq, 1)
        dve.reciprocal(rstd[:, :], rstd[:, :]).then_inc(done, 1)
        dve.wait_ge(done, 1)


def shared_ffn(nc, keep, w, probs, row_dram, sum_dram):
    tag = "sh"
    with ExitStack() as ctx:
        def sb(name, shape, dt=F32):
            return ctx.enter_context(nc.sbuf_tensor(f"{tag}_{name}", shape, dt))

        def sem(name):
            return keep["semaphore"](f"{tag}_{name}")

        X, MV, ident = keep["X"], keep["MV"], keep["ident"]
        w1 = sb("w1", [P, KC, HID])
        w2 = sb("w2", [P, HCH, D])
        gate = sb("gate", [P, KC, EXPERTS])
        b1 = sb("b1", [P, HCH])
        b2 = sb("b2", [P, D])
        rstd = sb("rstd", [P, TILES])
        row = sb("row", [P, G, ROW])
        xnT = sb("xnT", [P, KC, GT])
        hT = sb("hT", [P, HCH, GT])
        tmp = sb("tmp", [P, G, D])
        new = sb("new", [P, G, D])
        lg = sb("lg", [P, G, EXPERTS])
        lmx = sb("lmx", [P, G])
        lsum = sb("lsum", [P, G])
        banks = [ctx.enter_context(nc.psum_tensor(f"{tag}_ps{b}", [P, 512], F32)) for b in range(5)]
        ring = Ring(f"{tag}_ring", sem, banks, ["xt0", "xt1", "lg"] + [f"up{c}" for c in range(HCH)]
                    + [f"y{u}" for u in range(G)])
        w_loaded = sem("w_loaded")
        rstd_sq = sem("rstd_sq")
        rstd_done = sem("rstd_done")
        xn_ready = sem("xn_ready")
        lg_shifted = sem("lg_shifted")
        lg_exp = sem("lg_exp")
        row_ready = sem("row_ready")
        row_stored = sem("row_stored")
        sum_ready = sem("sum_ready")
        sum_stored = sem("sum_stored")
        dve_link = sem("dve_link")
        loads = [(gate[:, :, :], w["gate"].rearrange("(k p) n -> p k n", p=P)),
                 (w1[:, :, :], w["Ws1"].rearrange("(k p) n -> p k n", p=P)),
                 (w2[:, :, :], w["Ws2"].rearrange("(k p) n -> p k n", p=P)),
                 (b1[:, :], w["bs1"]), (b2[:, :], w["bs2"])]
        row_v = row_dram.rearrange("(t p) n -> p t n", p=P)
        sum_v = sum_dram.rearrange("(t p) n -> p t n", p=P)
        block = ctx.enter_context(nc.Block())

        @block.sync
        def _(sp):
            for dst, src in loads:
                sp.dma_start(dst, src).then_inc(w_loaded, 16)
            with sp.Fori(0, GROUPS) as g:
                sp.wait_ge(row_ready, g + 1)
                sp.dma_start(row_v[:, bass.ds(g * G, G), :], row[:, :, :]).then_inc(row_stored, 16)
                sp.wait_ge(sum_ready, g + 1)
                sp.dma_start(sum_v[:, bass.ds(g * G, G), :], new[:, :, :]).then_inc(sum_stored, 16)
            sp.wait_ge(row_stored, 16 * (GROUPS + 1))
            sp.wait_ge(sum_stored, 16 * (GROUPS + 1))

        @block.scalar
        def _(act):
            layer_norm_scale(act, None, keep, rstd, rstd_sq, rstd_done)
            with act.Fori(0, GROUPS) as g:
                for i in range(2):
                    ring.wait_full(act, g, f"xt{i}")
                    ring.take(act.activation(xnT[:, :, i * 256:(i + 1) * 256],
                                             ring.bank(f"xt{i}")[:, :].rearrange("p (k n) -> p k n", k=KC),
                                             ACT.Copy), f"xt{i}")
                act.wait_ge(lg_shifted, g + 1)
                act.activation(lg[:, :, :], lg[:, :, :], ACT.Exp).then_inc(lg_exp, 1)
                for c in range(HCH):
                    ring.wait_full(act, g, f"up{c}")
                    ring.take(act.activation(hT[:, c, :], ring.bank(f"up{c}")[:, :], ACT.Gelu_apprx_tanh,
                                             bias=b1[:, c:c + 1]), f"up{c}")

        @block.tensor
        def _(pe):
            ring.start_empty(pe)
            pe.wait_ge(w_loaded, 16 * len(loads))
            with pe.Fori(0, GROUPS) as g:
                for i in range(2):
                    ring.claim(pe, g, f"xt{i}")
                    for u in (2 * i, 2 * i + 1):
                        pe.wait_ge(xn_ready, g * G + u + 1)
                        for k in range(KC):
                            at = k * 256 + (u % 2) * P
                            ins = pe.transpose(ring.bank(f"xt{i}")[:, at:at + P], row[:, u, k * P:(k + 1) * P],
                                               ident[:, :])
                    ring.filled(ins)
                for i in range(2):
                    ring.wait_taken(pe, g, f"xt{i}")
                ring.claim(pe, g, "lg")
                for u in range(G):
                    for k in range(KC):
                        ins = pe.matmul(ring.bank("lg")[:, u * EXPERTS:(u + 1) * EXPERTS],
                                        xnT[:, k, u * P:(u + 1) * P], gate[:, k, :], start=(k == 0),
                                        stop=(k == KC - 1))
                ring.filled(ins)
                for c in range(HCH):
                    ring.claim(pe, g, f"up{c}")
                    for k in range(KC):
                        ins = pe.matmul(ring.bank(f"up{c}")[:, :], w1[:, k, c * P:(c + 1) * P], xnT[:, k, :],
                                        start=(k == 0), stop=(k == KC - 1))
                    ring.filled(ins)
                for u in range(G):
                    ring.claim(pe, g, f"y{u}")
                    for c in range(HCH):
                        if u == 0:
                            ring.wait_taken(pe, g, f"up{c}")
                        ins = pe.matmul(ring.bank(f"y{u}")[:, 0:D], hT[:, c, u * P:(u + 1) * P], w2[:, c, :],
                                        start=(c == 0), stop=(c == HCH - 1))
                    ring.filled(ins)

        @block.vector
        def _(dve):
            layer_norm_scale(None, dve, keep, rstd, rstd_sq, rstd_done)
            dve.sem_inc(row_stored, 16)
            dve.sem_inc(sum_stored, 16)
            with dve.Fori(0, GROUPS) as g:
                link = Tally(dve_link, g, 3 + G)
                dve.wait_ge(row_stored, g * 16 + 16)
                for u in range(G):
                    t = g * G + u
                    dve.tensor_scalar(row[:, u:u + 1, 0:D], X[:, bass.ds(t, 1), :], MV[:, bass.ds(t, 1), 0],
                                      rstd[:, bass.ds(t, 1)], ALU.subtract, ALU.mult).then_inc(xn_ready, 1)
                ring.wait_full(dve, g, "lg")
                lv = ring.bank("lg")[:, 0:G * EXPERTS].rearrange("p (u e) -> p u e", u=G)
                link.inc(dve.tensor_reduce(lmx[:, :], lv, AX_X, ALU.max))
                link.wait(dve)
                ring.take(dve.tensor_tensor(lg[:, :, :], lv, lmx[:, :].rearrange(
                    "p (u a) -> p u a", a=1).broadcast_to([P, G, EXPERTS]), ALU.subtract), "lg")
                ring.wait_taken(dve, g, "lg")
                dve.sem_inc(lg_shifted, 1)
                dve.wait_ge(lg_exp, g + 1)
                link.inc(dve.tensor_reduce(lsum[:, :], lg[:, :, :], AX_X, ALU.add))
                link.wait(dve)
                link.inc(dve.reciprocal(lsum[:, :], lsum[:, :]))
                link.wait(dve)
                lb = lsum[:, :].rearrange("p (u a) -> p u a", a=1).broadcast_to([P, G, EXPERTS])
                dve.tensor_tensor(probs[:, bass.ds(g * G, G), :], lg[:, :, :], lb, ALU.mult)
                dve.tensor_tensor(row[:, :, D:ROW], lg[:, :, :], lb, ALU.mult).then_inc(row_ready, 1)
                dve.wait_ge(sum_stored, g * 16 + 16)
                for u in range(G):
                    t = g * G + u
                    ring.wait_full(dve, g, f"y{u}")
                    ring.take(dve.tensor_tensor(tmp[:, u, :], ring.bank(f"y{u}")[:, 0:D], b2[:, :], ALU.add), f"y{u}")
                    ring.wait_taken(dve, g, f"y{u}")
                    link.inc(dve.tensor_tensor(new[:, u:u + 1, :], X[:, bass.ds(t, 1), :],
                                               tmp[:, u:u + 1, :], ALU.add))
                link.wait(dve)
                dve.sem_inc(sum_ready, 1)
                link.close()


def choose_tokens(nc, keep, probs, idx):
    tag = "ch"
    BITS = 30
    ET = EXPERTS * TILES
    with ExitStack() as ctx:
        def sb(name, shape, dt=F32):
            return ctx.enter_context(nc.sbuf_tensor(f"{tag}_{name}", shape, dt))

        def sem(name):
            return keep["semaphore"](f"{tag}_{name}")

        ones = sb("ones", [P, P])
        before = sb("before", [P, P])
        iota_i = sb("iota_i", [P, P], I32)
        iota = sb("iota", [P, P])
        part_i = sb("part_i", [P, 1], I32)
        part = sb("part", [P, 1])
        tile_i = sb("tile_i", [P, ET], I32)
        tile_f = sb("tile_f", [P, ET])
        thr = sb("thr", [P, EXPERTS], I32)
        bit = sb("bit", [P, EXPERTS], I32)
        cand = sb("cand", [P, EXPERTS], I32)
        hit = sb("hit", [P, EXPERTS], I32)
        pe_t = sb("pe_t", [P, EXPERTS, TILES])
        flag = sb("flag", [P, EXPERTS, TILES])
        over = sb("over", [P, EXPERTS, TILES])
        count = sb("count", [P, EXPERTS])
        need = sb("need", [P, EXPERTS])
        carry = sb("carry", [P, ET])
        tot = sb("tot", [P, ET])
        inc_s = sb("inc_s", [P, ET])
        pos = sb("pos", [P, ET])
        pos_i = sb("pos_i", [P, ET], I32)
        hi_i = sb("hi_i", [P, ET], I32)
        hi = sb("hi", [P, ET])
        lo = sb("lo", [P, ET])
        chosen = sb("chosen", [P, ET])
        oh = sb("oh", [P, ET, SLOTS])
        rhs = sb("rhs", [P, ET, 2 * SLOTS], BF16)
        lohot = sb("lohot", [P, 2, TILES, P], BF16)
        half = sb("half", [P, EXPERTS, SLOTS])
        ps_c = ctx.enter_context(nc.psum_tensor(f"{tag}_ps_c", [P, EXPERTS], F32))
        ps_a = ctx.enter_context(nc.psum_tensor(f"{tag}_ps_a", [P, ET], F32))
        ps_b = ctx.enter_context(nc.psum_tensor(f"{tag}_ps_b", [P, ET], F32))
        ps_i = ctx.enter_context(nc.psum_tensor(f"{tag}_ps_i", [P, EXPERTS, 2 * SLOTS], F32))
        consts = sem("consts")
        pool_link = sem("pool_link")
        bit_link = sem("bit_link")
        part_ready = sem("part_ready")
        counted = sem("counted")
        flags_ready = sem("flags_ready")
        summed = sem("summed")
        dl = sem("dl")
        lohot_ready = sem("lohot_ready")
        placed = sem("placed")
        block = ctx.enter_context(nc.Block())

        @block.gpsimd
        def _(pool):
            pool.memset(ones[:, :], 1.0).then_inc(pool_link, 1)
            pool.memset(carry[:, :], 1.0).then_inc(pool_link, 1)
            pool.wait_ge(pool_link, 2)
            pool.affine_select(out=before[:, :], in_=ones[:, :], compare_op=ALU.is_gt, fill=0.0, base=0,
                               pattern=[[1, P]], channel_multiplier=-1).then_inc(consts, 1)
            pool.memset(carry[:, :].rearrange("p (e t) -> p e t", e=EXPERTS)[:, :, 0:1], 0.0).then_inc(consts, 1)
            pool.iota(iota_i[:, :], [[1, P]], base=0, channel_multiplier=0).then_inc(pool_link, 1)
            pool.iota(part_i[:, :], [[0, 1]], base=0, channel_multiplier=1).then_inc(pool_link, 1)
            pool.iota(tile_i[:, :], [[0, EXPERTS], [1, TILES]], base=0, channel_multiplier=0).then_inc(pool_link, 1)
            pool.wait_ge(pool_link, 5)
            pool.tensor_copy(iota[:, :], iota_i[:, :]).then_inc(consts, 1)
            pool.tensor_copy(part[:, :], part_i[:, :]).then_inc(consts, 1)
            pool.tensor_copy(tile_f[:, :], tile_i[:, :]).then_inc(consts, 1)

        @block.tensor
        def _(pe):
            pe.wait_ge(consts, 5)
            with pe.Fori(0, BITS + 1) as b:
                pe.wait_ge(part_ready, b + 1)
                pe.matmul(ps_c[:, :], ones[:, :], count[:, :], start=True, stop=True).then_inc(counted, 1)
            for n in range(2):
                pe.wait_ge(flags_ready, n + 1)
                src = (over if n == 0 else chosen)
                src = over[:, :, :].rearrange("p e t -> p (e t)") if n == 0 else chosen[:, :]
                pe.matmul(ps_a[:, :], before[:, :], src, start=True, stop=True)
                pe.matmul(ps_b[:, :], ones[:, :], src, start=True, stop=True).then_inc(summed, 1)
            with pe.Fori(0, EXPERTS // 2) as i:
                for s in range(2):
                    e = i * 2 + s
                    pe.wait_ge(lohot_ready, e + 1)
                    for t in range(TILES):
                        ins = pe.matmul(ps_i[:, bass.ds(e, 1), :], lohot[:, s, t, :],
                                        rhs[:, bass.ds(e * TILES + t, 1), :], start=(t == 0), stop=(t == TILES - 1))
                    ins.then_inc(placed, 1)

        @block.vector
        def _(dve):
            dve.memset(thr[:, :], 0)
            dve.memset(bit[:, :], 1 << (BITS - 1)).then_inc(dl, 1)
            dve.tensor_copy(pe_t[:, :, :], probs[:, :, :].rearrange("p t e -> p e t")).then_inc(dl, 1)
            dve.wait_ge(dl, 2)

            def wide(v):
                return v.rearrange("p (e a) -> p e a", a=1).broadcast_to([P, EXPERTS, TILES])

            with dve.Fori(0, BITS) as b:
                link = Tally(bit_link, b, 6)
                link.inc(dve.tensor_tensor(cand[:, :], thr[:, :], bit[:, :], ALU.bitwise_or))
                link.wait(dve)
                link.inc(dve.tensor_tensor(flag[:, :, :], pe_t[:, :, :], wide(cand[:, :].bitcast(F32)), ALU.is_ge))
                link.wait(dve)
                dve.tensor_reduce(count[:, :], flag[:, :, :], AX_X, ALU.add).then_inc(part_ready, 1)
                dve.wait_ge(counted, b + 1)
                link.inc(dve.tensor_scalar(hit[:, :], ps_c[:, :], float(CAPACITY), -1.0, ALU.is_ge, ALU.mult))
                link.wait(dve)
                link.inc(dve.tensor_tensor(hit[:, :], hit[:, :], bit[:, :], ALU.bitwise_and))
                link.wait(dve)
                link.inc(dve.tensor_tensor(thr[:, :], thr[:, :], hit[:, :], ALU.bitwise_or))
                link.inc(dve.tensor_scalar(bit[:, :], bit[:, :], 1, None, ALU.logical_shift_right))
                link.wait(dve)
                link.close()
            steps = [2]

            def step(ins):
                ins.then_inc(dl, 1)
                steps[0] += 1
                dve.wait_ge(dl, steps[0])

            T = wide(thr[:, :].bitcast(F32))
            step(dve.tensor_tensor(flag[:, :, :], pe_t[:, :, :], T, ALU.is_gt))
            dve.tensor_tensor(over[:, :, :], pe_t[:, :, :], T, ALU.is_equal).then_inc(flags_ready, 1)
            dve.tensor_reduce(count[:, :], flag[:, :, :], AX_X, ALU.add).then_inc(part_ready, 1)
            dve.wait_ge(counted, BITS + 1)
            step(dve.tensor_scalar(need[:, :], ps_c[:, :], -1.0, float(CAPACITY), ALU.mult, ALU.add))

            def rank(n):
                dve.wait_ge(summed, n)
                step(dve.tensor_copy(tot[:, :], ps_b[:, :]))
                step(dve.tensor_tensor_scan(inc_s[:, :], carry[:, :], tot[:, :], 0.0, ALU.mult, ALU.add))
                step(dve.tensor_tensor(inc_s[:, :], inc_s[:, :], tot[:, :], ALU.subtract))
                step(dve.tensor_tensor(pos[:, :], ps_a[:, :], inc_s[:, :], ALU.add))

            dve.wait_ge(consts, 5)
            rank(1)
            step(dve.tensor_tensor(pos[:, :].rearrange("p (e t) -> p e t", e=EXPERTS),
                                   pos[:, :].rearrange("p (e t) -> p e t", e=EXPERTS), wide(need[:, :]), ALU.is_lt))
            step(dve.tensor_tensor(pos[:, :], pos[:, :], over[:, :, :].rearrange("p e t -> p (e t)"), ALU.mult))
            step(dve.tensor_tensor(chosen[:, :], pos[:, :], flag[:, :, :].rearrange("p e t -> p (e t)"), ALU.add))
            dve.sem_inc(flags_ready, 1)
            rank(2)
            step(dve.tensor_copy(pos_i[:, :], pos[:, :]))
            step(dve.tensor_scalar(hi_i[:, :], pos_i[:, :], 7, None, ALU.logical_shift_right))
            step(dve.tensor_copy(hi[:, :], hi_i[:, :]))
            step(dve.tensor_scalar(pos_i[:, :], pos_i[:, :], P - 1, None, ALU.bitwise_and))
            step(dve.tensor_copy(lo[:, :], pos_i[:, :]))
            four = [P, ET, SLOTS]
            step(dve.tensor_tensor(oh[:, :, :], hi[:, :].rearrange("p (n a) -> p n a", a=1).broadcast_to(four),
                                   iota[:, 0:SLOTS].rearrange("p (a c) -> p a c", a=1).broadcast_to(four),
                                   ALU.is_equal))
            step(dve.tensor_tensor(oh[:, :, :], oh[:, :, :],
                                   chosen[:, :].rearrange("p (n a) -> p n a", a=1).broadcast_to(four), ALU.mult))
            step(dve.tensor_scalar(rhs[:, :, 0:SLOTS], oh[:, :, :], part[:, 0:1], None, ALU.mult))
            step(dve.tensor_tensor(rhs[:, :, SLOTS:2 * SLOTS], oh[:, :, :],
                                   tile_f[:, :].rearrange("p (n a) -> p n a", a=1).broadcast_to(four), ALU.mult))
            dve.sem_inc(placed, 2)
            with dve.Fori(0, EXPERTS // 2) as i:
                for s in range(2):
                    e = i * 2 + s
                    dve.wait_ge(placed, e + 1)
                    dve.tensor_tensor(lohot[:, s, :, :],
                                      iota[:, :].rearrange("p (a n) -> p a n", a=1).broadcast_to([P, TILES, P]),
                                      lo[:, bass.ds(e * TILES, TILES)].rearrange("p (t a) -> p t a", a=1).broadcast_to(
                                          [P, TILES, P]), ALU.is_equal).then_inc(lohot_ready, 1)
            dve.wait_ge(placed, EXPERTS + 2)
            step(dve.tensor_copy(half[:, :, :], ps_i[:, :, 0:SLOTS]))
            step(dve.scalar_tensor_tensor(idx[:, :, :], ps_i[:, :, SLOTS:2 * SLOTS], float(P), half[:, :, :],
                                          ALU.mult, ALU.add))


def routed_ffn(nc, keep, w, idx, row_dram, sum_dram):
    tag = "ro"
    with ExitStack() as ctx:
        def sb(name, shape, dt=F32):
            return ctx.enter_context(nc.sbuf_tensor(f"{tag}_{name}", shape, dt))

        def sem(name):
            return keep["semaphore"](f"{tag}_{name}")

        X, MV, ident = keep["X"], keep["MV"], keep["ident"]
        w1 = sb("w1", [P, 2, KC, HID])
        w2 = sb("w2", [P, 2, HCH, D])
        b1 = sb("b1", [P, 2, HCH])
        b2 = sb("b2", [P, 2, D])
        row = sb("row", [P, 2, SLOTS, ROW])
        score = sb("score", [P, 2, SLOTS])
        xnT = sb("xnT", [P, KC, CAPACITY])
        hT = sb("hT", [P, HCH, CAPACITY])
        tmp = sb("tmp", [P, SLOTS, D])
        y = sb("y", [P, 2, SLOTS, D])
        tok = sb("tok", [P, 2, SLOTS], U32)
        bst = sb("bst", [P, TILES, 6])
        banks = [ctx.enter_context(nc.psum_tensor(f"{tag}_ps{b}", [P, 512], F32)) for b in range(7)]
        ring = Ring(f"{tag}_ring", sem, banks, ["xt0", "xt1"] + [f"up{c}" for c in range(HCH)]
                    + [f"y{u}" for u in range(SLOTS)])
        w_loaded = [sem(f"w_loaded{s}") for s in range(2)]
        gathered = [sem(f"gathered{s}") for s in range(2)]
        scattered = sem("scattered")
        tok_ready = sem("tok_ready")
        scores_out = sem("scores_out")
        pool_passed = sem("pool_passed")
        y_stored = sem("y_stored")
        y_ready = sem("y_ready")
        x_loaded = sem("x_loaded")
        bn_link = sem("bn_link")
        sum_v = sum_dram.rearrange("(t p) n -> p t n", p=P)
        w1_v = w["W1"].rearrange("e (k p) n -> p e k n", p=P)
        w2_v = w["W2"].rearrange("e (k p) n -> p e k n", p=P)
        block = ctx.enter_context(nc.Block())

        @block.sync
        def _(sp):
            def load(s, e):
                one = bass.ds(e, 1)
                sp.dma_start(w1[:, s:s + 1, :, :], w1_v[:, one, :, :]).then_inc(w_loaded[s], 16)
                sp.dma_start(w2[:, s:s + 1, :, :], w2_v[:, one, :, :]).then_inc(w_loaded[s], 16)
                sp.dma_start(b1[:, s:s + 1, :], w["b1"][:, one, :]).then_inc(w_loaded[s], 16)
                sp.dma_start(b2[:, s:s + 1, :], w["b2"][:, one, :]).then_inc(w_loaded[s], 16)

            load(0, 0)
            load(1, 1)
            with sp.Fori(1, EXPERTS // 2) as i:
                for s in range(2):
                    sp.wait_ge(y_ready, (i - 1) * 2 + s + 2)
                    load(s, i * 2 + s)
            sp.wait_ge(scattered, 16 * SLOTS * EXPERTS)
            sp.dma_start(X[:, :, :], sum_v).then_inc(x_loaded, 16)
            sp.wait_ge(x_loaded, 16)

        @block.gpsimd
        def _(pool):
            def gather(s, e):
                pool.tensor_copy(tok[:, s:s + 1, :], idx[:, bass.ds(e, 1), :]).then_inc(tok_ready, 1)
                await_apart(pool, tok_ready, e + 1, pool_passed)
                for c in range(SLOTS):
                    pool.indirect_dma_start(out=row[:, s, c, :], out_offset=None, in_=row_dram[:, :],
                                            in_offset=bass.IndirectOffsetOnAxis(ap=tok[:, s, c:c + 1], axis=0),
                                            ).then_inc(gathered[s], 16)

            gather(0, 0)
            def turn(i, last):
                for s in range(2):
                    e = i * 2 + s
                    if not (last and s == 1):
                        gather(1 - s, e + 1)
                    await_apart(pool, y_ready, e + 2, pool_passed)
                    for c in range(SLOTS):
                        pool.indirect_dma_start(out=sum_dram[:, :], in_=y[:, s, c, :], in_offset=None,
                                                out_offset=bass.IndirectOffsetOnAxis(ap=tok[:, s, c:c + 1], axis=0),
                                                compute_op=ALU.add).then_inc(scattered, 16)
                    await_apart(pool, scattered, (e + 1) * 16 * SLOTS, y_stored)

            with pool.Fori(0, EXPERTS // 2 - 1) as i:
                turn(i, False)
            turn(EXPERTS // 2 - 1, True)

        @block.scalar
        def _(act):
            with act.Fori(0, EXPERTS // 2) as i:
                for s in range(2):
                    e = i * 2 + s
                    for n in range(2):
                        ring.wait_full(act, e, f"xt{n}")
                        ring.take(act.activation(xnT[:, :, n * 256:(n + 1) * 256],
                                                 ring.bank(f"xt{n}")[:, :].rearrange("p (k n) -> p k n", k=KC),
                                                 ACT.Copy), f"xt{n}")
                    if s == 0:
                        act.wait_ge(w_loaded[0], i * 64 + 64)
                    else:
                        act.wait_ge(w_loaded[1], i * 64 + 64)
                    for c in range(HCH):
                        ring.wait_full(act, e, f"up{c}")
                        ring.take(act.activation(hT[:, c, :], ring.bank(f"up{c}")[:, :], ACT.Gelu_apprx_tanh,
                                                 bias=b1[:, s, c:c + 1]), f"up{c}")

        @block.tensor
        def _(pe):
            ring.start_empty(pe)
            with pe.Fori(0, EXPERTS // 2) as i:
                for s in range(2):
                    e = i * 2 + s
                    pe.wait_ge(gathered[s], (i + 1) * 16 * SLOTS)
                    for n in range(2):
                        ring.claim(pe, e, f"xt{n}")
                        for u in (2 * n, 2 * n + 1):
                            for k in range(KC):
                                at = k * 256 + (u % 2) * P
                                ins = pe.transpose(ring.bank(f"xt{n}")[:, at:at + P],
                                                   row[:, s, u, k * P:(k + 1) * P], ident[:, :])
                        ring.filled(ins)
                    for n in range(2):
                        ring.wait_taken(pe, e, f"xt{n}")
                    pe.wait_ge(w_loaded[s], i * 64 + 64)
                    for c in range(HCH):
                        ring.claim(pe, e, f"up{c}")
                        for k in range(KC):
                            ins = pe.matmul(ring.bank(f"up{c}")[:, :], w1[:, s, k, c * P:(c + 1) * P], xnT[:, k, :],
                                            start=(k == 0), stop=(k == KC - 1))
                        ring.filled(ins)
                    for u in range(SLOTS):
                        ring.claim(pe, e, f"y{u}")
                        for c in range(HCH):
                            if u == 0:
                                ring.wait_taken(pe, e, f"up{c}")
                            ins = pe.matmul(ring.bank(f"y{u}")[:, 0:D], hT[:, c, u * P:(u + 1) * P], w2[:, s, c, :],
                                            start=(c == 0), stop=(c == HCH - 1))
                        ring.filled(ins)

        @block.vector
        def _(dve):
            dve.sem_inc(scores_out, 1)
            dve.sem_inc(y_ready, 1)
            dve.sem_inc(y_stored, 2)
            with dve.Fori(0, EXPERTS // 2) as i:
                for s in range(2):
                    e = i * 2 + s
                    dve.wait_ge(gathered[s], (i + 1) * 16 * SLOTS)
                    dve.tensor_scalar(score[:, s, :].rearrange("p (c a) -> p c a", a=1),
                                      row[:, s, :, bass.ds(D + e, 1)], 1.0, None, ALU.mult).then_inc(scores_out, 1)
                    dve.wait_ge(w_loaded[s], i * 64 + 64)
                    dve.wait_ge(y_ready, e + 1)
                    dve.wait_ge(y_stored, e + 1)
                    for u in range(SLOTS):
                        ring.wait_full(dve, e, f"y{u}")
                        ring.take(dve.tensor_tensor(tmp[:, u, :], ring.bank(f"y{u}")[:, 0:D], b2[:, s, :], ALU.add),
                                  f"y{u}")
                    dve.wait_ge(scores_out, e + 2)
                    for u in range(SLOTS):
                        ring.wait_taken(dve, e, f"y{u}")
                        ins = dve.tensor_scalar(y[:, s, u, :], tmp[:, u, :], score[:, s, u:u + 1], None, ALU.mult)
                    ins.then_inc(y_ready, 1)
            dve.wait_ge(x_loaded, 16)
            for t in range(TILES):
                ins = dve.bn_stats(bst[:, t, :], X[:, t, :])
            ins.then_inc(bn_link, 1)
            dve.wait_ge(bn_link, 1)
            for t in range(TILES):
                dve.bn_aggr(MV[:, t, :], bst[:, t, :])


INNER = 1024
ROUND = 12582912.0


def bit_ffn(nc, keep, w):
    tag = "bf"
    S2 = 2
    with ExitStack() as ctx:
        def sb(name, shape, dt=F32):
            return ctx.enter_context(nc.sbuf_tensor(f"{tag}_{name}", shape, dt))

        def sem(name):
            return keep["semaphore"](f"{tag}_{name}")

        X, MV = keep["X"], keep["MV"]
        names = ("gate", "up", "down")
        raw = {n: sb("raw_" + n, [P, KC * INNER]) for n in names}
        wb = {n: sb("wb_" + n, [P, KC * INNER], BF16) for n in names}
        wg = wb["gate"][:, :].rearrange("p (k n) -> p k n", k=KC)
        wu = wb["up"][:, :].rearrange("p (k n) -> p k n", k=KC)
        wd = wb["down"][:, :].rearrange("p (k n) -> p k n", k=INNER // P)
        ones = sb("ones", [P, P])
        identb = sb("identb", [P, P], BF16)
        asum = sb("asum", [P, 3])
        wmean = sb("wmean", [P, 3])
        wscale = sb("wscale", [P, 3])
        wq127 = sb("wq127", [P, 3])
        rstd = sb("rstd", [P, TILES])
        xn = sb("xn", [P, S2, D])
        xq = sb("xq", [P, S2, D], BF16)
        xqT = sb("xqT", [P, S2, KC, P], BF16)
        amx = sb("amx", [P, S2, 2])
        asc = sb("asc", [P, S2, 2])
        dq = sb("dq", [P, S2, 3])
        gt = sb("gt", [P, S2, INNER])
        h = sb("h", [P, S2, INNER])
        hq = sb("hq", [P, S2, INNER], BF16)
        hqT = sb("hqT", [P, S2, INNER // P, P], BF16)
        new = sb("new", [P, S2, D])
        bst = sb("bst", [P, 6])
        mv = sb("mv", [P, 2])
        banks = [ctx.enter_context(nc.psum_tensor(f"{tag}_ps{b}", [P, 512], F32)) for b in range(7)]
        ps_w = ctx.enter_context(nc.psum_tensor(f"{tag}_ps_w", [P, 3], F32))
        ring = Ring(f"{tag}_ring", sem, banks, ["xt0", "xt1"] + [f"{a}{n}_{s}" for s in range(S2) for a in "gu"
                    for n in range(2)] + ["ht0", "ht1", "y0", "y1"])
        w_loaded = [sem("w_loaded_" + n) for n in names]
        consts = sem("consts")
        rstd_sq = sem("rstd_sq")
        sums_ready = sem("sums_ready")
        summed = sem("summed")
        setup = sem("setup")
        xq_ready = sem("xq_ready")
        dq_ready = sem("dq_ready")
        hq_ready = sem("hq_ready")
        dve_link = sem("dve_link")
        block = ctx.enter_context(nc.Block())

        @block.sync
        def _(sp):
            for n, src, k in (("gate", w["w_gate"], KC), ("up", w["w_up"], KC), ("down", w["w_down"], INNER // P)):
                sp.dma_start(raw[n][:, :].rearrange("p (k n) -> p k n", k=k),
                             src.rearrange("(k p) n -> p k n", p=P)).then_inc(w_loaded[names.index(n)], 16)

        @block.gpsimd
        def _(pool):
            pool.memset(ones[:, :], 1.0).then_inc(consts, 1)
            pool.tensor_copy(identb[:, :], keep["ident"][:, :]).then_inc(consts, 1)

        @block.scalar
        def _(act):
            layer_norm_scale(act, None, keep, rstd, rstd_sq, None)
            with act.Fori(0, TILES // S2) as i:
                for s in range(S2):
                    ring.wait_full(act, i, f"xt{s}")
                    ring.take(act.activation(xqT[:, s, :, :], ring.bank(f"xt{s}")[:, :].bitcast(BF16)[:, 0:D].rearrange(
                        "p (k n) -> p k n", k=KC), ACT.Copy), f"xt{s}")
                for s in range(S2):
                    act.wait_ge(dq_ready, i * S2 + s + 1)
                    for n in range(2):
                        ring.wait_full(act, i, f"g{n}_{s}")
                        ring.take(act.activation(gt[:, s, n * 512:(n + 1) * 512], ring.bank(f"g{n}_{s}")[:, :],
                                                 ACT.Silu, scale=dq[:, s, 0:1]), f"g{n}_{s}")
                for s in range(S2):
                    ring.wait_full(act, i, f"ht{s}")
                    ring.take(act.activation(hqT[:, s, :, :], ring.bank(f"ht{s}")[:, :].bitcast(BF16).rearrange(
                        "p (k n) -> p k n", n=P), ACT.Copy), f"ht{s}")

        @block.tensor
        def _(pe):
            ring.start_empty(pe)
            pe.wait_ge(consts, 2)
            pe.wait_ge(sums_ready, 3)
            pe.matmul(ps_w[:, :], ones[:, :], asum[:, :], start=True, stop=True).then_inc(summed, 1)
            pe.wait_ge(setup, 16)
            with pe.Fori(0, TILES // S2) as i:
                for s in range(S2):
                    ring.claim(pe, i, f"xt{s}")
                    pe.wait_ge(xq_ready, i * S2 + s + 1)
                    for k in range(KC):
                        ins = pe.transpose(ring.bank(f"xt{s}")[:, :].bitcast(BF16)[:, k * P:(k + 1) * P],
                                           xq[:, s, k * P:(k + 1) * P], identb[:, :])
                    ring.filled(ins)
                for s in range(S2):
                    ring.wait_taken(pe, i, f"xt{s}")
                    for a, wt in (("g", wg), ("u", wu)):
                        for n in range(2):
                            ring.claim(pe, i, f"{a}{n}_{s}")
                            for k in range(KC):
                                ins = pe.matmul(ring.bank(f"{a}{n}_{s}")[:, :], xqT[:, s, k, :],
                                                wt[:, k, n * 512:(n + 1) * 512], start=(k == 0), stop=(k == KC - 1))
                            ring.filled(ins)
                for s in range(S2):
                    ring.claim(pe, i, f"ht{s}")
                    pe.wait_ge(hq_ready, i * S2 + s + 1)
                    for k in range(INNER // P):
                        ins = pe.transpose(ring.bank(f"ht{s}")[:, :].bitcast(BF16)[:, k * P:(k + 1) * P],
                                           hq[:, s, k * P:(k + 1) * P], identb[:, :])
                    ring.filled(ins)
                for s in range(S2):
                    ring.claim(pe, i, f"y{s}")
                    ring.wait_taken(pe, i, f"ht{s}")
                    for k in range(INNER // P):
                        ins = pe.matmul(ring.bank(f"y{s}")[:, 0:D], hqT[:, s, k, :], wd[:, k, :], start=(k == 0),
                                        stop=(k == INNER // P - 1))
                    ring.filled(ins)

        @block.vector
        def _(dve):
            layer_norm_scale(None, dve, keep, rstd, rstd_sq, setup)
            done = [1]

            def step(ins):
                ins.then_inc(setup, 1)
                done[0] += 1
                dve.wait_ge(setup, done[0])

            for n in range(3):
                dve.wait_ge(w_loaded[n], 16)
                dve.tensor_reduce(asum[:, n:n + 1], raw[names[n]][:, :], AX_X, ALU.add,
                                  apply_absolute_value=True).then_inc(sums_ready, 1)
            dve.wait_ge(summed, 1)
            step(dve.tensor_scalar(wmean[:, :], ps_w[:, :], 1.0 / (D * INNER), 1e-5, ALU.mult, ALU.max))
            step(dve.reciprocal(wscale[:, :], wmean[:, :]))
            step(dve.tensor_scalar(wq127[:, :], wmean[:, :], 1.0 / 127.0, None, ALU.mult))
            for n in range(3):
                r = raw[names[n]]
                step(dve.tensor_scalar(r[:, :], r[:, :], wscale[:, n:n + 1], ROUND, ALU.mult, ALU.add))
                step(dve.tensor_scalar(r[:, :], r[:, :], ROUND, 1.0, ALU.subtract, ALU.min))
                step(dve.tensor_scalar(r[:, :], r[:, :], -1.0, None, ALU.max))
                step(dve.tensor_copy(wb[names[n]][:, :], r[:, :]))

            with dve.Fori(0, TILES // S2) as i:
                link = Tally(dve_link, i, S2 * 16)

                def quantise(src, dst, s, a):
                    one = slice(a, a + 1)
                    link.inc(dve.tensor_reduce(amx[:, s, one], src, AX_X, ALU.max, apply_absolute_value=True))
                    link.wait(dve)
                    link.inc(dve.tensor_scalar(amx[:, s, one], amx[:, s, one], 1e-5, None, ALU.max))
                    link.wait(dve)
                    link.inc(dve.reciprocal(asc[:, s, one], amx[:, s, one]))
                    link.wait(dve)
                    link.inc(dve.tensor_scalar(asc[:, s, one], asc[:, s, one], 127.0, None, ALU.mult))
                    link.wait(dve)
                    link.inc(dve.tensor_scalar(src, src, asc[:, s, one], -128.0, ALU.mult, ALU.max))
                    link.wait(dve)
                    link.inc(dve.tensor_scalar(src, src, 127.0, ROUND, ALU.min, ALU.add))
                    link.wait(dve)
                    return dve.tensor_scalar(dst, src, ROUND, None, ALU.subtract)

                for s in range(S2):
                    t = i * S2 + s
                    link.inc(dve.tensor_scalar(xn[:, s:s + 1, :], X[:, bass.ds(t, 1), :], MV[:, bass.ds(t, 1), 0],
                                               rstd[:, bass.ds(t, 1)], ALU.subtract, ALU.mult))
                    link.wait(dve)
                    quantise(xn[:, s, :], xq[:, s, :], s, 0).then_inc(xq_ready, 1)
                    dve.tensor_scalar(dq[:, s, 0:2], wq127[:, 0:2], amx[:, s, 0:1], None, ALU.mult).then_inc(
                        dq_ready, 1)
                for s in range(S2):
                    dve.wait_ge(dq_ready, i * S2 + s + 1)
                    for n in range(2):
                        ring.wait_taken(dve, i, f"g{n}_{s}")
                        ring.wait_full(dve, i, f"u{n}_{s}")
                        ring.take(dve.scalar_tensor_tensor(h[:, s, n * 512:(n + 1) * 512],
                                                           ring.bank(f"u{n}_{s}")[:, :], dq[:, s, 1:2],
                                                           gt[:, s, n * 512:(n + 1) * 512], ALU.mult, ALU.mult),
                                  f"u{n}_{s}")
                    for n in range(2):
                        ring.wait_taken(dve, i, f"u{n}_{s}")
                    quantise(h[:, s, :], hq[:, s, :], s, 1).then_inc(hq_ready, 1)
                    link.inc(dve.tensor_scalar(dq[:, s, 2:3], wq127[:, 2:3], amx[:, s, 1:2], None, ALU.mult))
                for s in range(S2):
                    t = i * S2 + s
                    ring.wait_full(dve, i, f"y{s}")
                    link.wait(dve)
                    ring.take(dve.scalar_tensor_tensor(new[:, s:s + 1, :], ring.bank(f"y{s}")[:, 0:D].rearrange(
                        "p (a n) -> p a n", a=1), dq[:, s, 2:3], X[:, bass.ds(t, 1), :], ALU.mult, ALU.add), f"y{s}")
                    ring.wait_taken(dve, i, f"y{s}")
                    finish_rows(dve, keep, link, t, new[:, s, :], bst, mv)
                link.close()


WINDOW = 16.0
DEV_POW = 128.0
MASKED = 1e9


def windowed_attention(nc, keep, w, ctxT, ctx_n):
    tag = "wa"
    with ExitStack() as ctx:
        def sb(name, shape, dt=F32):
            return ctx.enter_context(nc.sbuf_tensor(f"{tag}_{name}", shape, dt))

        def sem(name):
            return keep["semaphore"](f"{tag}_{name}")

        X, MV, ident = keep["X"], keep["MV"], keep["ident"]
        wa = sb("wa", [P, KC, D])
        wc = sb("wc", [P, 2 * KC, D])
        pt = sb("pt", [P, TILES])
        len_i = sb("len_i", [P, TILES], I32)
        first = sb("first", [P, TILES])
        last = sb("last", [P, TILES])
        neg_pt = sb("neg_pt", [P, TILES])
        iota_i = sb("iota_i", [P, P], I32)
        iota = sb("iota", [P, P])
        rstd = sb("rstd", [P, TILES])
        ctx_t = sb("ctx_t", [P, KC, GT])
        ctx_r = sb("ctx_r", [P, G, D])
        xn = sb("xn", [P, G, D])
        xnT = sb("xnT", [P, KC, GT])
        aT = sb("aT", [P, KC, GT])
        inside = sb("inside", [P, G, P])
        low = sb("low", [P, G, P])
        gauss = sb("gauss", [P, G, P])
        sc = sb("sc", [P, G, P])
        mx = sb("mx", [P, G])
        den = sb("den", [P, G])
        al = sb("al", [P, G, P])
        alT = sb("alT", [P, G, P])
        cxT = sb("cxT", [P, G, KC, P])
        th = sb("th", [P, G, D])
        new = sb("new", [P, D])
        bst = sb("bst", [P, 6])
        mv = sb("mv", [P, 2])
        banks = [ctx.enter_context(nc.psum_tensor(f"{tag}_ps{b}", [P, 512], F32)) for b in range(5)]
        ring = Ring(f"{tag}_ring", sem, banks, ["xt0", "xt1", "a0", "a1"]
                    + [f"{n}{u}" for n in ("sc", "al", "cx", "y") for u in range(G)])
        w_loaded = sem("w_loaded")
        ctx_loaded = sem("ctx_loaded")
        pool_link = sem("pool_link")
        consts = sem("consts")
        rstd_sq = sem("rstd_sq")
        setup = sem("setup")
        xn_ready = sem("xn_ready")
        gauss_sq = sem("gauss_sq")
        gauss_ready = sem("gauss_ready")
        mx_ready = sem("mx_ready")
        exp_ready = sem("exp_ready")
        al_ready = sem("al_ready")
        dve_link = sem("dve_link")
        loads = [(wa[:, :, :], w["W_a"].rearrange("(k p) n -> p k n", p=P)),
                 (wc[:, :, :], w["W_c"].rearrange("(k p) n -> p k n", p=P)),
                 (pt[:, :], w["pt"]), (len_i[:, :], w["len"])]
        ctxT_v = ctxT.rearrange("(k p) n -> p k n", p=P)
        ctx_v = ctx_n.rearrange("(t p) d -> p t d", p=P)
        block = ctx.enter_context(nc.Block())

        @block.sync
        def _(sp):
            for dst, src in loads:
                sp.dma_start(dst, src).then_inc(w_loaded, 16)
            sp.dma_start(ctx_t[:, :, :], ctxT_v[:, :, 0:GT]).then_inc(ctx_loaded, 16)
            sp.dma_start(ctx_r[:, :, :], ctx_v[:, 0:G, :]).then_inc(ctx_loaded, 16)
            with sp.Fori(1, GROUPS) as g:
                ring.wait_full(sp, g - 1, f"cx{G - 1}")
                sp.dma_start(ctx_t[:, :, :], ctxT_v[:, :, bass.ds(g * GT, GT)]).then_inc(ctx_loaded, 16)
                sp.dma_start(ctx_r[:, :, :], ctx_v[:, bass.ds(g * G, G), :]).then_inc(ctx_loaded, 16)

        @block.gpsimd
        def _(pool):
            pool.iota(iota_i[:, :], [[1, P]], base=0, channel_multiplier=0).then_inc(pool_link, 1)
            pool.wait_ge(pool_link, 1)
            pool.tensor_copy(iota[:, :], iota_i[:, :]).then_inc(consts, 1)

        @block.scalar
        def _(act):
            layer_norm_scale(act, None, keep, rstd, rstd_sq, None)
            act.wait_ge(consts, 1)
            act.wait_ge(setup, 6)
            with act.Fori(0, GROUPS) as g:
                for n in range(2):
                    ring.wait_full(act, g, f"xt{n}")
                    ring.take(act.activation(xnT[:, :, n * 256:(n + 1) * 256],
                                             ring.bank(f"xt{n}")[:, :].rearrange("p (k n) -> p k n", k=KC),
                                             ACT.Copy), f"xt{n}")
                for u in range(G):
                    act.activation(gauss[:, u, :], iota[:, :], ACT.Square,
                                   bias=neg_pt[:, bass.ds(g * G + u, 1)]).then_inc(gauss_sq, 1)
                act.wait_ge(gauss_sq, g * G + G)
                act.activation(gauss[:, :, :], gauss[:, :, :], ACT.Exp, scale=-1.0 / DEV_POW).then_inc(gauss_ready, 1)
                for k in range(KC):
                    ring.wait_full(act, g, f"a{k}")
                    ring.take(act.activation(aT[:, k, :], ring.bank(f"a{k}")[:, :], ACT.Copy), f"a{k}")
                for u in range(G):
                    act.wait_ge(mx_ready, g * G + u + 1)
                    act.activation(sc[:, u, :], sc[:, u, :], ACT.Exp, bias=mx[:, u:u + 1],
                                   accum_out=den[:, u:u + 1]).then_inc(exp_ready, 1)
                for u in range(G):
                    ring.wait_full(act, g, f"al{u}")
                    ring.take(act.activation(alT[:, u, :], ring.bank(f"al{u}")[:, 0:P], ACT.Copy), f"al{u}")
                for u in range(G):
                    ring.wait_full(act, g, f"cx{u}")
                    ring.take(act.activation(cxT[:, u, :, :], ring.bank(f"cx{u}")[:, 0:D].rearrange(
                        "p (k n) -> p k n", k=KC), ACT.Copy), f"cx{u}")
                for u in range(G):
                    ring.wait_full(act, g, f"y{u}")
                    ring.take(act.activation(th[:, u, :], ring.bank(f"y{u}")[:, 0:D], ACT.Tanh), f"y{u}")

        @block.tensor
        def _(pe):
            ring.start_empty(pe)
            pe.wait_ge(w_loaded, 16 * len(loads))
            with pe.Fori(0, GROUPS) as g:
                for n in range(2):
                    ring.claim(pe, g, f"xt{n}")
                    for u in (2 * n, 2 * n + 1):
                        pe.wait_ge(xn_ready, g * G + u + 1)
                        for k in range(KC):
                            at = k * 256 + (u % 2) * P
                            ins = pe.transpose(ring.bank(f"xt{n}")[:, at:at + P], xn[:, u, k * P:(k + 1) * P],
                                               ident[:, :])
                    ring.filled(ins)
                for n in range(2):
                    ring.wait_taken(pe, g, f"xt{n}")
                for c in range(KC):
                    ring.claim(pe, g, f"a{c}")
                    for k in range(KC):
                        ins = pe.matmul(ring.bank(f"a{c}")[:, :], wa[:, k, c * P:(c + 1) * P], xnT[:, k, :],
                                        start=(k == 0), stop=(k == KC - 1))
                    ring.filled(ins)
                pe.wait_ge(ctx_loaded, g * 32 + 32)
                for c in range(KC):
                    ring.wait_taken(pe, g, f"a{c}")
                for u in range(G):
                    ring.claim(pe, g, f"sc{u}")
                    for k in range(KC):
                        ins = pe.matmul(ring.bank(f"sc{u}")[:, 0:P], aT[:, k, u * P:(u + 1) * P],
                                        ctx_t[:, k, u * P:(u + 1) * P], start=(k == 0), stop=(k == KC - 1))
                    ring.filled(ins)
                for u in range(G):
                    ring.claim(pe, g, f"al{u}")
                    pe.wait_ge(al_ready, g * G + u + 1)
                    ring.filled(pe.transpose(ring.bank(f"al{u}")[:, 0:P], al[:, u, :], ident[:, :]))
                for u in range(G):
                    ring.claim(pe, g, f"cx{u}")
                    ring.wait_taken(pe, g, f"al{u}")
                    for c in range(KC):
                        ins = pe.matmul(ring.bank(f"cx{u}")[:, c * P:(c + 1) * P], ctx_r[:, u, c * P:(c + 1) * P],
                                        alT[:, u, :], start=True, stop=True)
                    ring.filled(ins)
                for u in range(G):
                    ring.claim(pe, g, f"y{u}")
                    ring.wait_taken(pe, g, f"cx{u}")
                    for k in range(2 * KC):
                        lhs = cxT[:, u, k, :] if k < KC else xnT[:, k - KC, u * P:(u + 1) * P]
                        ins = pe.matmul(ring.bank(f"y{u}")[:, 0:D], lhs, wc[:, k, :], start=(k == 0),
                                        stop=(k == 2 * KC - 1))
                    ring.filled(ins)

        @block.vector
        def _(dve):
            layer_norm_scale(None, dve, keep, rstd, rstd_sq, setup)
            dve.wait_ge(w_loaded, 16 * len(loads))
            dve.tensor_copy(last[:, :], len_i[:, :]).then_inc(setup, 1)
            dve.tensor_scalar(first[:, :], pt[:, :], WINDOW, 0.0, ALU.subtract, ALU.max).then_inc(setup, 1)
            dve.tensor_scalar(neg_pt[:, :], pt[:, :], -1.0, None, ALU.mult).then_inc(setup, 1)
            dve.wait_ge(setup, 4)
            dve.scalar_tensor_tensor(last[:, :], pt[:, :], WINDOW, last[:, :], ALU.add, ALU.min).then_inc(setup, 1)
            dve.memset(mv[:, :], 0.0).then_inc(setup, 1)
            dve.wait_ge(setup, 6)
            dve.wait_ge(consts, 1)
            with dve.Fori(0, GROUPS) as g:
                link = Tally(dve_link, g, 3 + 6 * G)
                for u in range(G):
                    t = g * G + u
                    dve.tensor_scalar(xn[:, u:u + 1, :], X[:, bass.ds(t, 1), :], MV[:, bass.ds(t, 1), 0],
                                      rstd[:, bass.ds(t, 1)], ALU.subtract, ALU.mult).then_inc(xn_ready, 1)
                for u in range(G):
                    t = g * G + u
                    ins = dve.tensor_scalar(low[:, u, :], iota[:, :], first[:, bass.ds(t, 1)], None, ALU.is_ge)
                link.inc(ins)
                link.wait(dve)
                for u in range(G):
                    t = g * G + u
                    ins = dve.scalar_tensor_tensor(inside[:, u, :], iota[:, :], last[:, bass.ds(t, 1)], low[:, u, :],
                                                   ALU.is_le, ALU.mult)
                link.inc(ins)
                link.wait(dve)
                link.inc(dve.tensor_scalar(low[:, :, :], inside[:, :, :], MASKED, MASKED, ALU.mult, ALU.subtract))
                link.wait(dve)
                for u in range(G):
                    ring.wait_full(dve, g, f"sc{u}")
                    ring.take(dve.tensor_tensor(sc[:, u, :], ring.bank(f"sc{u}")[:, 0:P], inside[:, u, :], ALU.mult),
                              f"sc{u}")
                    ring.wait_taken(dve, g, f"sc{u}")
                    link.inc(dve.tensor_tensor(sc[:, u, :], sc[:, u, :], low[:, u, :], ALU.add))
                    link.wait(dve)
                    link.inc(dve.tensor_reduce(mx[:, u:u + 1], sc[:, u, :], AX_X, ALU.max))
                    link.wait(dve)
                    dve.tensor_scalar(mx[:, u:u + 1], mx[:, u:u + 1], -1.0, None, ALU.mult).then_inc(mx_ready, 1)
                dve.wait_ge(gauss_ready, g + 1)
                for u in range(G):
                    dve.wait_ge(exp_ready, g * G + u + 1)
                    link.inc(dve.reciprocal(den[:, u:u + 1], den[:, u:u + 1]))
                    link.wait(dve)
                    dve.scalar_tensor_tensor(al[:, u, :], sc[:, u, :], den[:, u:u + 1], gauss[:, u, :],
                                             ALU.mult, ALU.mult).then_inc(al_ready, 1)
                for u in range(G):
                    t = g * G + u
                    ring.wait_taken(dve, g, f"y{u}")
                    link.inc(dve.tensor_tensor(new[:, :].rearrange("p (a n) -> p a n", a=1), th[:, u:u + 1, :],
                                               X[:, bass.ds(t, 1), :], ALU.add))
                    finish_rows(dve, keep, link, t, new, bst, mv)
                link.close()


BN_EPS = 1e-5
PK_HEADS = 8
PK_KEYS = 64
PK_TOP = 8
PK_DIM = 128
PK_EXPERTS = PK_KEYS * PK_KEYS
ECH = PK_EXPERTS // P
PICKS = PK_HEADS * PK_TOP
TB = 16
LO_SCALE = 4096.0


def product_key_experts(nc, keep, w):
    tag = "pk"
    with ExitStack() as ctx:
        def sb(name, shape, dt=F32):
            return ctx.enter_context(nc.sbuf_tensor(f"{tag}_{name}", shape, dt))

        def sem(name):
            return keep["semaphore"](f"{tag}_{name}")

        X, MV, ident = keep["X"], keep["MV"], keep["ident"]
        NT = sb("NT", [P, KC, TOKENS])
        wm = sb("wm", [P, KC, 2 * PK_HEADS * PK_KEYS])
        bn = sb("bn", [P, KC, 2])
        rstd = sb("rstd", [P, TILES])
        with ExitStack() as c2:
            def sb2(name, shape, dt=F32):
                return c2.enter_context(nc.sbuf_tensor(f"{tag}1_{name}", shape, dt))

            def sem2(name):
                return keep["semaphore"](f"{tag}_{name}")

            wq = sb2("wq", [P, 2 * PK_HEADS, D])
            keys = sb2("keys", [P, 2 * PK_HEADS, PK_KEYS])
            gamma = sb2("gamma", [P, KC])
            beta = sb2("beta", [P, KC])
            xn = sb2("xn", [P, G, D])
            nT = sb2("nT", [P, KC, GT])
            bst = sb2("bst", [P, KC, GROUPS, 6])
            mvb = sb2("mvb", [P, KC, 2])
            sd = sb2("sd", [P, KC])
            banks = [c2.enter_context(nc.psum_tensor(f"{tag}_p1_{b}", [P, 512], F32)) for b in range(2)]
            ps_w = [c2.enter_context(nc.psum_tensor(f"{tag}_pw_{b}", [P, 512], F32)) for b in range(4)]
            ring = Ring(f"{tag}_ring1", sem2, banks, ["xt0", "xt1"])
            w_loaded = sem2("w1_loaded")
            folded = sem2("folded")
            rstd_sq = sem2("rstd_sq")
            setup = sem2("setup1")
            xn_ready = sem2("xn1_ready")
            stats = sem2("stats")
            sd_sq = sem2("sd_sq")
            block = c2.enter_context(nc.Block())

            @block.sync
            def _(sp):
                sp.dma_start(wq[:, :, :], w["w_q"].rearrange("(c p) n -> p c n", p=P)).then_inc(w_loaded, 16)
                sp.dma_start(keys[:, :, :], w["keys"]).then_inc(w_loaded, 16)
                sp.dma_start(gamma[:, :], w["gamma"]).then_inc(w_loaded, 16)
                sp.dma_start(beta[:, :], w["beta"]).then_inc(w_loaded, 16)

            @block.scalar
            def _(act):
                layer_norm_scale(act, None, keep, rstd, rstd_sq, None)
                act.wait_ge(folded, 1)
                for k in range(KC):
                    for n in range(2):
                        act.activation(wm[:, k, n * 512:(n + 1) * 512], ps_w[2 * k + n][:, :], ACT.Copy)
                with act.Fori(0, GROUPS) as g:
                    for n in range(2):
                        ring.wait_full(act, g, f"xt{n}")
                        ring.take(act.activation(NT[:, :, bass.ds(g * GT + n * 256, 256)],
                                                 ring.bank(f"xt{n}")[:, :].rearrange("p (k n) -> p k n", k=KC),
                                                 ACT.Copy), f"xt{n}")
                act.wait_ge(stats, 2)
                act.activation(sd[:, :], mvb[:, :, 1], ACT.Sqrt, bias=keep["eps"][:, 0:1]).then_inc(sd_sq, 1)

            @block.tensor
            def _(pe):
                ring.start_empty(pe)
                pe.wait_ge(w_loaded, 64)
                for k in range(KC):
                    for c in range(2 * PK_HEADS):
                        at = (c % PK_HEADS) * PK_KEYS
                        ins = pe.matmul(ps_w[2 * k + c // PK_HEADS][:, at:at + PK_KEYS], wq[:, c, k * P:(k + 1) * P],
                                        keys[:, c, :], start=True, stop=True)
                ins.then_inc(folded, 1)
                with pe.Fori(0, GROUPS) as g:
                    for n in range(2):
                        ring.claim(pe, g, f"xt{n}")
                        for u in (2 * n, 2 * n + 1):
                            pe.wait_ge(xn_ready, g * G + u + 1)
                            for k in range(KC):
                                at = k * 256 + (u % 2) * P
                                ins = pe.transpose(ring.bank(f"xt{n}")[:, at:at + P], xn[:, u, k * P:(k + 1) * P],
                                                   ident[:, :])
                        ring.filled(ins)

            @block.vector
            def _(dve):
                layer_norm_scale(None, dve, keep, rstd, rstd_sq, setup)
                for g in range(GROUPS):
                    for u in range(G):
                        t = g * G + u
                        if g:
                            ring.wait_full(dve, g - 1, f"xt{u // 2}")
                        dve.tensor_scalar(xn[:, u, :], X[:, t, :], MV[:, t, 0:1], rstd[:, t:t + 1], ALU.subtract,
                                          ALU.mult).then_inc(xn_ready, 1)
                    if g:
                        for n in range(2):
                            ring.wait_taken(dve, g - 1, f"xt{n}")
                        for k in range(KC):
                            dve.bn_stats(bst[:, k, g - 1, :], NT[:, k, (g - 1) * GT:g * GT])
                for n in range(2):
                    ring.wait_taken(dve, GROUPS - 1, f"xt{n}")
                for k in range(KC):
                    ins = dve.bn_stats(bst[:, k, GROUPS - 1, :], NT[:, k, (GROUPS - 1) * GT:])
                ins.then_inc(setup, 1)
                dve.wait_ge(setup, 2)
                for k in range(KC):
                    dve.bn_aggr(mvb[:, k, :], bst[:, k, :, :].rearrange("p g s -> p (g s)")).then_inc(stats, 1)
                dve.wait_ge(sd_sq, 1)
                dve.wait_ge(w_loaded, 64)
                dve.reciprocal(sd[:, :], sd[:, :]).then_inc(setup, 1)
                dve.wait_ge(setup, 3)
                dve.tensor_tensor(bn[:, :, 0], sd[:, :], gamma[:, :], ALU.mult).then_inc(setup, 1)
                dve.wait_ge(setup, 4)
                dve.tensor_tensor(sd[:, :], mvb[:, :, 0], bn[:, :, 0], ALU.mult).then_inc(setup, 1)
                dve.wait_ge(setup, 5)
                dve.tensor_tensor(bn[:, :, 1], beta[:, :], sd[:, :], ALU.subtract)

        downT = sb("downT", [P, KC, PK_EXPERTS])
        up = sb("up", [P, ECH, D])
        iota_i = sb("iota_i", [P, P], I32)
        iota = sb("iota", [P, P])
        iota_h = sb("iota_h", [P, P], F16)
        iota_w = sb("iota_w", [P, P, TB], F16)
        nt = sb("nt", [P, 2, KC, P])
        xb = sb("xb", [P, 2, KC, P])
        best = sb("best", [P, 2, PK_HEADS, PK_TOP])
        best_i = sb("best_i", [P, 2, PK_HEADS, PK_TOP], U32)
        best_f = sb("best_f", [P, 2, PK_HEADS, PK_TOP])
        pairs = sb("pairs", [P, PK_HEADS, PK_TOP * PK_TOP])
        score = sb("score", [P, PK_HEADS, PK_TOP])
        pick = sb("pick", [P, PK_HEADS, PK_TOP], U32)
        half_i = sb("half_i", [P, 2, PICKS], U32)
        half_f = sb("half_f", [P, 2, PICKS])
        hot = sb("hot", [P, 2, PICKS, PK_TOP])
        key = sb("key", [P, 2, PICKS])
        eid = sb("eid", [P, PICKS])
        eid_i = sb("eid_i", [P, PICKS], I32)
        ehl_i = sb("ehl_i", [P, 2, PICKS], I32)
        sig = sb("sig", [P, PICKS])
        rows = sb("rows", [P, 3, 2, PICKS], F16)
        identh = sb("identh", [P, P], F16)
        cols = sb("cols", [P, 3, P], F16)
        lohot = sb("lohot", [P, 2, P, TB], F16)
        hihot = sb("hihot", [P, 2, ECH, TB], F16)
        hisig = sb("hisig", [P, 2, ECH, TB], F16)
        act_h = sb("act_h", [P, 2, ECH, P])
        new = sb("new", [P, D])
        bst = sb("bst", [P, 6])
        mv = sb("mv", [P, 2])
        NB = P // TB

        def bank(n):
            return ctx.enter_context(nc.psum_tensor(f"{tag}_ps{n}", [P, 512], F32))

        sims = Ring(f"{tag}_sims", sem, [bank(0), bank(1)], ["s0", "s1"])
        tail = Ring(f"{tag}_tail", sem, [bank(2), bank(3)], ["cols", "y"])
        hid = Ring(f"{tag}_hid", sem, [bank(4), bank(5)], [f"h{c}" for c in range(ECH // 4)])
        wts = Ring(f"{tag}_wts", sem, [bank(6), bank(7)], [f"w{b}" for b in range(NB)])
        w_loaded = sem("w2_loaded")
        pool_link = sem("pool_link")
        consts = sem("consts")
        xb_ready = sem("xb_ready")
        score_ready = sem("score_ready")
        sig_ready = sem("sig_ready")
        rows_ready = sem("rows_ready")
        hot_ready = sem("hot_ready")
        hihot_ready = sem("hihot_ready")
        dve_link = sem("dve_link")
        passed = sem("passed")
        block = ctx.enter_context(nc.Block())

        @block.sync
        def _(sp):
            sp.dma_start(downT[:, :, :], w["downT"][:, 0:PK_EXPERTS].rearrange("(k p) n -> p k n", p=P)).then_inc(
                w_loaded, 16)
            sp.dma_start(up[:, :, :], w["up"][0:PK_EXPERTS, :].rearrange("(c p) n -> p c n", p=P)).then_inc(
                w_loaded, 16)

        @block.gpsimd
        def _(pool):
            pool.iota(iota_i[:, :], [[1, P]], base=0, channel_multiplier=0).then_inc(pool_link, 1)
            pool.wait_ge(pool_link, 1)
            pool.tensor_copy(iota[:, :], iota_i[:, :]).then_inc(consts, 1)
            pool.tensor_copy(iota_h[:, :], iota_i[:, :]).then_inc(consts, 1)
            pool.tensor_copy(identh[:, :], ident[:, :]).then_inc(consts, 1)
            pool.wait_ge(pool_link, 1)
            pool.tensor_copy(iota_w[:, :, :], iota_i[:, :].rearrange("p (n a) -> p n a", a=1).broadcast_to(
                [P, P, TB])).then_inc(consts, 1)

        @block.scalar
        def _(act):
            def hidden(t, s, c):
                hid.wait_full(act, t, f"h{c}")
                hid.take(act.activation(act_h[:, s, 4 * c:4 * c + 4, :], hid.bank(f"h{c}")[:, :].rearrange(
                    "p (c n) -> p c n", c=4), ACT.Gelu), f"h{c}")

            def turn(i, last):
                for s in range(2):
                    t = i * 2 + s
                    act.wait_ge(score_ready, t + 1)
                    act.activation(sig[:, :], score[:, :, :].rearrange("p h k -> p (h k)"),
                                   ACT.Sigmoid).then_inc(sig_ready, 1)
                    tail.wait_full(act, t, "cols")
                    tail.take(act.activation(cols[:, :, :], tail.bank("cols")[:, :].bitcast(F16)[:, 0:3 * P].rearrange(
                        "p (c n) -> p c n", c=3), ACT.Copy), "cols")
                    if not (last and s == 1):
                        for c in range(ECH // 4):
                            hidden(t + 1, 1 - s, c)

            for c in range(ECH // 4):
                hidden(0, 0, c)
            with act.Fori(0, TILES // 2 - 1) as i:
                turn(i, False)
            turn(TILES // 2 - 1, True)

        @block.tensor
        def _(pe):
            for r in (sims, tail, hid, wts):
                r.start_empty(pe)
            pe.wait_ge(w_loaded, 32)
            pe.wait_ge(consts, 4)

            def similarity(t, s):
                pe.wait_ge(xb_ready, t + 1)
                for n in range(2):
                    sims.claim(pe, t, f"s{n}")
                    for k in range(KC):
                        ins = pe.matmul(sims.bank(f"s{n}")[:, :], xb[:, s, k, :], wm[:, k, n * 512:(n + 1) * 512],
                                        start=(k == 0), stop=(k == KC - 1))
                    sims.filled(ins)

            def hidden(t, s, c):
                hid.claim(pe, t, f"h{c}")
                for j in range(4):
                    for k in range(KC):
                        e = 4 * c + j
                        ins = pe.matmul(hid.bank(f"h{c}")[:, j * P:(j + 1) * P], downT[:, k, e * P:(e + 1) * P],
                                        nt[:, s, k, :], start=(k == 0), stop=(k == KC - 1))
                hid.filled(ins)

            def turn(i, last):
                for s in range(2):
                    t = i * 2 + s
                    more = not (last and s == 1)
                    tail.claim(pe, t, "cols")
                    pe.wait_ge(rows_ready, t + 1)
                    for n in range(3):
                        ins = pe.transpose(tail.bank("cols")[:, :].bitcast(F16)[:, n * P:(n + 1) * P],
                                           rows[:, n, :, :].rearrange("p a n -> p (a n)"), identh[:, :])
                    tail.filled(ins)
                    if more:
                        similarity(t + 1, 1 - s)
                    for b in range(NB):
                        wts.claim(pe, t, f"w{b}")
                        pe.wait_ge(hot_ready, t * NB + b + 1)
                        for j in range(TB):
                            ins = pe.matmul(wts.bank(f"w{b}")[:, j * ECH:(j + 1) * ECH], lohot[:, b % 2, :, j],
                                            hisig[:, b % 2, :, j], start=True, stop=True)
                        wts.filled(ins)
                        if more:
                            hidden(t + 1, 1 - s, b)
                    tail.claim(pe, t, "y")
                    for b in (NB - 2, NB - 1):
                        wts.wait_taken(pe, t, f"w{b}")
                    for c in range(ECH):
                        ins = pe.matmul(tail.bank("y")[:, 0:D], act_h[:, s, c, :], up[:, c, :], start=(c == 0),
                                        stop=(c == ECH - 1))
                    tail.filled(ins)

            similarity(0, 0)
            for c in range(ECH // 4):
                hidden(0, 0, c)
            with pe.Fori(0, TILES // 2 - 1) as i:
                turn(i, False)
            turn(TILES // 2 - 1, True)

        @block.vector
        def _(dve):
            dve.wait_ge(consts, 4)
            LINKS = 18

            def norm(t, s):
                for k in range(KC):
                    dve.tensor_scalar(nt[:, s, k, :], NT[:, k, bass.ds(t * P, P)], 1.0, None, ALU.mult)
                    ins = dve.tensor_scalar(xb[:, s, k, :], NT[:, k, bass.ds(t * P, P)], bn[:, k, 0:1], bn[:, k, 1:2],
                                            ALU.mult, ALU.add)
                ins.then_inc(xb_ready, 1)

            def picks(t, link):
                for n in range(2):
                    await_apart(dve, sims.full, t * 2 + n + 1, passed)
                    for h in range(PK_HEADS):
                        ins = dve.max(best[:, n, h, :], sims.bank(f"s{n}")[:, h * PK_KEYS:(h + 1) * PK_KEYS])
                    link.inc(ins)
                    await_apart(dve, link.sem, link.base + link.n, passed)
                    for h in range(PK_HEADS):
                        ins = dve.max_index(best_i[:, n, h, :], best[:, n, h, :],
                                            sims.bank(f"s{n}")[:, h * PK_KEYS:(h + 1) * PK_KEYS])
                    sims.take(ins, f"s{n}")
                for n in range(2):
                    sims.wait_taken(dve, t, f"s{n}")
                pair4 = pairs[:, :, :].rearrange("p h (i j) -> p h i j", i=PK_TOP)
                shape4 = [P, PK_HEADS, PK_TOP, PK_TOP]
                link.inc(dve.tensor_tensor(pair4,
                                           best[:, 0, :, :].rearrange("p h (i a) -> p h i a", a=1).broadcast_to(shape4),
                                           best[:, 1, :, :].rearrange("p h (a j) -> p h a j", a=1).broadcast_to(shape4),
                                           ALU.add))
                link.inc(dve.tensor_copy(best_f[:, :, :, :], best_i[:, :, :, :]))
                await_apart(dve, link.sem, link.base + link.n, passed)
                for h in range(PK_HEADS):
                    ins = dve.max(score[:, h, :], pairs[:, h, :])
                ins.then_inc(score_ready, 1)
                await_apart(dve, score_ready, t + 1, passed)
                for h in range(PK_HEADS):
                    ins = dve.max_index(pick[:, h, :], score[:, h, :], pairs[:, h, :])
                link.inc(ins)
                link.wait(dve)
                pk = pick[:, :, :].rearrange("p h k -> p (h k)")
                dve.tensor_scalar(half_i[:, 0, :], pk, 3, None, ALU.logical_shift_right)
                link.inc(dve.tensor_scalar(half_i[:, 1, :], pk, PK_TOP - 1, None, ALU.bitwise_and))
                link.wait(dve)
                link.inc(dve.tensor_copy(half_f[:, :, :], half_i[:, :, :]))
                link.wait(dve)
                wide = [P, 2 * PICKS, PK_TOP]
                link.inc(dve.tensor_tensor(hot[:, :, :, :].rearrange("p n k a -> p (n k) a"),
                                           half_f[:, :, :].rearrange("p n (k a) -> p (n k) a", a=1).broadcast_to(wide),
                                           iota[:, 0:PK_TOP].rearrange("p (a b) -> p a b", a=1).broadcast_to(wide),
                                           ALU.is_equal))
                link.wait(dve)
                for n in range(2):
                    h4 = hot[:, n, :, :].rearrange("p (h k) a -> p h k a", h=PK_HEADS)
                    ins = dve.tensor_tensor(h4, h4, best_f[:, n, :, :].rearrange(
                        "p h (b a) -> p h b a", b=1).broadcast_to([P, PK_HEADS, PK_TOP, PK_TOP]), ALU.mult)
                link.inc(ins)
                link.wait(dve)
                link.inc(dve.tensor_reduce(key[:, :, :], hot[:, :, :, :], AX_X, ALU.add))
                link.wait(dve)
                link.inc(dve.scalar_tensor_tensor(eid[:, :], key[:, 0, :], float(PK_KEYS), key[:, 1, :], ALU.mult,
                                                  ALU.add))
                link.wait(dve)
                link.inc(dve.tensor_copy(eid_i[:, :], eid[:, :]))
                link.wait(dve)
                dve.tensor_scalar(ehl_i[:, 0, :], eid_i[:, :], P - 1, None, ALU.bitwise_and)
                link.inc(dve.tensor_scalar(ehl_i[:, 1, :], eid_i[:, :], 7, None, ALU.logical_shift_right))
                link.wait(dve)
                dve.tensor_copy(rows[:, 0:2, 0, :], ehl_i[:, :, :])
                link.inc(dve.tensor_copy(rows[:, 0:2, 1, :], ehl_i[:, :, :]))
                dve.wait_ge(sig_ready, t + 1)
                link.inc(dve.tensor_scalar(sig[:, :], sig[:, :], LO_SCALE, None, ALU.mult))
                link.wait(dve)
                link.inc(dve.tensor_copy(rows[:, 2, 0, :], sig[:, :]))
                link.wait(dve)
                dve.tensor_tensor(rows[:, 2, 1, :], sig[:, :], rows[:, 2, 0, :], ALU.subtract).then_inc(rows_ready, 1)

            def weigh(t, s, b):
                wts.wait_full(dve, t, f"w{b}")
                hv = act_h[:, s, :, b * TB:(b + 1) * TB]
                wts.take(dve.tensor_tensor(hv, hv, wts.bank(f"w{b}")[:, :].rearrange("p (j c) -> p c j", c=ECH),
                                           ALU.mult), f"w{b}")

            def experts(t, s):
                tail.wait_taken(dve, t, "cols")
                for b in range(NB):
                    if b >= 2:
                        wts.wait_full(dve, t, f"w{b - 2}")
                    blk = slice(b * TB, (b + 1) * TB)

                    def spread(n, width):
                        return cols[:, n, blk].rearrange("p (a j) -> p a j", a=1).broadcast_to([P, width, TB])

                    dve.tensor_tensor(hihot[:, b % 2, :, :], iota_w[:, 0:ECH, :], spread(1, ECH),
                                      ALU.is_equal).then_inc(hihot_ready, 1)
                    dve.tensor_tensor(lohot[:, b % 2, :, :], iota_w[:, :, :], spread(0, P), ALU.is_equal)
                    dve.wait_ge(hihot_ready, t * NB + b + 1)
                    dve.tensor_tensor(hisig[:, b % 2, :, :], hihot[:, b % 2, :, :], spread(2, ECH),
                                      ALU.mult).then_inc(hot_ready, 1)
                    if b == 0:
                        hid.wait_taken(dve, t, f"h{ECH // 4 - 2}")
                        hid.wait_taken(dve, t, f"h{ECH // 4 - 1}")
                    if b:
                        weigh(t, s, b - 1)
                weigh(t, s, NB - 1)

            def finish(t, link):
                tail.wait_full(dve, t, "y")
                tail.take(dve.scalar_tensor_tensor(new[:, :].rearrange("p (a n) -> p a n", a=1),
                                                   tail.bank("y")[:, 0:D].rearrange("p (a n) -> p a n", a=1),
                                                   1.0 / LO_SCALE, X[:, bass.ds(t, 1), :], ALU.mult, ALU.add), "y")
                tail.wait_taken(dve, t, "y")
                finish_rows(dve, keep, link, t, new, bst, mv)

            def turn(i, last):
                for s in range(2):
                    t = i * 2 + s
                    link = Tally(dve_link, t, LINKS)
                    picks(t, link)
                    if not (last and s == 1):
                        norm(t + 1, 1 - s)
                    experts(t, s)
                    finish(t, link)
                    link.close()

            norm(0, 0)
            with dve.Fori(0, TILES // 2 - 1) as i:
                turn(i, False)
            turn(TILES // 2 - 1, True)


MOE = 8


def top2_experts(nc, keep, w, out):
    tag = "mo"
    with ExitStack() as ctx:
        def sb(name, shape, dt=F32):
            return ctx.enter_context(nc.sbuf_tensor(f"{tag}_{name}", shape, dt))

        def sem(name):
            return keep["semaphore"](f"{tag}_{name}")

        X, MV, ident = keep["X"], keep["MV"], keep["ident"]
        we = sb("we", [P, KC, MOE, D])
        gate = sb("gate", [P, KC, MOE])
        iota_i = sb("iota_i", [P, MOE], I32)
        iota = sb("iota", [P, MOE])
        rstd = sb("rstd", [P, TILES])
        xn = sb("xn", [P, G, D])
        xnT = sb("xnT", [P, KC, GT])
        lg = sb("lg", [P, G, MOE])
        top = sb("top", [P, G, 8])
        top_i = sb("top_i", [P, G, 8], U32)
        top_f = sb("top_f", [P, G, 2])
        e2 = sb("e2", [P, G])
        den = sb("den", [P, G])
        pair = sb("pair", [P, 2, G])
        wf = sb("wf", [P, G, MOE])
        wf2 = sb("wf2", [P, G, MOE])
        acc = sb("acc", [P, 2, G, D])
        banks = [ctx.enter_context(nc.psum_tensor(f"{tag}_ps{b}", [P, 512], F32)) for b in range(5)]
        ring = Ring(f"{tag}_ring", sem, banks, ["xt0", "xt1", "lg0", "lg1"]
                    + [f"e{q}_{u}" for u in range(G) for q in range(MOE // 2)])
        w_loaded = sem("w_loaded")
        pool_link = sem("pool_link")
        consts = sem("consts")
        rstd_sq = sem("rstd_sq")
        setup = sem("setup")
        xn_ready = sem("xn_ready")
        diff_ready = sem("diff_ready")
        e2_ready = sem("e2_ready")
        acc_ready = sem("acc_ready")
        stored = sem("stored")
        passed = sem("passed")
        dve_link = sem("dve_link")
        out_v = out.rearrange("t p d -> p t d")
        block = ctx.enter_context(nc.Block())

        @block.sync
        def _(sp):
            sp.dma_start(gate[:, :, :], w["gate"].rearrange("(k p) n -> p k n", p=P)).then_inc(w_loaded, 16)
            sp.dma_start(we[:, :, :, :], w["we"]).then_inc(w_loaded, 16)
            with sp.Fori(0, GROUPS) as g:
                sp.wait_ge(acc_ready, g + 1)
                sp.dma_start(out_v[:, bass.ds(g * G, G), :], acc[:, 1, :, :]).then_inc(stored, 16)
            sp.wait_ge(stored, 16 * (GROUPS + 1))

        @block.gpsimd
        def _(pool):
            pool.iota(iota_i[:, :], [[1, MOE]], base=0, channel_multiplier=0).then_inc(pool_link, 1)
            pool.wait_ge(pool_link, 1)
            pool.tensor_copy(iota[:, :], iota_i[:, :]).then_inc(consts, 1)

        @block.scalar
        def _(act):
            layer_norm_scale(act, None, keep, rstd, rstd_sq, None)
            with act.Fori(0, GROUPS) as g:
                for n in range(2):
                    ring.wait_full(act, g, f"xt{n}")
                    ring.take(act.activation(xnT[:, :, n * 256:(n + 1) * 256],
                                             ring.bank(f"xt{n}")[:, :].rearrange("p (k n) -> p k n", k=KC),
                                             ACT.Copy), f"xt{n}")
                act.wait_ge(diff_ready, g + 1)
                act.activation(e2[:, :], e2[:, :], ACT.Exp).then_inc(e2_ready, 1)

        @block.tensor
        def _(pe):
            ring.start_empty(pe)
            pe.wait_ge(w_loaded, 32)
            with pe.Fori(0, GROUPS) as g:
                for n in range(2):
                    ring.claim(pe, g, f"xt{n}")
                    for u in (2 * n, 2 * n + 1):
                        pe.wait_ge(xn_ready, g * G + u + 1)
                        for k in range(KC):
                            at = k * 256 + (u % 2) * P
                            ins = pe.transpose(ring.bank(f"xt{n}")[:, at:at + P], xn[:, u, k * P:(k + 1) * P],
                                               ident[:, :])
                    ring.filled(ins)
                for n in range(2):
                    ring.wait_taken(pe, g, f"xt{n}")
                for n in range(2):
                    ring.claim(pe, g, f"lg{n}")
                    for u in (2 * n, 2 * n + 1):
                        for k in range(KC):
                            ins = pe.matmul(ring.bank(f"lg{n}")[:, (u % 2) * MOE:(u % 2 + 1) * MOE],
                                            xnT[:, k, u * P:(u + 1) * P], gate[:, k, :], start=(k == 0),
                                            stop=(k == KC - 1))
                    ring.filled(ins)
                for u in range(G):
                    for q in range(MOE // 2):
                        ring.claim(pe, g, f"e{q}_{u}")
                        for k in range(KC):
                            ins = pe.matmul(ring.bank(f"e{q}_{u}")[:, :], xnT[:, k, u * P:(u + 1) * P],
                                            we[:, k, 2 * q:2 * q + 2, :].rearrange("p e n -> p (e n)"),
                                            start=(k == 0), stop=(k == KC - 1))
                        ring.filled(ins)

        @block.vector
        def _(dve):
            layer_norm_scale(None, dve, keep, rstd, rstd_sq, setup)
            dve.wait_ge(consts, 1)
            dve.sem_inc(stored, 16)
            with dve.Fori(0, GROUPS) as g:
                link = Tally(dve_link, g, 11 + 4 * G)
                for u in range(G):
                    t = g * G + u
                    dve.tensor_scalar(xn[:, u:u + 1, :], X[:, bass.ds(t, 1), :], MV[:, bass.ds(t, 1), 0],
                                      rstd[:, bass.ds(t, 1)], ALU.subtract, ALU.mult).then_inc(xn_ready, 1)
                for n in range(2):
                    ring.wait_full(dve, g, f"lg{n}")
                    ring.take(dve.tensor_copy(lg[:, 2 * n:2 * n + 2, :], ring.bank(f"lg{n}")[:, 0:2 * MOE].rearrange(
                        "p (u e) -> p u e", u=2)), f"lg{n}")
                for n in range(2):
                    use = f"lg{n}"
                    m = ring.at[use]
                    await_apart(dve, ring.taken[m % ring.n_banks],
                                g * (ring.per // ring.n_banks) + m // ring.n_banks + 2, passed)
                for u in range(G):
                    ins = dve.max(top[:, u, :], lg[:, u, :])
                link.inc(ins)
                await_apart(dve, link.sem, link.base + link.n, passed)
                for u in range(G):
                    ins = dve.max_index(top_i[:, u, :], top[:, u, :], lg[:, u, :])
                link.inc(ins)
                dve.tensor_tensor(e2[:, :], top[:, :, 1], top[:, :, 0], ALU.subtract).then_inc(diff_ready, 1)
                link.wait(dve)
                link.inc(dve.tensor_copy(top_f[:, :, :], top_i[:, :, 0:2]))
                dve.wait_ge(e2_ready, g + 1)
                link.inc(dve.tensor_scalar(den[:, :], e2[:, :], 1.0, None, ALU.add))
                link.wait(dve)
                link.inc(dve.reciprocal(pair[:, 0, :], den[:, :]))
                link.wait(dve)
                link.inc(dve.tensor_tensor(pair[:, 1, :], e2[:, :], pair[:, 0, :], ALU.mult))
                link.wait(dve)
                shape = [P, G, MOE]
                place = iota[:, :].rearrange("p (a e) -> p a e", a=1).broadcast_to(shape)
                for n, dst in ((0, wf), (1, wf2)):
                    link.inc(dve.tensor_tensor(dst[:, :, :], top_f[:, :, n:n + 1].broadcast_to(shape), place,
                                               ALU.is_equal))
                    link.wait(dve)
                    link.inc(dve.tensor_tensor(dst[:, :, :], dst[:, :, :], pair[:, n, :].rearrange(
                        "p (u a) -> p u a", a=1).broadcast_to(shape), ALU.mult))
                    link.wait(dve)
                link.inc(dve.tensor_tensor(wf[:, :, :], wf[:, :, :], wf2[:, :, :], ALU.add))
                link.wait(dve)
                dve.wait_ge(stored, g * 16 + 16)
                for u in range(G):
                    t = g * G + u
                    for q in range(MOE // 2):
                        ring.wait_full(dve, g, f"e{q}_{u}")
                        for j in range(2):
                            e = 2 * q + j
                            src = ring.bank(f"e{q}_{u}")[:, j * D:(j + 1) * D].rearrange("p (a n) -> p a n", a=1)
                            prev = X[:, bass.ds(t, 1), :] if e == 0 else acc[:, (e + 1) % 2, u:u + 1, :]
                            ins = dve.scalar_tensor_tensor(acc[:, e % 2, u:u + 1, :], src, wf[:, u, e:e + 1], prev,
                                                           ALU.mult, ALU.add)
                            if j == 0:
                                link.inc(ins)
                                link.wait(dve)
                            else:
                                ring.take(ins, f"e{q}_{u}")
                                ring.wait_taken(dve, g, f"e{q}_{u}")
                dve.sem_inc(acc_ready, 1)
                link.close()


def build(nc, a, out, stages):
    with ExitStack() as ctx:
        def sb(name, shape, dt=F32):
            return ctx.enter_context(nc.sbuf_tensor(name, shape, dt))

        keep = {"X": sb("X", [P, TILES, D]), "MV": sb("MV", [P, TILES, 2]), "ident": sb("ident", [P, P]),
                "eps": sb("eps", [P, 1]), "tau": sb("tau", [P, TILES]), "quarter": sb("quarter", [P, 1]),
                "delta_rows": a["delta_rows"]}
        X, MV, ident = keep["X"], keep["MV"], keep["ident"]
        in_use = []

        def semaphore(name):
            in_use.append(nc.alloc_semaphore(name))
            return in_use[-1]

        def clear_semaphores():
            nc.clear_and_free_semaphores(in_use)
            nc.all_engine_barrier()
            in_use.clear()

        keep["semaphore"] = semaphore
        with ExitStack() as c2:
            x_loaded = c2.enter_context(nc.semaphore("x_loaded"))
            c_loaded = c2.enter_context(nc.semaphore("c_loaded"))
            id_zero = c2.enter_context(nc.semaphore("id_zero"))
            start_link = c2.enter_context(nc.semaphore("start_link"))
            bst = c2.enter_context(nc.sbuf_tensor("bst0", [P, TILES, 6], F32))
            block = c2.enter_context(nc.Block())

            @block.sync
            def _(sp):
                sp.dma_start(X[:, :, :], a["x"].rearrange("t p d -> p t d")).then_inc(x_loaded, 16)
                sp.dma_start(keep["tau"][:, :], a["tau"]).then_inc(c_loaded, 16)
                sp.dma_start(keep["quarter"][:, :], a["quarter"]).then_inc(c_loaded, 16)
                sp.wait_ge(c_loaded, 32)

            @block.gpsimd
            def _(pool):
                pool.memset(ident[:, :], 0.0).then_inc(id_zero, 1)
                pool.memset(keep["eps"][:, :], LN_EPS)
                pool.wait_ge(id_zero, 1)
                pool.affine_select(out=ident[:, :], in_=ident[:, :], compare_op=ALU.not_equal, fill=1.0,
                                   base=0, pattern=[[-1, P]], channel_multiplier=1)

            @block.vector
            def _(dve):
                dve.wait_ge(x_loaded, 16)
                for t in range(TILES):
                    ins = dve.bn_stats(bst[:, t, :], X[:, t, :])
                ins.then_inc(start_link, 1)
                dve.wait_ge(start_link, 1)
                for t in range(TILES):
                    dve.bn_aggr(MV[:, t, :], bst[:, t, :])

        def att(n):
            return {k: a[f"L{n}_{k}"] for k in ("wq", "wk", "wv", "wo", "bq", "bk", "bv", "bo")}

        if stages >= 1:
            attention(nc, keep, "a0", att(0), a["ctxT"])
        if stages >= 2:
            row_dram = nc.dram_tensor("row_dram", (TOKENS, ROW), F32, kind="Internal").ap()
            sum_dram = nc.dram_tensor("sum_dram", (TOKENS, D), F32, kind="Internal").ap()
            with ExitStack() as c2:
                idx = c2.enter_context(nc.sbuf_tensor("idx", [P, EXPERTS, SLOTS], U32))
                probs = c2.enter_context(nc.sbuf_tensor("gate_probs", [P, TILES, EXPERTS], F32))
                fw = {k: a[f"L0_{k}"] for k in ("gate", "Ws1", "Ws2", "bs1", "bs2", "W1", "W2", "b1", "b2")}
                shared_ffn(nc, keep, fw, probs, row_dram, sum_dram)
                choose_tokens(nc, keep, probs, idx)
                routed_ffn(nc, keep, fw, idx, row_dram, sum_dram)
        clear_semaphores()
        if stages >= 3:
            attention(nc, keep, "a1", att(1), a["ctxT"])
        if stages >= 4:
            bit_ffn(nc, keep, {n: a[f"L1_{n}"] for n in ("w_gate", "w_up", "w_down")})
        if stages >= 5:
            windowed_attention(nc, keep, {n: a[f"L2_{n}"] for n in ("W_a", "W_c", "pt", "len")}, a["ctxT"], a["ctx"])
        clear_semaphores()
        if stages >= 6:
            product_key_experts(nc, keep, {n: a[f"L2_{n}"] for n in ("w_q", "keys", "gamma", "beta", "downT", "up")})
        if stages >= 7:
            attention(nc, keep, "a3", att(3), a["ctxT"])
        if stages >= 8:
            top2_experts(nc, keep, {n: a[f"L3_{n}"] for n in ("gate", "we")}, out)
            return
        with ExitStack() as c2:
            stored = c2.enter_context(nc.semaphore("stored"))
            block = c2.enter_context(nc.Block())

            @block.sync
            def _(sp):
                sp.dma_start(out.rearrange("t p d -> p t d"), X[:, :, :]).then_inc(stored, 16)
                sp.wait_ge(stored, 16)


STAGES = 8


def lay_out(i):
    import numpy as np

    def rows(v):
        return np.ascontiguousarray(np.broadcast_to(np.asarray(v).reshape(1, -1), (P, np.asarray(v).size)))

    def padded(wt):
        o = np.zeros((wt.shape[0], HC * 4, 32), np.float32)
        o[:, :, 0:DK] = wt.reshape(wt.shape[0], HC * 4, DK)
        return o.reshape(wt.shape[0], HC * P)

    def turned(w):
        return np.ascontiguousarray(np.asarray(w).T)

    a = {"x": np.asarray(i["x"]), "ctxT": turned(np.asarray(i["ctx_1024"]).reshape(TILES * P, D))}
    a["tau"] = rows(i["condB_tau"])
    dr = np.zeros((P, TILES * P), np.float32)
    dr[DK::32, :] = np.asarray(i["fside_BxS2_0"]).reshape(1, -1)
    a["delta_rows"] = dr
    qr = np.zeros((P, 1), np.float32)
    qr[DK::32, :] = 1.0 / DK ** 0.5
    a["quarter"] = qr
    for n in (0, 1, 3):
        for m in "qk":
            a[f"L{n}_w{m}"] = padded(turned(i[f"L{n}_xcond_W{m}"]))
            a[f"L{n}_b{m}"] = turned(padded(np.asarray(i[f"L{n}_xcond_b{m}"]).reshape(1, -1)).reshape(HC, P))
        for m in "vo":
            a[f"L{n}_w{m}"] = turned(i[f"L{n}_xcond_W{m}"])
            a[f"L{n}_b{m}"] = rows(i[f"L{n}_xcond_b{m}"])
    for m in ("gate", "Ws1", "Ws2", "W1", "W2"):
        a[f"L0_{m}"] = np.asarray(i[f"L0_ffn_{m}"])
    a["L0_bs1"] = turned(np.asarray(i["L0_ffn_bs1"]).reshape(HCH, P))
    a["L0_bs2"] = rows(i["L0_ffn_bs2"])
    a["L0_b1"] = np.ascontiguousarray(np.asarray(i["L0_ffn_b1"]).reshape(EXPERTS, HCH, P).transpose(2, 0, 1))
    a["ctx"] = np.asarray(i["ctx_1024"]).reshape(TILES * P, D)
    for m in ("w_gate", "w_up", "w_down"):
        a[f"L1_{m}"] = turned(i[f"L1_ffn_{m}"])
    a["L2_W_a"] = np.asarray(i["L2_xcond_W_a"])
    a["L2_W_c"] = turned(i["L2_xcond_W_c"])
    a["L2_pt"] = rows(i["condB_pt"])
    a["L2_len"] = rows(i["_lenS2"])
    a["L2_w_q"] = np.asarray(i["L2_ffn_w_q"])
    a["L2_keys"] = np.ascontiguousarray(np.asarray(i["L2_ffn_keys_p"]).transpose(3, 2, 0, 1)).reshape(
        PK_DIM, 2 * PK_HEADS, PK_KEYS)
    a["L2_gamma"] = turned(np.asarray(i["L2_ffn_bn_gamma"]).reshape(KC, P))
    a["L2_beta"] = turned(np.asarray(i["L2_ffn_bn_beta"]).reshape(KC, P))
    a["L2_downT"] = turned(i["L2_ffn_down"])
    a["L2_up"] = np.asarray(i["L2_ffn_up"])
    a["L3_gate"] = turned(i["L3_ffn_gate_w"])
    a["L3_we"] = np.ascontiguousarray(np.asarray(i["L3_ffn_expert_w"]).transpose(2, 0, 1).reshape(
        KC, P, MOE, D).transpose(1, 0, 2, 3))
    a["L0_b2"] = np.ascontiguousarray(np.broadcast_to(np.asarray(i["L0_ffn_b2"])[None], (P, EXPERTS, D)))
    return a


def kernel(**inputs):
    import numpy as np
    import concourse.bacc as bacc
    from concourse.bass_utils import run_bass_kernel_spmd

    arrays = lay_out(inputs)
    nc = bacc.Bacc("TRN2", target_bir_lowering=False, num_devices=1)
    a = {n: nc.dram_tensor(f"in_{n}", v.shape, mybir.dt.from_np(v.dtype), kind="ExternalInput").ap()
         for n, v in arrays.items()}
    out = nc.dram_tensor("out_0", (TILES, P, D), F32, kind="ExternalOutput").ap()
    build(nc, a, out, STAGES)
    r = run_bass_kernel_spmd(nc, [{f"in_{n}": v for n, v in arrays.items()}], core_ids=[0])
    return r.results[0]["out_0"]
```

```python
from contextlib import ExitStack

import concourse.bass as bass
from concourse import mybir

ALU = mybir.AluOpType
ACT = mybir.ActivationFunctionType
F32 = mybir.dt.float32
BF16 = mybir.dt.bfloat16
F16 = mybir.dt.float16
I32 = mybir.dt.int32
U32 = mybir.dt.uint32
AX_X = mybir.AxisListType.X

P = 128
TILES = 32
D = 256
KC = D // P
HEADS = 16
DK = D // HEADS
HC = 4
G = 4
GT = G * P
GROUPS = TILES // G
LN_EPS = 1e-5


class Tally:

    def __init__(self, sem, turn, per):
        self.sem, self.base, self.per, self.n = sem, turn * per, per, 0

    def inc(self, ins):
        ins.then_inc(self.sem, 1)
        self.n += 1

    def wait(self, eng):
        eng.wait_ge(self.sem, self.base + self.n)

    def close(self):
        assert self.n == self.per, (self.sem, self.n, self.per)


def await_apart(eng, sem, value, passed):
    eng.wait_ge(sem, value)
    eng.sem_inc(passed, 1)


class Ring:

    def __init__(self, name, sem, banks, uses):
        assert len(uses) % len(banks) == 0
        self.banks, self.uses = banks, uses
        self.n_banks, self.per = len(banks), len(uses)
        self.full = sem(name + "_full")
        self.taken = [sem(f"{name}_taken{b}") for b in range(len(banks))]
        self.at = {u: n for n, u in enumerate(uses)}

    def bank(self, use):
        return self.banks[self.at[use] % self.n_banks]

    def start_empty(self, eng):
        for s in self.taken:
            eng.sem_inc(s, 1)

    def skip(self, eng, use):
        eng.sem_inc(self.full, 1)
        eng.sem_inc(self.taken[self.at[use] % self.n_banks], 1)

    def claim(self, pe, turn, use):
        n = self.at[use]
        pe.wait_ge(self.taken[n % self.n_banks], turn * (self.per // self.n_banks) + n // self.n_banks + 1)

    def wait_full(self, eng, turn, use):
        eng.wait_ge(self.full, turn * self.per + self.at[use] + 1)

    def filled(self, ins):
        ins.then_inc(self.full, 1)

    def take(self, ins, use):
        ins.then_inc(self.taken[self.at[use] % self.n_banks], 1)

    def wait_taken(self, eng, turn, use):
        n = self.at[use]
        eng.wait_ge(self.taken[n % self.n_banks], turn * (self.per // self.n_banks) + n // self.n_banks + 2)


def finish_rows(dve, keep, link, t, new, bst, mv):
    link.wait(dve)
    link.inc(dve.bn_stats(bst[:, :], new[:, :]))
    link.wait(dve)
    dve.tensor_scalar(keep["X"][:, bass.ds(t, 1), :], new[:, :].rearrange("p (a n) -> p a n", a=1), 1.0, None,
                      ALU.mult)
    link.inc(dve.bn_aggr(mv[:, :], bst[:, :]))
    link.wait(dve)
    dve.tensor_scalar(keep["MV"][:, bass.ds(t, 1), :], mv[:, :].rearrange("p (a n) -> p a n", a=1), 1.0, None,
                      ALU.mult)


def attention(nc, keep, tag, w, ctxT):
    with ExitStack() as ctx:
        def sb(name, shape, dt=F32):
            return ctx.enter_context(nc.sbuf_tensor(f"{tag}_{name}", shape, dt))

        def sem(name):
            return keep["semaphore"](f"{tag}_{name}")

        def psum(name, shape):
            return ctx.enter_context(nc.psum_tensor(f"{tag}_ps_{name}", shape, F32))

        X, MV, ident = keep["X"], keep["MV"], keep["ident"]
        wq = sb("wq", [P, KC, HC * P])
        wk = sb("wk", [P, KC, HC * P])
        wv = sb("wv", [P, KC, D])
        wo = sb("wo", [P, KC, D])
        bq = sb("bq", [P, HC])
        bk = sb("bk", [P, HC])
        bv = sb("bv", [P, D])
        bo = sb("bo", [P, D])
        delta = sb("delta", [P, TILES * P])
        tau4 = sb("tau4", [P, TILES])
        rstd = sb("rstd", [P, TILES])
        rstd_tau = sb("rstd_tau", [P, TILES])
        bq_tau = sb("bq_tau", [P, HC, TILES])
        ctx_t = sb("ctx_t", [P, 2, KC, P])
        xn = sb("xn", [P, D])
        xnT = sb("xnT", [P, KC, P])
        vraw = sb("vraw", [P, D])
        qT = sb("qT", [P, HC, P])
        kT = sb("kT", [P, 2, HC, P])
        v32 = sb("v32", [P, D])
        kraw = sb("kraw", [P, HC, P])
        v_parts = sb("v_parts", [P, 2, 2, HEADS, DK + 1], F16)
        probs = sb("probs", [P, 2, HEADS * P])
        pT = sb("pT", [P, 2, HEADS, P], F16)
        mx = sb("mx", [P, HEADS])
        rden = sb("rden", [P, HEADS])
        on = sb("on", [P, D])
        oT = sb("oT", [P, KC, P])
        tmp = sb("tmp", [P, D])
        new = sb("new", [P, D])
        bst = sb("bst", [P, 6])
        mv = sb("mv", [P, 2])

        ps_s = psum("s", [P, 4, HC, P])
        tr = Ring(f"{tag}_tr", sem, [psum("t0", [P, 4, P]), psum("t1", [P, 4, P])], [f"t{j}" for j in range(4)])
        proj = Ring(f"{tag}_proj", sem, [psum("p", [P, 512])], ["v", "x", "k", "q"])
        outs = Ring(f"{tag}_outs", sem, [psum("o", [P, 512])], ["pv", "ot", "y"])

        w_loaded = sem("w_loaded")
        ctx_loaded = [sem(f"ctx_loaded{s}") for s in range(2)]
        rstd_sq = sem("rstd_sq")
        xn_ready = sem("xn_ready")
        s_ready = sem("s_ready")
        s_taken = sem("s_taken")
        p_ready = sem("p_ready")
        high_ready = sem("high_ready")
        pool_link = sem("pool_link")
        v_ready = sem("v_ready")
        k_ready = sem("k_ready")
        shift_link = sem("shift_link")
        norm_link = sem("norm_link")
        row_link = sem("row_link")
        setup_link = sem("setup_link")

        loads = [(wq[:, :, :], w["wq"].rearrange("(k p) n -> p k n", p=P)),
                 (wk[:, :, :], w["wk"].rearrange("(k p) n -> p k n", p=P)),
                 (wv[:, :, :], w["wv"].rearrange("(k p) n -> p k n", p=P)),
                 (wo[:, :, :], w["wo"].rearrange("(k p) n -> p k n", p=P)),
                 (delta[:, :], keep["delta_rows"]), (bq[:, :], w["bq"]), (bk[:, :], w["bk"]),
                 (bv[:, :], w["bv"]), (bo[:, :], w["bo"])]
        ctx_v = ctxT.rearrange("(k p) n -> p k n", p=P)
        block = ctx.enter_context(nc.Block())

        def slots(eng, slot):
            for t in range(2):
                slot(t, t, None)
            with eng.Fori(1, TILES // 2 - 2) as i:
                for s in range(2):
                    slot(i * 2 + s, s, None)
            for t in range(TILES - 4, TILES):
                slot(t, t % 2, TILES - 1 - t)

        def is_first(t):
            return isinstance(t, int) and t == 0

        @block.sync
        def _(sp):
            for dst, src in loads:
                sp.dma_start(dst, src).then_inc(w_loaded, 16)
            for s in range(2):
                sp.dma_start(ctx_t[:, s, :, :], ctx_v[:, :, s * P:(s + 1) * P]).then_inc(ctx_loaded[s], 16)
            with sp.Fori(1, TILES // 2) as i:
                for s in range(2):
                    proj.wait_full(sp, i * 2 + s - 1, "v")
                    sp.dma_start(ctx_t[:, s, :, :], ctx_v[:, :, bass.ds((i * 2 + s) * P, P)]).then_inc(
                        ctx_loaded[s], 16)

        @block.scalar
        def _(act):
            def norm_columns(t):
                proj.wait_full(act, t, "x")
                proj.take(act.activation(xnT[:, :, :], proj.bank("x")[:, 0:D].rearrange("p (k n) -> p k n", k=KC),
                                         ACT.Copy), "x")

            def keys(t):
                proj.wait_full(act, t, "k")
                if not is_first(t):
                    act.wait_ge(k_ready, t)
                for c in range(HC):
                    ins = act.activation(kraw[:, c, :], proj.bank("k")[:, c * P:(c + 1) * P], ACT.Identity,
                                         bias=bk[:, c:c + 1])
                proj.take(ins, "k")

            def values(t):
                proj.wait_full(act, t + 1, "v")
                if not is_first(t):
                    act.wait_ge(v_ready, t)
                proj.take(act.activation(vraw[:, :], proj.bank("v")[:, 0:D], ACT.Copy), "v")

            def exps(t, s, half):
                act.wait_ge(s_taken, 2 * t + half + 3)
                p = probs[:, s, half * 8 * P:(half + 1) * 8 * P]
                act.activation(p, p, ACT.Exp).then_inc(p_ready, 1)

            def turned_outputs(t):
                outs.wait_full(act, t, "ot")
                outs.take(act.activation(oT[:, :, :], outs.bank("ot")[:, 0:D].rearrange("p (k n) -> p k n", k=KC),
                                         ACT.Copy), "ot")

            def high_parts(t, j):
                tr.wait_full(act, t, f"t{j}")
                act.activation(pT[:, 0, 4 * j:4 * j + 4, :], tr.bank(f"t{j}")[:, :, :], ACT.Copy).then_inc(
                    high_ready, 1)

            def slot(t, s, after):
                high_parts(t, 0)
                high_parts(t, 1)
                if not is_first(t):
                    turned_outputs(t - 1)
                if after is None or after >= 1:
                    values(t + 1)
                high_parts(t, 2)
                if after is None or after >= 2:
                    norm_columns(t + 2)
                high_parts(t, 3)
                if after is None or after >= 2:
                    keys(t + 2)
                if after is None or after >= 1:
                    for half in range(2):
                        exps(t + 1, 1 - s, half)

            act.activation(rstd[:, :], MV[:, :, 1], ACT.Sqrt, bias=keep["eps"][:, 0:1]).then_inc(rstd_sq, 1)
            act.wait_ge(setup_link, 5)
            norm_columns(0)
            keys(0)
            values(0)
            norm_columns(1)
            for half in range(2):
                exps(0, 0, half)
            keys(1)
            slots(act, slot)
            turned_outputs(TILES - 1)

        @block.gpsimd
        def _(pool):
            def values(t, s):
                link = Tally(pool_link, t, 2)
                high, low = (v_parts[:, s, n, :, 0:DK] for n in range(2))
                proj.wait_taken(pool, t + 1, "v")
                link.inc(pool.tensor_tensor(v32[:, :], vraw[:, :], bv[:, :], ALU.add))
                link.inc(pool.tensor_tensor(high, vraw[:, :].rearrange("p (h d) -> p h d", h=HEADS),
                                            bv[:, :].rearrange("p (h d) -> p h d", h=HEADS), ALU.add))
                link.wait(pool)
                pool.tensor_tensor(low, v32[:, :].rearrange("p (h d) -> p h d", h=HEADS), high,
                                   ALU.subtract).then_inc(v_ready, 1)
                link.close()

            def keys(t, s):
                proj.wait_taken(pool, t, "k")
                pool.tensor_tensor(kT[:, s, :, :], kraw[:, :, :], delta[:, bass.ds(t * P, P)].rearrange(
                    "p (a n) -> p a n", a=1).broadcast_to([P, HC, P]), ALU.add).then_inc(k_ready, 1)

            pool.wait_ge(w_loaded, 16 * len(loads))
            keys(0, 0)
            values(0, 0)
            keys(1, 1)
            values(1, 1)
            with pool.Fori(1, TILES // 2) as i:
                for s in range(2):
                    keys(i * 2 + s, s)
                    values(i * 2 + s, s)

        @block.tensor
        def _(pe):
            for r in (tr, proj, outs):
                r.start_empty(pe)
            pe.sem_inc(s_taken, 2)
            pe.wait_ge(w_loaded, 16 * len(loads))

            def norm_columns(t):
                proj.claim(pe, t, "x")
                pe.wait_ge(xn_ready, t + 1)
                for k in range(KC):
                    ins = pe.transpose(proj.bank("x")[:, k * P:(k + 1) * P], xn[:, k * P:(k + 1) * P], ident[:, :])
                proj.filled(ins)

            def project(t, use, wt, rhs):
                proj.claim(pe, t, use)
                for c in range(HC):
                    for k in range(KC):
                        ins = pe.matmul(proj.bank(use)[:, c * P:(c + 1) * P], wt[:, k, c * P:(c + 1) * P],
                                        rhs[:, k, :], start=(k == 0), stop=(k == KC - 1))
                        if (c, k) == (HC - 1, KC - 1):
                            proj.filled(ins)
                        yield

            def queries(t):
                return project(t, "q", wq, xnT)

            def keys(t, s):
                pe.wait_ge(ctx_loaded[s], (t - s) * 8 + 16)
                return project(t, "k", wk, ctx_t[:, s, :, :])

            def finish(steps):
                for _ in steps:
                    pass

            def values(t, s):
                proj.claim(pe, t + 1, "v")
                for k in range(KC):
                    ins = pe.matmul(proj.bank("v")[:, 0:D], ctx_t[:, s, k, :], wv[:, k, :], start=(k == 0),
                                    stop=(k == KC - 1))
                proj.filled(ins)

            def scores(t, s, half, beside):
                pe.wait_ge(s_taken, 2 * t + half + 1)
                if half == 0:
                    pe.wait_ge(k_ready, t + 1)
                for c in range(HC):
                    for r in (2 * half, 2 * half + 1):
                        if c == 0 and r == 0:
                            proj.wait_taken(pe, t, "q")
                        ins = pe.matmul(ps_s[:, r, c, :], qT[32 * r:32 * r + 32, c, :], kT[32 * r:32 * r + 32, s, c, :],
                                        start=True, stop=True, skip_group_check=True)
                        if (c, r) == (HC - 1, 2 * half + 1):
                            ins.then_inc(s_ready, 1)
                        next(beside, None)

            def turn_outputs(t):
                outs.claim(pe, t, "ot")
                for k in range(KC):
                    ins = pe.transpose(outs.bank("ot")[:, k * P:(k + 1) * P], on[:, k * P:(k + 1) * P], ident[:, :])
                outs.filled(ins)

            def output_rows(t):
                outs.claim(pe, t, "y")
                for k in range(KC):
                    ins = pe.matmul(outs.bank("y")[:, 0:D], oT[:, k, :], wo[:, k, :], start=(k == 0),
                                    stop=(k == KC - 1))
                outs.filled(ins)

            def turn_probs(t, s, j):
                if j % 2 == 0:
                    pe.wait_ge(p_ready, 2 * t + j // 2 + 1)
                tr.claim(pe, t, f"t{j}")
                for c in range(4):
                    ins = pe.transpose(tr.bank(f"t{j}")[:, c, :], probs[:, s, (4 * j + c) * P:(4 * j + c + 1) * P],
                                       ident[:, :])
                tr.filled(ins)

            def weighted_values(s, j, beside):
                for c in range(4):
                    h = 4 * c + j
                    for n in range(4):
                        ins = pe.matmul(outs.bank("pv")[:, h * (DK + 1):(h + 1) * (DK + 1)],
                                        pT[:, n // 2, 4 * j + c, :], v_parts[:, s, n % 2, h, :], start=(n == 0),
                                        stop=(n == 3), skip_group_check=True)
                    next(beside, None)
                return ins

            def slot(t, s, after):
                turn_probs(t, s, 0)
                turn_probs(t, s, 1)
                if not is_first(t):
                    turn_outputs(t - 1)
                if after is None or after >= 1:
                    values(t + 1, 1 - s)
                turn_probs(t, s, 2)
                more = after is None or after >= 2
                if more:
                    norm_columns(t + 2)
                turn_probs(t, s, 3)
                beside = keys(t + 2, s) if more else iter(())
                if after is None or after >= 1:
                    scores(t + 1, 1 - s, 0, beside)
                if not is_first(t):
                    output_rows(t - 1)
                if after is None or after >= 1:
                    scores(t + 1, 1 - s, 1, beside)
                finish(beside)
                outs.claim(pe, t, "pv")
                pe.wait_ge(v_ready, t + 1)
                for j in range(4):
                    tr.wait_taken(pe, t, f"t{j}")
                    if j == 1 and more:
                        beside = queries(t + 2)
                    ins = weighted_values(s, j, beside)
                outs.filled(ins)
                finish(beside)

            proj.skip(pe, "v")
            norm_columns(0)
            finish(keys(0, 0))
            finish(queries(0))
            values(0, 0)
            for half in range(2):
                scores(0, 0, half, iter(()))
            norm_columns(1)
            finish(keys(1, 1))
            finish(queries(1))
            slots(pe, slot)
            turn_outputs(TILES - 1)
            output_rows(TILES - 1)

        @block.vector
        def _(dve):
            def norm(t):
                if not is_first(t):
                    proj.wait_full(dve, t - 1, "x")
                dve.tensor_scalar(xn[:, :].rearrange("p (a n) -> p a n", a=1), X[:, bass.ds(t, 1), :],
                                  MV[:, bass.ds(t, 1), 0], rstd_tau[:, bass.ds(t, 1)], ALU.subtract,
                                  ALU.mult).then_inc(xn_ready, 1)

            def queries(t):
                proj.wait_full(dve, t, "q")
                proj.take(dve.tensor_tensor(qT[:, :, :], proj.bank("q")[:, :].rearrange("p (c n) -> p c n", c=HC),
                                            bq_tau[:, :, bass.ds(t, 1)].broadcast_to([P, HC, P]), ALU.add), "q")

            def shift(t, s, half):
                link = Tally(shift_link, 2 * t + half, 1)
                dve.wait_ge(s_ready, 2 * t + half + 1)
                sv = ps_s[:, 2 * half:2 * half + 2, :, :].rearrange("p r c n -> p (r c) n")
                m = mx[:, 8 * half:8 * half + 8]
                link.inc(dve.tensor_reduce(m, sv, AX_X, ALU.max))
                link.wait(dve)
                if not (isinstance(t, int) and t < 2):
                    tr.wait_full(dve, t - 2, f"t{2 * half + 1}")
                dve.tensor_tensor(probs[:, s, half * 8 * P:(half + 1) * 8 * P].rearrange("p (h n) -> p h n", n=P), sv,
                                  m.rearrange("p (h a) -> p h a", a=1).broadcast_to([P, 8, P]),
                                  ALU.subtract).then_inc(s_taken, 1)
                link.close()

            def divide(t):
                link = Tally(norm_link, t, 1)
                b = outs.bank("pv")[:, 0:HEADS * (DK + 1)].rearrange("p (h d) -> p h d", h=HEADS)
                outs.wait_full(dve, t, "pv")
                link.inc(dve.reciprocal(rden[:, :], b[:, :, DK]))
                link.wait(dve)
                outs.take(dve.tensor_tensor(on[:, :].rearrange("p (h d) -> p h d", h=HEADS), b[:, :, 0:DK],
                                            rden[:, :].rearrange("p (h a) -> p h a", a=1).broadcast_to(
                                                [P, HEADS, DK]), ALU.mult), "pv")
                link.close()

            def read_rows(t):
                outs.wait_full(dve, t, "y")
                outs.take(dve.tensor_tensor(tmp[:, :], outs.bank("y")[:, 0:D], bo[:, :], ALU.add), "y")

            def finish(t):
                link = Tally(row_link, t, 3)
                outs.wait_taken(dve, t, "y")
                link.inc(dve.tensor_tensor(new[:, :].rearrange("p (a n) -> p a n", a=1), X[:, bass.ds(t, 1), :],
                                           tmp[:, :].rearrange("p (a n) -> p a n", a=1), ALU.add))
                finish_rows(dve, keep, link, t, new, bst, mv)
                link.close()

            def low_parts(t, j):
                dve.wait_ge(high_ready, 4 * t + j + 1)
                at = slice(4 * j, 4 * j + 4)
                tr.take(dve.tensor_tensor(pT[:, 1, at, :], tr.bank(f"t{j}")[:, :, :], pT[:, 0, at, :],
                                          ALU.subtract), f"t{j}")

            def slot(t, s, after):
                for j in range(4):
                    low_parts(t, j)
                if not (isinstance(t, int) and t < 2):
                    finish(t - 2)
                if after is None or after >= 3:
                    norm(t + 3)
                if not is_first(t):
                    read_rows(t - 1)
                if after is None or after >= 1:
                    for half in range(2):
                        shift(t + 1, 1 - s, half)
                if after is None or after >= 2:
                    queries(t + 2)
                divide(t)

            dve.memset(v_parts[:, :, 0, :, DK:DK + 1], 1.0)
            dve.memset(v_parts[:, :, 1, :, DK:DK + 1], 0.0).then_inc(setup_link, 1)
            dve.wait_ge(rstd_sq, 1)
            dve.reciprocal(rstd[:, :], rstd[:, :]).then_inc(setup_link, 1)
            dve.tensor_scalar(tau4[:, :], keep["tau"][:, :], 1.0 / DK ** 0.5, None, ALU.mult).then_inc(setup_link, 1)
            dve.wait_ge(setup_link, 3)
            dve.tensor_tensor(rstd_tau[:, :], rstd[:, :], tau4[:, :], ALU.mult).then_inc(setup_link, 1)
            dve.wait_ge(w_loaded, 16 * len(loads))
            for c in range(HC):
                ins = dve.tensor_scalar(bq_tau[:, c, :], tau4[:, :], bq[:, c:c + 1], keep["quarter"][:, 0:1],
                                        ALU.mult, ALU.add)
            ins.then_inc(setup_link, 1)
            dve.wait_ge(setup_link, 5)
            norm(0)
            norm(1)
            queries(0)
            for half in range(2):
                shift(0, 0, half)
            norm(2)
            queries(1)
            slots(dve, slot)
            finish(TILES - 2)
            read_rows(TILES - 1)
            finish(TILES - 1)


TOKENS = TILES * P
EXPERTS = 8
CAPACITY = TOKENS // EXPERTS
SLOTS = CAPACITY // P
HID = 1024
HCH = HID // P
ROW = D + EXPERTS


def layer_norm_scale(act, dve, keep, rstd, sq, done):
    if act is not None:
        act.activation(rstd[:, :], keep["MV"][:, :, 1], ACT.Sqrt, bias=keep["eps"][:, 0:1]).then_inc(sq, 1)
    if dve is not None:
        dve.wait_ge(sq, 1)
        dve.reciprocal(rstd[:, :], rstd[:, :]).then_inc(done, 1)
        dve.wait_ge(done, 1)


def shared_ffn(nc, keep, w, probs, row_dram, sum_dram):
    tag = "sh"
    with ExitStack() as ctx:
        def sb(name, shape, dt=F32):
            return ctx.enter_context(nc.sbuf_tensor(f"{tag}_{name}", shape, dt))

        def sem(name):
            return keep["semaphore"](f"{tag}_{name}")

        X, MV, ident = keep["X"], keep["MV"], keep["ident"]
        w1 = sb("w1", [P, KC, HID])
        w2 = sb("w2", [P, HCH, D])
        gate = sb("gate", [P, KC, EXPERTS])
        b1 = sb("b1", [P, HCH])
        b2 = sb("b2", [P, D])
        rstd = sb("rstd", [P, TILES])
        row = sb("row", [P, G, ROW])
        xnT = sb("xnT", [P, KC, GT])
        hT = sb("hT", [P, HCH, GT])
        tmp = sb("tmp", [P, G, D])
        new = sb("new", [P, G, D])
        lg = sb("lg", [P, G, EXPERTS])
        lmx = sb("lmx", [P, G])
        lsum = sb("lsum", [P, G])
        banks = [ctx.enter_context(nc.psum_tensor(f"{tag}_ps{b}", [P, 512], F32)) for b in range(5)]
        ring = Ring(f"{tag}_ring", sem, banks, ["xt0", "xt1", "lg"] + [f"up{c}" for c in range(HCH)]
                    + [f"y{u}" for u in range(G)])
        w_loaded = sem("w_loaded")
        rstd_sq = sem("rstd_sq")
        rstd_done = sem("rstd_done")
        xn_ready = sem("xn_ready")
        lg_shifted = sem("lg_shifted")
        lg_exp = sem("lg_exp")
        row_ready = sem("row_ready")
        row_stored = sem("row_stored")
        sum_ready = sem("sum_ready")
        sum_stored = sem("sum_stored")
        dve_link = sem("dve_link")
        loads = [(gate[:, :, :], w["gate"].rearrange("(k p) n -> p k n", p=P)),
                 (w1[:, :, :], w["Ws1"].rearrange("(k p) n -> p k n", p=P)),
                 (w2[:, :, :], w["Ws2"].rearrange("(k p) n -> p k n", p=P)),
                 (b1[:, :], w["bs1"]), (b2[:, :], w["bs2"])]
        row_v = row_dram.rearrange("(t p) n -> p t n", p=P)
        sum_v = sum_dram.rearrange("(t p) n -> p t n", p=P)
        block = ctx.enter_context(nc.Block())

        @block.sync
        def _(sp):
            for dst, src in loads:
                sp.dma_start(dst, src).then_inc(w_loaded, 16)
            with sp.Fori(0, GROUPS) as g:
                sp.wait_ge(row_ready, g + 1)
                sp.dma_start(row_v[:, bass.ds(g * G, G), :], row[:, :, :]).then_inc(row_stored, 16)
                sp.wait_ge(sum_ready, g + 1)
                sp.dma_start(sum_v[:, bass.ds(g * G, G), :], new[:, :, :]).then_inc(sum_stored, 16)
            sp.wait_ge(row_stored, 16 * (GROUPS + 1))
            sp.wait_ge(sum_stored, 16 * (GROUPS + 1))

        @block.scalar
        def _(act):
            layer_norm_scale(act, None, keep, rstd, rstd_sq, rstd_done)
            with act.Fori(0, GROUPS) as g:
                for i in range(2):
                    ring.wait_full(act, g, f"xt{i}")
                    ring.take(act.activation(xnT[:, :, i * 256:(i + 1) * 256],
                                             ring.bank(f"xt{i}")[:, :].rearrange("p (k n) -> p k n", k=KC),
                                             ACT.Copy), f"xt{i}")
                act.wait_ge(lg_shifted, g + 1)
                act.activation(lg[:, :, :], lg[:, :, :], ACT.Exp).then_inc(lg_exp, 1)
                for c in range(HCH):
                    ring.wait_full(act, g, f"up{c}")
                    ring.take(act.activation(hT[:, c, :], ring.bank(f"up{c}")[:, :], ACT.Gelu_apprx_tanh,
                                             bias=b1[:, c:c + 1]), f"up{c}")

        @block.tensor
        def _(pe):
            ring.start_empty(pe)
            pe.wait_ge(w_loaded, 16 * len(loads))
            with pe.Fori(0, GROUPS) as g:
                for i in range(2):
                    ring.claim(pe, g, f"xt{i}")
                    for u in (2 * i, 2 * i + 1):
                        pe.wait_ge(xn_ready, g * G + u + 1)
                        for k in range(KC):
                            at = k * 256 + (u % 2) * P
                            ins = pe.transpose(ring.bank(f"xt{i}")[:, at:at + P], row[:, u, k * P:(k + 1) * P],
                                               ident[:, :])
                    ring.filled(ins)
                for i in range(2):
                    ring.wait_taken(pe, g, f"xt{i}")
                ring.claim(pe, g, "lg")
                for u in range(G):
                    for k in range(KC):
                        ins = pe.matmul(ring.bank("lg")[:, u * EXPERTS:(u + 1) * EXPERTS],
                                        xnT[:, k, u * P:(u + 1) * P], gate[:, k, :], start=(k == 0),
                                        stop=(k == KC - 1))
                ring.filled(ins)
                for c in range(HCH):
                    ring.claim(pe, g, f"up{c}")
                    for k in range(KC):
                        ins = pe.matmul(ring.bank(f"up{c}")[:, :], w1[:, k, c * P:(c + 1) * P], xnT[:, k, :],
                                        start=(k == 0), stop=(k == KC - 1))
                    ring.filled(ins)
                for u in range(G):
                    ring.claim(pe, g, f"y{u}")
                    for c in range(HCH):
                        if u == 0:
                            ring.wait_taken(pe, g, f"up{c}")
                        ins = pe.matmul(ring.bank(f"y{u}")[:, 0:D], hT[:, c, u * P:(u + 1) * P], w2[:, c, :],
                                        start=(c == 0), stop=(c == HCH - 1))
                    ring.filled(ins)

        @block.vector
        def _(dve):
            layer_norm_scale(None, dve, keep, rstd, rstd_sq, rstd_done)
            dve.sem_inc(row_stored, 16)
            dve.sem_inc(sum_stored, 16)
            with dve.Fori(0, GROUPS) as g:
                link = Tally(dve_link, g, 3 + G)
                dve.wait_ge(row_stored, g * 16 + 16)
                for u in range(G):
                    t = g * G + u
                    dve.tensor_scalar(row[:, u:u + 1, 0:D], X[:, bass.ds(t, 1), :], MV[:, bass.ds(t, 1), 0],
                                      rstd[:, bass.ds(t, 1)], ALU.subtract, ALU.mult).then_inc(xn_ready, 1)
                ring.wait_full(dve, g, "lg")
                lv = ring.bank("lg")[:, 0:G * EXPERTS].rearrange("p (u e) -> p u e", u=G)
                link.inc(dve.tensor_reduce(lmx[:, :], lv, AX_X, ALU.max))
                link.wait(dve)
                ring.take(dve.tensor_tensor(lg[:, :, :], lv, lmx[:, :].rearrange(
                    "p (u a) -> p u a", a=1).broadcast_to([P, G, EXPERTS]), ALU.subtract), "lg")
                ring.wait_taken(dve, g, "lg")
                dve.sem_inc(lg_shifted, 1)
                dve.wait_ge(lg_exp, g + 1)
                link.inc(dve.tensor_reduce(lsum[:, :], lg[:, :, :], AX_X, ALU.add))
                link.wait(dve)
                link.inc(dve.reciprocal(lsum[:, :], lsum[:, :]))
                link.wait(dve)
                lb = lsum[:, :].rearrange("p (u a) -> p u a", a=1).broadcast_to([P, G, EXPERTS])
                dve.tensor_tensor(probs[:, bass.ds(g * G, G), :], lg[:, :, :], lb, ALU.mult)
                dve.tensor_tensor(row[:, :, D:ROW], lg[:, :, :], lb, ALU.mult).then_inc(row_ready, 1)
                dve.wait_ge(sum_stored, g * 16 + 16)
                for u in range(G):
                    t = g * G + u
                    ring.wait_full(dve, g, f"y{u}")
                    ring.take(dve.tensor_tensor(tmp[:, u, :], ring.bank(f"y{u}")[:, 0:D], b2[:, :], ALU.add), f"y{u}")
                    ring.wait_taken(dve, g, f"y{u}")
                    link.inc(dve.tensor_tensor(new[:, u:u + 1, :], X[:, bass.ds(t, 1), :],
                                               tmp[:, u:u + 1, :], ALU.add))
                link.wait(dve)
                dve.sem_inc(sum_ready, 1)
                link.close()


def choose_tokens(nc, keep, probs, idx):
    tag = "ch"
    BITS = 30
    ET = EXPERTS * TILES
    with ExitStack() as ctx:
        def sb(name, shape, dt=F32):
            return ctx.enter_context(nc.sbuf_tensor(f"{tag}_{name}", shape, dt))

        def sem(name):
            return keep["semaphore"](f"{tag}_{name}")

        ones = sb("ones", [P, P])
        before = sb("before", [P, P])
        iota_i = sb("iota_i", [P, P], I32)
        iota = sb("iota", [P, P])
        part_i = sb("part_i", [P, 1], I32)
        part = sb("part", [P, 1])
        tile_i = sb("tile_i", [P, ET], I32)
        tile_f = sb("tile_f", [P, ET])
        thr = sb("thr", [P, EXPERTS], I32)
        bit = sb("bit", [P, EXPERTS], I32)
        cand = sb("cand", [P, EXPERTS], I32)
        hit = sb("hit", [P, EXPERTS], I32)
        pe_t = sb("pe_t", [P, EXPERTS, TILES])
        flag = sb("flag", [P, EXPERTS, TILES])
        over = sb("over", [P, EXPERTS, TILES])
        count = sb("count", [P, EXPERTS])
        need = sb("need", [P, EXPERTS])
        carry = sb("carry", [P, ET])
        tot = sb("tot", [P, ET])
        inc_s = sb("inc_s", [P, ET])
        pos = sb("pos", [P, ET])
        pos_i = sb("pos_i", [P, ET], I32)
        hi_i = sb("hi_i", [P, ET], I32)
        hi = sb("hi", [P, ET])
        lo = sb("lo", [P, ET])
        chosen = sb("chosen", [P, ET])
        oh = sb("oh", [P, ET, SLOTS])
        rhs = sb("rhs", [P, ET, 2 * SLOTS], BF16)
        lohot = sb("lohot", [P, 2, TILES, P], BF16)
        half = sb("half", [P, EXPERTS, SLOTS])
        ps_c = ctx.enter_context(nc.psum_tensor(f"{tag}_ps_c", [P, EXPERTS], F32))
        ps_a = ctx.enter_context(nc.psum_tensor(f"{tag}_ps_a", [P, ET], F32))
        ps_b = ctx.enter_context(nc.psum_tensor(f"{tag}_ps_b", [P, ET], F32))
        ps_i = ctx.enter_context(nc.psum_tensor(f"{tag}_ps_i", [P, EXPERTS, 2 * SLOTS], F32))
        consts = sem("consts")
        pool_link = sem("pool_link")
        bit_link = sem("bit_link")
        part_ready = sem("part_ready")
        counted = sem("counted")
        flags_ready = sem("flags_ready")
        summed = sem("summed")
        dl = sem("dl")
        lohot_ready = sem("lohot_ready")
        placed = sem("placed")
        block = ctx.enter_context(nc.Block())

        @block.gpsimd
        def _(pool):
            pool.memset(ones[:, :], 1.0).then_inc(pool_link, 1)
            pool.memset(carry[:, :], 1.0).then_inc(pool_link, 1)
            pool.wait_ge(pool_link, 2)
            pool.affine_select(out=before[:, :], in_=ones[:, :], compare_op=ALU.is_gt, fill=0.0, base=0,
                               pattern=[[1, P]], channel_multiplier=-1).then_inc(consts, 1)
            pool.memset(carry[:, :].rearrange("p (e t) -> p e t", e=EXPERTS)[:, :, 0:1], 0.0).then_inc(consts, 1)
            pool.iota(iota_i[:, :], [[1, P]], base=0, channel_multiplier=0).then_inc(pool_link, 1)
            pool.iota(part_i[:, :], [[0, 1]], base=0, channel_multiplier=1).then_inc(pool_link, 1)
            pool.iota(tile_i[:, :], [[0, EXPERTS], [1, TILES]], base=0, channel_multiplier=0).then_inc(pool_link, 1)
            pool.wait_ge(pool_link, 5)
            pool.tensor_copy(iota[:, :], iota_i[:, :]).then_inc(consts, 1)
            pool.tensor_copy(part[:, :], part_i[:, :]).then_inc(consts, 1)
            pool.tensor_copy(tile_f[:, :], tile_i[:, :]).then_inc(consts, 1)

        @block.tensor
        def _(pe):
            pe.wait_ge(consts, 5)
            with pe.Fori(0, BITS + 1) as b:
                pe.wait_ge(part_ready, b + 1)
                pe.matmul(ps_c[:, :], ones[:, :], count[:, :], start=True, stop=True).then_inc(counted, 1)
            for n in range(2):
                pe.wait_ge(flags_ready, n + 1)
                src = (over if n == 0 else chosen)
                src = over[:, :, :].rearrange("p e t -> p (e t)") if n == 0 else chosen[:, :]
                pe.matmul(ps_a[:, :], before[:, :], src, start=True, stop=True)
                pe.matmul(ps_b[:, :], ones[:, :], src, start=True, stop=True).then_inc(summed, 1)
            with pe.Fori(0, EXPERTS // 2) as i:
                for s in range(2):
                    e = i * 2 + s
                    pe.wait_ge(lohot_ready, e + 1)
                    for t in range(TILES):
                        ins = pe.matmul(ps_i[:, bass.ds(e, 1), :], lohot[:, s, t, :],
                                        rhs[:, bass.ds(e * TILES + t, 1), :], start=(t == 0), stop=(t == TILES - 1))
                    ins.then_inc(placed, 1)

        @block.vector
        def _(dve):
            dve.memset(thr[:, :], 0)
            dve.memset(bit[:, :], 1 << (BITS - 1)).then_inc(dl, 1)
            dve.tensor_copy(pe_t[:, :, :], probs[:, :, :].rearrange("p t e -> p e t")).then_inc(dl, 1)
            dve.wait_ge(dl, 2)

            def wide(v):
                return v.rearrange("p (e a) -> p e a", a=1).broadcast_to([P, EXPERTS, TILES])

            with dve.Fori(0, BITS) as b:
                link = Tally(bit_link, b, 6)
                link.inc(dve.tensor_tensor(cand[:, :], thr[:, :], bit[:, :], ALU.bitwise_or))
                link.wait(dve)
                link.inc(dve.tensor_tensor(flag[:, :, :], pe_t[:, :, :], wide(cand[:, :].bitcast(F32)), ALU.is_ge))
                link.wait(dve)
                dve.tensor_reduce(count[:, :], flag[:, :, :], AX_X, ALU.add).then_inc(part_ready, 1)
                dve.wait_ge(counted, b + 1)
                link.inc(dve.tensor_scalar(hit[:, :], ps_c[:, :], float(CAPACITY), -1.0, ALU.is_ge, ALU.mult))
                link.wait(dve)
                link.inc(dve.tensor_tensor(hit[:, :], hit[:, :], bit[:, :], ALU.bitwise_and))
                link.wait(dve)
                link.inc(dve.tensor_tensor(thr[:, :], thr[:, :], hit[:, :], ALU.bitwise_or))
                link.inc(dve.tensor_scalar(bit[:, :], bit[:, :], 1, None, ALU.logical_shift_right))
                link.wait(dve)
                link.close()
            steps = [2]

            def step(ins):
                ins.then_inc(dl, 1)
                steps[0] += 1
                dve.wait_ge(dl, steps[0])

            T = wide(thr[:, :].bitcast(F32))
            step(dve.tensor_tensor(flag[:, :, :], pe_t[:, :, :], T, ALU.is_gt))
            dve.tensor_tensor(over[:, :, :], pe_t[:, :, :], T, ALU.is_equal).then_inc(flags_ready, 1)
            dve.tensor_reduce(count[:, :], flag[:, :, :], AX_X, ALU.add).then_inc(part_ready, 1)
            dve.wait_ge(counted, BITS + 1)
            step(dve.tensor_scalar(need[:, :], ps_c[:, :], -1.0, float(CAPACITY), ALU.mult, ALU.add))

            def rank(n):
                dve.wait_ge(summed, n)
                step(dve.tensor_copy(tot[:, :], ps_b[:, :]))
                step(dve.tensor_tensor_scan(inc_s[:, :], carry[:, :], tot[:, :], 0.0, ALU.mult, ALU.add))
                step(dve.tensor_tensor(inc_s[:, :], inc_s[:, :], tot[:, :], ALU.subtract))
                step(dve.tensor_tensor(pos[:, :], ps_a[:, :], inc_s[:, :], ALU.add))

            dve.wait_ge(consts, 5)
            rank(1)
            step(dve.tensor_tensor(pos[:, :].rearrange("p (e t) -> p e t", e=EXPERTS),
                                   pos[:, :].rearrange("p (e t) -> p e t", e=EXPERTS), wide(need[:, :]), ALU.is_lt))
            step(dve.tensor_tensor(pos[:, :], pos[:, :], over[:, :, :].rearrange("p e t -> p (e t)"), ALU.mult))
            step(dve.tensor_tensor(chosen[:, :], pos[:, :], flag[:, :, :].rearrange("p e t -> p (e t)"), ALU.add))
            dve.sem_inc(flags_ready, 1)
            rank(2)
            step(dve.tensor_copy(pos_i[:, :], pos[:, :]))
            step(dve.tensor_scalar(hi_i[:, :], pos_i[:, :], 7, None, ALU.logical_shift_right))
            step(dve.tensor_copy(hi[:, :], hi_i[:, :]))
            step(dve.tensor_scalar(pos_i[:, :], pos_i[:, :], P - 1, None, ALU.bitwise_and))
            step(dve.tensor_copy(lo[:, :], pos_i[:, :]))
            four = [P, ET, SLOTS]
            step(dve.tensor_tensor(oh[:, :, :], hi[:, :].rearrange("p (n a) -> p n a", a=1).broadcast_to(four),
                                   iota[:, 0:SLOTS].rearrange("p (a c) -> p a c", a=1).broadcast_to(four),
                                   ALU.is_equal))
            step(dve.tensor_tensor(oh[:, :, :], oh[:, :, :],
                                   chosen[:, :].rearrange("p (n a) -> p n a", a=1).broadcast_to(four), ALU.mult))
            step(dve.tensor_scalar(rhs[:, :, 0:SLOTS], oh[:, :, :], part[:, 0:1], None, ALU.mult))
            step(dve.tensor_tensor(rhs[:, :, SLOTS:2 * SLOTS], oh[:, :, :],
                                   tile_f[:, :].rearrange("p (n a) -> p n a", a=1).broadcast_to(four), ALU.mult))
            dve.sem_inc(placed, 2)
            with dve.Fori(0, EXPERTS // 2) as i:
                for s in range(2):
                    e = i * 2 + s
                    dve.wait_ge(placed, e + 1)
                    dve.tensor_tensor(lohot[:, s, :, :],
                                      iota[:, :].rearrange("p (a n) -> p a n", a=1).broadcast_to([P, TILES, P]),
                                      lo[:, bass.ds(e * TILES, TILES)].rearrange("p (t a) -> p t a", a=1).broadcast_to(
                                          [P, TILES, P]), ALU.is_equal).then_inc(lohot_ready, 1)
            dve.wait_ge(placed, EXPERTS + 2)
            step(dve.tensor_copy(half[:, :, :], ps_i[:, :, 0:SLOTS]))
            step(dve.scalar_tensor_tensor(idx[:, :, :], ps_i[:, :, SLOTS:2 * SLOTS], float(P), half[:, :, :],
                                          ALU.mult, ALU.add))


def routed_ffn(nc, keep, w, idx, row_dram, sum_dram):
    tag = "ro"
    with ExitStack() as ctx:
        def sb(name, shape, dt=F32):
            return ctx.enter_context(nc.sbuf_tensor(f"{tag}_{name}", shape, dt))

        def sem(name):
            return keep["semaphore"](f"{tag}_{name}")

        X, MV, ident = keep["X"], keep["MV"], keep["ident"]
        w1 = sb("w1", [P, 2, KC, HID])
        w2 = sb("w2", [P, 2, HCH, D])
        b1 = sb("b1", [P, 2, HCH])
        b2 = sb("b2", [P, 2, D])
        row = sb("row", [P, 2, SLOTS, ROW])
        score = sb("score", [P, 2, SLOTS])
        xnT = sb("xnT", [P, KC, CAPACITY])
        hT = sb("hT", [P, HCH, CAPACITY])
        tmp = sb("tmp", [P, SLOTS, D])
        y = sb("y", [P, 2, SLOTS, D])
        tok = sb("tok", [P, 2, SLOTS], U32)
        bst = sb("bst", [P, TILES, 6])
        banks = [ctx.enter_context(nc.psum_tensor(f"{tag}_ps{b}", [P, 512], F32)) for b in range(7)]
        ring = Ring(f"{tag}_ring", sem, banks, ["xt0", "xt1"] + [f"up{c}" for c in range(HCH)]
                    + [f"y{u}" for u in range(SLOTS)])
        w_loaded = [sem(f"w_loaded{s}") for s in range(2)]
        gathered = [sem(f"gathered{s}") for s in range(2)]
        scattered = sem("scattered")
        tok_ready = sem("tok_ready")
        scores_out = sem("scores_out")
        pool_passed = sem("pool_passed")
        y_stored = sem("y_stored")
        y_ready = sem("y_ready")
        x_loaded = sem("x_loaded")
        bn_link = sem("bn_link")
        sum_v = sum_dram.rearrange("(t p) n -> p t n", p=P)
        w1_v = w["W1"].rearrange("e (k p) n -> p e k n", p=P)
        w2_v = w["W2"].rearrange("e (k p) n -> p e k n", p=P)
        block = ctx.enter_context(nc.Block())

        @block.sync
        def _(sp):
            def load(s, e):
                one = bass.ds(e, 1)
                sp.dma_start(w1[:, s:s + 1, :, :], w1_v[:, one, :, :]).then_inc(w_loaded[s], 16)
                sp.dma_start(w2[:, s:s + 1, :, :], w2_v[:, one, :, :]).then_inc(w_loaded[s], 16)
                sp.dma_start(b1[:, s:s + 1, :], w["b1"][:, one, :]).then_inc(w_loaded[s], 16)
                sp.dma_start(b2[:, s:s + 1, :], w["b2"][:, one, :]).then_inc(w_loaded[s], 16)

            load(0, 0)
            load(1, 1)
            with sp.Fori(1, EXPERTS // 2) as i:
                for s in range(2):
                    sp.wait_ge(y_ready, (i - 1) * 2 + s + 2)
                    load(s, i * 2 + s)
            sp.wait_ge(scattered, 16 * SLOTS * EXPERTS)
            sp.dma_start(X[:, :, :], sum_v).then_inc(x_loaded, 16)
            sp.wait_ge(x_loaded, 16)

        @block.gpsimd
        def _(pool):
            def gather(s, e):
                pool.tensor_copy(tok[:, s:s + 1, :], idx[:, bass.ds(e, 1), :]).then_inc(tok_ready, 1)
                await_apart(pool, tok_ready, e + 1, pool_passed)
                for c in range(SLOTS):
                    pool.indirect_dma_start(out=row[:, s, c, :], out_offset=None, in_=row_dram[:, :],
                                            in_offset=bass.IndirectOffsetOnAxis(ap=tok[:, s, c:c + 1], axis=0),
                                            ).then_inc(gathered[s], 16)

            gather(0, 0)
            def turn(i, last):
                for s in range(2):
                    e = i * 2 + s
                    if not (last and s == 1):
                        gather(1 - s, e + 1)
                    await_apart(pool, y_ready, e + 2, pool_passed)
                    for c in range(SLOTS):
                        pool.indirect_dma_start(out=sum_dram[:, :], in_=y[:, s, c, :], in_offset=None,
                                                out_offset=bass.IndirectOffsetOnAxis(ap=tok[:, s, c:c + 1], axis=0),
                                                compute_op=ALU.add).then_inc(scattered, 16)
                    await_apart(pool, scattered, (e + 1) * 16 * SLOTS, y_stored)

            with pool.Fori(0, EXPERTS // 2 - 1) as i:
                turn(i, False)
            turn(EXPERTS // 2 - 1, True)

        @block.scalar
        def _(act):
            with act.Fori(0, EXPERTS // 2) as i:
                for s in range(2):
                    e = i * 2 + s
                    for n in range(2):
                        ring.wait_full(act, e, f"xt{n}")
                        ring.take(act.activation(xnT[:, :, n * 256:(n + 1) * 256],
                                                 ring.bank(f"xt{n}")[:, :].rearrange("p (k n) -> p k n", k=KC),
                                                 ACT.Copy), f"xt{n}")
                    if s == 0:
                        act.wait_ge(w_loaded[0], i * 64 + 64)
                    else:
                        act.wait_ge(w_loaded[1], i * 64 + 64)
                    for c in range(HCH):
                        ring.wait_full(act, e, f"up{c}")
                        ring.take(act.activation(hT[:, c, :], ring.bank(f"up{c}")[:, :], ACT.Gelu_apprx_tanh,
                                                 bias=b1[:, s, c:c + 1]), f"up{c}")

        @block.tensor
        def _(pe):
            ring.start_empty(pe)
            with pe.Fori(0, EXPERTS // 2) as i:
                for s in range(2):
                    e = i * 2 + s
                    pe.wait_ge(gathered[s], (i + 1) * 16 * SLOTS)
                    for n in range(2):
                        ring.claim(pe, e, f"xt{n}")
                        for u in (2 * n, 2 * n + 1):
                            for k in range(KC):
                                at = k * 256 + (u % 2) * P
                                ins = pe.transpose(ring.bank(f"xt{n}")[:, at:at + P],
                                                   row[:, s, u, k * P:(k + 1) * P], ident[:, :])
                        ring.filled(ins)
                    for n in range(2):
                        ring.wait_taken(pe, e, f"xt{n}")
                    pe.wait_ge(w_loaded[s], i * 64 + 64)
                    for c in range(HCH):
                        ring.claim(pe, e, f"up{c}")
                        for k in range(KC):
                            ins = pe.matmul(ring.bank(f"up{c}")[:, :], w1[:, s, k, c * P:(c + 1) * P], xnT[:, k, :],
                                            start=(k == 0), stop=(k == KC - 1))
                        ring.filled(ins)
                    for u in range(SLOTS):
                        ring.claim(pe, e, f"y{u}")
                        for c in range(HCH):
                            if u == 0:
                                ring.wait_taken(pe, e, f"up{c}")
                            ins = pe.matmul(ring.bank(f"y{u}")[:, 0:D], hT[:, c, u * P:(u + 1) * P], w2[:, s, c, :],
                                            start=(c == 0), stop=(c == HCH - 1))
                        ring.filled(ins)

        @block.vector
        def _(dve):
            dve.sem_inc(scores_out, 1)
            dve.sem_inc(y_ready, 1)
            dve.sem_inc(y_stored, 2)
            with dve.Fori(0, EXPERTS // 2) as i:
                for s in range(2):
                    e = i * 2 + s
                    dve.wait_ge(gathered[s], (i + 1) * 16 * SLOTS)
                    dve.tensor_scalar(score[:, s, :].rearrange("p (c a) -> p c a", a=1),
                                      row[:, s, :, bass.ds(D + e, 1)], 1.0, None, ALU.mult).then_inc(scores_out, 1)
                    dve.wait_ge(w_loaded[s], i * 64 + 64)
                    dve.wait_ge(y_ready, e + 1)
                    dve.wait_ge(y_stored, e + 1)
                    for u in range(SLOTS):
                        ring.wait_full(dve, e, f"y{u}")
                        ring.take(dve.tensor_tensor(tmp[:, u, :], ring.bank(f"y{u}")[:, 0:D], b2[:, s, :], ALU.add),
                                  f"y{u}")
                    dve.wait_ge(scores_out, e + 2)
                    for u in range(SLOTS):
                        ring.wait_taken(dve, e, f"y{u}")
                        ins = dve.tensor_scalar(y[:, s, u, :], tmp[:, u, :], score[:, s, u:u + 1], None, ALU.mult)
                    ins.then_inc(y_ready, 1)
            dve.wait_ge(x_loaded, 16)
            for t in range(TILES):
                ins = dve.bn_stats(bst[:, t, :], X[:, t, :])
            ins.then_inc(bn_link, 1)
            dve.wait_ge(bn_link, 1)
            for t in range(TILES):
                dve.bn_aggr(MV[:, t, :], bst[:, t, :])


INNER = 1024
ROUND = 12582912.0


def bit_ffn(nc, keep, w):
    tag = "bf"
    S2 = 2
    with ExitStack() as ctx:
        def sb(name, shape, dt=F32):
            return ctx.enter_context(nc.sbuf_tensor(f"{tag}_{name}", shape, dt))

        def sem(name):
            return keep["semaphore"](f"{tag}_{name}")

        X, MV = keep["X"], keep["MV"]
        names = ("gate", "up", "down")
        raw = {n: sb("raw_" + n, [P, KC * INNER]) for n in names}
        wb = {n: sb("wb_" + n, [P, KC * INNER], BF16) for n in names}
        wg = wb["gate"][:, :].rearrange("p (k n) -> p k n", k=KC)
        wu = wb["up"][:, :].rearrange("p (k n) -> p k n", k=KC)
        wd = wb["down"][:, :].rearrange("p (k n) -> p k n", k=INNER // P)
        ones = sb("ones", [P, P])
        identb = sb("identb", [P, P], BF16)
        asum = sb("asum", [P, 3])
        wmean = sb("wmean", [P, 3])
        wscale = sb("wscale", [P, 3])
        wq127 = sb("wq127", [P, 3])
        rstd = sb("rstd", [P, TILES])
        xn = sb("xn", [P, S2, D])
        xq = sb("xq", [P, S2, D], BF16)
        xqT = sb("xqT", [P, S2, KC, P], BF16)
        amx = sb("amx", [P, S2, 2])
        asc = sb("asc", [P, S2, 2])
        dq = sb("dq", [P, S2, 3])
        gt = sb("gt", [P, S2, INNER])
        h = sb("h", [P, S2, INNER])
        hq = sb("hq", [P, S2, INNER], BF16)
        hqT = sb("hqT", [P, S2, INNER // P, P], BF16)
        new = sb("new", [P, S2, D])
        bst = sb("bst", [P, 6])
        mv = sb("mv", [P, 2])
        banks = [ctx.enter_context(nc.psum_tensor(f"{tag}_ps{b}", [P, 512], F32)) for b in range(7)]
        ps_w = ctx.enter_context(nc.psum_tensor(f"{tag}_ps_w", [P, 3], F32))
        ring = Ring(f"{tag}_ring", sem, banks, ["xt0", "xt1"] + [f"{a}{n}_{s}" for s in range(S2) for a in "gu"
                    for n in range(2)] + ["ht0", "ht1", "y0", "y1"])
        w_loaded = [sem("w_loaded_" + n) for n in names]
        consts = sem("consts")
        rstd_sq = sem("rstd_sq")
        sums_ready = sem("sums_ready")
        summed = sem("summed")
        setup = sem("setup")
        xq_ready = sem("xq_ready")
        dq_ready = sem("dq_ready")
        hq_ready = sem("hq_ready")
        dve_link = sem("dve_link")
        block = ctx.enter_context(nc.Block())

        @block.sync
        def _(sp):
            for n, src, k in (("gate", w["w_gate"], KC), ("up", w["w_up"], KC), ("down", w["w_down"], INNER // P)):
                sp.dma_start(raw[n][:, :].rearrange("p (k n) -> p k n", k=k),
                             src.rearrange("(k p) n -> p k n", p=P)).then_inc(w_loaded[names.index(n)], 16)

        @block.gpsimd
        def _(pool):
            pool.memset(ones[:, :], 1.0).then_inc(consts, 1)
            pool.tensor_copy(identb[:, :], keep["ident"][:, :]).then_inc(consts, 1)

        @block.scalar
        def _(act):
            layer_norm_scale(act, None, keep, rstd, rstd_sq, None)
            with act.Fori(0, TILES // S2) as i:
                for s in range(S2):
                    ring.wait_full(act, i, f"xt{s}")
                    ring.take(act.activation(xqT[:, s, :, :], ring.bank(f"xt{s}")[:, :].bitcast(BF16)[:, 0:D].rearrange(
                        "p (k n) -> p k n", k=KC), ACT.Copy), f"xt{s}")
                for s in range(S2):
                    act.wait_ge(dq_ready, i * S2 + s + 1)
                    for n in range(2):
                        ring.wait_full(act, i, f"g{n}_{s}")
                        ring.take(act.activation(gt[:, s, n * 512:(n + 1) * 512], ring.bank(f"g{n}_{s}")[:, :],
                                                 ACT.Silu, scale=dq[:, s, 0:1]), f"g{n}_{s}")
                for s in range(S2):
                    ring.wait_full(act, i, f"ht{s}")
                    ring.take(act.activation(hqT[:, s, :, :], ring.bank(f"ht{s}")[:, :].bitcast(BF16).rearrange(
                        "p (k n) -> p k n", n=P), ACT.Copy), f"ht{s}")

        @block.tensor
        def _(pe):
            ring.start_empty(pe)
            pe.wait_ge(consts, 2)
            pe.wait_ge(sums_ready, 3)
            pe.matmul(ps_w[:, :], ones[:, :], asum[:, :], start=True, stop=True).then_inc(summed, 1)
            pe.wait_ge(setup, 16)
            with pe.Fori(0, TILES // S2) as i:
                for s in range(S2):
                    ring.claim(pe, i, f"xt{s}")
                    pe.wait_ge(xq_ready, i * S2 + s + 1)
                    for k in range(KC):
                        ins = pe.transpose(ring.bank(f"xt{s}")[:, :].bitcast(BF16)[:, k * P:(k + 1) * P],
                                           xq[:, s, k * P:(k + 1) * P], identb[:, :])
                    ring.filled(ins)
                for s in range(S2):
                    ring.wait_taken(pe, i, f"xt{s}")
                    for a, wt in (("g", wg), ("u", wu)):
                        for n in range(2):
                            ring.claim(pe, i, f"{a}{n}_{s}")
                            for k in range(KC):
                                ins = pe.matmul(ring.bank(f"{a}{n}_{s}")[:, :], xqT[:, s, k, :],
                                                wt[:, k, n * 512:(n + 1) * 512], start=(k == 0), stop=(k == KC - 1))
                            ring.filled(ins)
                for s in range(S2):
                    ring.claim(pe, i, f"ht{s}")
                    pe.wait_ge(hq_ready, i * S2 + s + 1)
                    for k in range(INNER // P):
                        ins = pe.transpose(ring.bank(f"ht{s}")[:, :].bitcast(BF16)[:, k * P:(k + 1) * P],
                                           hq[:, s, k * P:(k + 1) * P], identb[:, :])
                    ring.filled(ins)
                for s in range(S2):
                    ring.claim(pe, i, f"y{s}")
                    ring.wait_taken(pe, i, f"ht{s}")
                    for k in range(INNER // P):
                        ins = pe.matmul(ring.bank(f"y{s}")[:, 0:D], hqT[:, s, k, :], wd[:, k, :], start=(k == 0),
                                        stop=(k == INNER // P - 1))
                    ring.filled(ins)

        @block.vector
        def _(dve):
            layer_norm_scale(None, dve, keep, rstd, rstd_sq, setup)
            done = [1]

            def step(ins):
                ins.then_inc(setup, 1)
                done[0] += 1
                dve.wait_ge(setup, done[0])

            for n in range(3):
                dve.wait_ge(w_loaded[n], 16)
                dve.tensor_reduce(asum[:, n:n + 1], raw[names[n]][:, :], AX_X, ALU.add,
                                  apply_absolute_value=True).then_inc(sums_ready, 1)
            dve.wait_ge(summed, 1)
            step(dve.tensor_scalar(wmean[:, :], ps_w[:, :], 1.0 / (D * INNER), 1e-5, ALU.mult, ALU.max))
            step(dve.reciprocal(wscale[:, :], wmean[:, :]))
            step(dve.tensor_scalar(wq127[:, :], wmean[:, :], 1.0 / 127.0, None, ALU.mult))
            for n in range(3):
                r = raw[names[n]]
                step(dve.tensor_scalar(r[:, :], r[:, :], wscale[:, n:n + 1], ROUND, ALU.mult, ALU.add))
                step(dve.tensor_scalar(r[:, :], r[:, :], ROUND, 1.0, ALU.subtract, ALU.min))
                step(dve.tensor_scalar(r[:, :], r[:, :], -1.0, None, ALU.max))
                step(dve.tensor_copy(wb[names[n]][:, :], r[:, :]))

            with dve.Fori(0, TILES // S2) as i:
                link = Tally(dve_link, i, S2 * 16)

                def quantise(src, dst, s, a):
                    one = slice(a, a + 1)
                    link.inc(dve.tensor_reduce(amx[:, s, one], src, AX_X, ALU.max, apply_absolute_value=True))
                    link.wait(dve)
                    link.inc(dve.tensor_scalar(amx[:, s, one], amx[:, s, one], 1e-5, None, ALU.max))
                    link.wait(dve)
                    link.inc(dve.reciprocal(asc[:, s, one], amx[:, s, one]))
                    link.wait(dve)
                    link.inc(dve.tensor_scalar(asc[:, s, one], asc[:, s, one], 127.0, None, ALU.mult))
                    link.wait(dve)
                    link.inc(dve.tensor_scalar(src, src, asc[:, s, one], -128.0, ALU.mult, ALU.max))
                    link.wait(dve)
                    link.inc(dve.tensor_scalar(src, src, 127.0, ROUND, ALU.min, ALU.add))
                    link.wait(dve)
                    return dve.tensor_scalar(dst, src, ROUND, None, ALU.subtract)

                for s in range(S2):
                    t = i * S2 + s
                    link.inc(dve.tensor_scalar(xn[:, s:s + 1, :], X[:, bass.ds(t, 1), :], MV[:, bass.ds(t, 1), 0],
                                               rstd[:, bass.ds(t, 1)], ALU.subtract, ALU.mult))
                    link.wait(dve)
                    quantise(xn[:, s, :], xq[:, s, :], s, 0).then_inc(xq_ready, 1)
                    dve.tensor_scalar(dq[:, s, 0:2], wq127[:, 0:2], amx[:, s, 0:1], None, ALU.mult).then_inc(
                        dq_ready, 1)
                for s in range(S2):
                    dve.wait_ge(dq_ready, i * S2 + s + 1)
                    for n in range(2):
                        ring.wait_taken(dve, i, f"g{n}_{s}")
                        ring.wait_full(dve, i, f"u{n}_{s}")
                        ring.take(dve.scalar_tensor_tensor(h[:, s, n * 512:(n + 1) * 512],
                                                           ring.bank(f"u{n}_{s}")[:, :], dq[:, s, 1:2],
                                                           gt[:, s, n * 512:(n + 1) * 512], ALU.mult, ALU.mult),
                                  f"u{n}_{s}")
                    for n in range(2):
                        ring.wait_taken(dve, i, f"u{n}_{s}")
                    quantise(h[:, s, :], hq[:, s, :], s, 1).then_inc(hq_ready, 1)
                    link.inc(dve.tensor_scalar(dq[:, s, 2:3], wq127[:, 2:3], amx[:, s, 1:2], None, ALU.mult))
                for s in range(S2):
                    t = i * S2 + s
                    ring.wait_full(dve, i, f"y{s}")
                    link.wait(dve)
                    ring.take(dve.scalar_tensor_tensor(new[:, s:s + 1, :], ring.bank(f"y{s}")[:, 0:D].rearrange(
                        "p (a n) -> p a n", a=1), dq[:, s, 2:3], X[:, bass.ds(t, 1), :], ALU.mult, ALU.add), f"y{s}")
                    ring.wait_taken(dve, i, f"y{s}")
                    finish_rows(dve, keep, link, t, new[:, s, :], bst, mv)
                link.close()


WINDOW = 16.0
DEV_POW = 128.0
MASKED = 1e9


def windowed_attention(nc, keep, w, ctxT, ctx_n):
    tag = "wa"
    with ExitStack() as ctx:
        def sb(name, shape, dt=F32):
            return ctx.enter_context(nc.sbuf_tensor(f"{tag}_{name}", shape, dt))

        def sem(name):
            return keep["semaphore"](f"{tag}_{name}")

        X, MV, ident = keep["X"], keep["MV"], keep["ident"]
        wa = sb("wa", [P, KC, D])
        wc = sb("wc", [P, 2 * KC, D])
        pt = sb("pt", [P, TILES])
        len_i = sb("len_i", [P, TILES], I32)
        first = sb("first", [P, TILES])
        last = sb("last", [P, TILES])
        neg_pt = sb("neg_pt", [P, TILES])
        iota_i = sb("iota_i", [P, P], I32)
        iota = sb("iota", [P, P])
        rstd = sb("rstd", [P, TILES])
        ctx_t = sb("ctx_t", [P, KC, GT])
        ctx_r = sb("ctx_r", [P, G, D])
        xn = sb("xn", [P, G, D])
        xnT = sb("xnT", [P, KC, GT])
        aT = sb("aT", [P, KC, GT])
        inside = sb("inside", [P, G, P])
        low = sb("low", [P, G, P])
        gauss = sb("gauss", [P, G, P])
        sc = sb("sc", [P, G, P])
        mx = sb("mx", [P, G])
        den = sb("den", [P, G])
        al = sb("al", [P, G, P])
        alT = sb("alT", [P, G, P])
        cxT = sb("cxT", [P, G, KC, P])
        th = sb("th", [P, G, D])
        new = sb("new", [P, D])
        bst = sb("bst", [P, 6])
        mv = sb("mv", [P, 2])
        banks = [ctx.enter_context(nc.psum_tensor(f"{tag}_ps{b}", [P, 512], F32)) for b in range(5)]
        ring = Ring(f"{tag}_ring", sem, banks, ["xt0", "xt1", "a0", "a1"]
                    + [f"{n}{u}" for n in ("sc", "al", "cx", "y") for u in range(G)])
        w_loaded = sem("w_loaded")
        ctx_loaded = sem("ctx_loaded")
        pool_link = sem("pool_link")
        consts = sem("consts")
        rstd_sq = sem("rstd_sq")
        setup = sem("setup")
        xn_ready = sem("xn_ready")
        gauss_sq = sem("gauss_sq")
        gauss_ready = sem("gauss_ready")
        mx_ready = sem("mx_ready")
        exp_ready = sem("exp_ready")
        al_ready = sem("al_ready")
        dve_link = sem("dve_link")
        loads = [(wa[:, :, :], w["W_a"].rearrange("(k p) n -> p k n", p=P)),
                 (wc[:, :, :], w["W_c"].rearrange("(k p) n -> p k n", p=P)),
                 (pt[:, :], w["pt"]), (len_i[:, :], w["len"])]
        ctxT_v = ctxT.rearrange("(k p) n -> p k n", p=P)
        ctx_v = ctx_n.rearrange("(t p) d -> p t d", p=P)
        block = ctx.enter_context(nc.Block())

        @block.sync
        def _(sp):
            for dst, src in loads:
                sp.dma_start(dst, src).then_inc(w_loaded, 16)
            sp.dma_start(ctx_t[:, :, :], ctxT_v[:, :, 0:GT]).then_inc(ctx_loaded, 16)
            sp.dma_start(ctx_r[:, :, :], ctx_v[:, 0:G, :]).then_inc(ctx_loaded, 16)
            with sp.Fori(1, GROUPS) as g:
                ring.wait_full(sp, g - 1, f"cx{G - 1}")
                sp.dma_start(ctx_t[:, :, :], ctxT_v[:, :, bass.ds(g * GT, GT)]).then_inc(ctx_loaded, 16)
                sp.dma_start(ctx_r[:, :, :], ctx_v[:, bass.ds(g * G, G), :]).then_inc(ctx_loaded, 16)

        @block.gpsimd
        def _(pool):
            pool.iota(iota_i[:, :], [[1, P]], base=0, channel_multiplier=0).then_inc(pool_link, 1)
            pool.wait_ge(pool_link, 1)
            pool.tensor_copy(iota[:, :], iota_i[:, :]).then_inc(consts, 1)

        @block.scalar
        def _(act):
            layer_norm_scale(act, None, keep, rstd, rstd_sq, None)
            act.wait_ge(consts, 1)
            act.wait_ge(setup, 6)
            with act.Fori(0, GROUPS) as g:
                for n in range(2):
                    ring.wait_full(act, g, f"xt{n}")
                    ring.take(act.activation(xnT[:, :, n * 256:(n + 1) * 256],
                                             ring.bank(f"xt{n}")[:, :].rearrange("p (k n) -> p k n", k=KC),
                                             ACT.Copy), f"xt{n}")
                for u in range(G):
                    act.activation(gauss[:, u, :], iota[:, :], ACT.Square,
                                   bias=neg_pt[:, bass.ds(g * G + u, 1)]).then_inc(gauss_sq, 1)
                act.wait_ge(gauss_sq, g * G + G)
                act.activation(gauss[:, :, :], gauss[:, :, :], ACT.Exp, scale=-1.0 / DEV_POW).then_inc(gauss_ready, 1)
                for k in range(KC):
                    ring.wait_full(act, g, f"a{k}")
                    ring.take(act.activation(aT[:, k, :], ring.bank(f"a{k}")[:, :], ACT.Copy), f"a{k}")
                for u in range(G):
                    act.wait_ge(mx_ready, g * G + u + 1)
                    act.activation(sc[:, u, :], sc[:, u, :], ACT.Exp, bias=mx[:, u:u + 1],
                                   accum_out=den[:, u:u + 1]).then_inc(exp_ready, 1)
                for u in range(G):
                    ring.wait_full(act, g, f"al{u}")
                    ring.take(act.activation(alT[:, u, :], ring.bank(f"al{u}")[:, 0:P], ACT.Copy), f"al{u}")
                for u in range(G):
                    ring.wait_full(act, g, f"cx{u}")
                    ring.take(act.activation(cxT[:, u, :, :], ring.bank(f"cx{u}")[:, 0:D].rearrange(
                        "p (k n) -> p k n", k=KC), ACT.Copy), f"cx{u}")
                for u in range(G):
                    ring.wait_full(act, g, f"y{u}")
                    ring.take(act.activation(th[:, u, :], ring.bank(f"y{u}")[:, 0:D], ACT.Tanh), f"y{u}")

        @block.tensor
        def _(pe):
            ring.start_empty(pe)
            pe.wait_ge(w_loaded, 16 * len(loads))
            with pe.Fori(0, GROUPS) as g:
                for n in range(2):
                    ring.claim(pe, g, f"xt{n}")
                    for u in (2 * n, 2 * n + 1):
                        pe.wait_ge(xn_ready, g * G + u + 1)
                        for k in range(KC):
                            at = k * 256 + (u % 2) * P
                            ins = pe.transpose(ring.bank(f"xt{n}")[:, at:at + P], xn[:, u, k * P:(k + 1) * P],
                                               ident[:, :])
                    ring.filled(ins)
                for n in range(2):
                    ring.wait_taken(pe, g, f"xt{n}")
                for c in range(KC):
                    ring.claim(pe, g, f"a{c}")
                    for k in range(KC):
                        ins = pe.matmul(ring.bank(f"a{c}")[:, :], wa[:, k, c * P:(c + 1) * P], xnT[:, k, :],
                                        start=(k == 0), stop=(k == KC - 1))
                    ring.filled(ins)
                pe.wait_ge(ctx_loaded, g * 32 + 32)
                for c in range(KC):
                    ring.wait_taken(pe, g, f"a{c}")
                for u in range(G):
                    ring.claim(pe, g, f"sc{u}")
                    for k in range(KC):
                        ins = pe.matmul(ring.bank(f"sc{u}")[:, 0:P], aT[:, k, u * P:(u + 1) * P],
                                        ctx_t[:, k, u * P:(u + 1) * P], start=(k == 0), stop=(k == KC - 1))
                    ring.filled(ins)
                for u in range(G):
                    ring.claim(pe, g, f"al{u}")
                    pe.wait_ge(al_ready, g * G + u + 1)
                    ring.filled(pe.transpose(ring.bank(f"al{u}")[:, 0:P], al[:, u, :], ident[:, :]))
                for u in range(G):
                    ring.claim(pe, g, f"cx{u}")
                    ring.wait_taken(pe, g, f"al{u}")
                    for c in range(KC):
                        ins = pe.matmul(ring.bank(f"cx{u}")[:, c * P:(c + 1) * P], ctx_r[:, u, c * P:(c + 1) * P],
                                        alT[:, u, :], start=True, stop=True)
                    ring.filled(ins)
                for u in range(G):
                    ring.claim(pe, g, f"y{u}")
                    ring.wait_taken(pe, g, f"cx{u}")
                    for k in range(2 * KC):
                        lhs = cxT[:, u, k, :] if k < KC else xnT[:, k - KC, u * P:(u + 1) * P]
                        ins = pe.matmul(ring.bank(f"y{u}")[:, 0:D], lhs, wc[:, k, :], start=(k == 0),
                                        stop=(k == 2 * KC - 1))
                    ring.filled(ins)

        @block.vector
        def _(dve):
            layer_norm_scale(None, dve, keep, rstd, rstd_sq, setup)
            dve.wait_ge(w_loaded, 16 * len(loads))
            dve.tensor_copy(last[:, :], len_i[:, :]).then_inc(setup, 1)
            dve.tensor_scalar(first[:, :], pt[:, :], WINDOW, 0.0, ALU.subtract, ALU.max).then_inc(setup, 1)
            dve.tensor_scalar(neg_pt[:, :], pt[:, :], -1.0, None, ALU.mult).then_inc(setup, 1)
            dve.wait_ge(setup, 4)
            dve.scalar_tensor_tensor(last[:, :], pt[:, :], WINDOW, last[:, :], ALU.add, ALU.min).then_inc(setup, 1)
            dve.memset(mv[:, :], 0.0).then_inc(setup, 1)
            dve.wait_ge(setup, 6)
            dve.wait_ge(consts, 1)
            with dve.Fori(0, GROUPS) as g:
                link = Tally(dve_link, g, 3 + 6 * G)
                for u in range(G):
                    t = g * G + u
                    dve.tensor_scalar(xn[:, u:u + 1, :], X[:, bass.ds(t, 1), :], MV[:, bass.ds(t, 1), 0],
                                      rstd[:, bass.ds(t, 1)], ALU.subtract, ALU.mult).then_inc(xn_ready, 1)
                for u in range(G):
                    t = g * G + u
                    ins = dve.tensor_scalar(low[:, u, :], iota[:, :], first[:, bass.ds(t, 1)], None, ALU.is_ge)
                link.inc(ins)
                link.wait(dve)
                for u in range(G):
                    t = g * G + u
                    ins = dve.scalar_tensor_tensor(inside[:, u, :], iota[:, :], last[:, bass.ds(t, 1)], low[:, u, :],
                                                   ALU.is_le, ALU.mult)
                link.inc(ins)
                link.wait(dve)
                link.inc(dve.tensor_scalar(low[:, :, :], inside[:, :, :], MASKED, MASKED, ALU.mult, ALU.subtract))
                link.wait(dve)
                for u in range(G):
                    ring.wait_full(dve, g, f"sc{u}")
                    ring.take(dve.tensor_tensor(sc[:, u, :], ring.bank(f"sc{u}")[:, 0:P], inside[:, u, :], ALU.mult),
                              f"sc{u}")
                    ring.wait_taken(dve, g, f"sc{u}")
                    link.inc(dve.tensor_tensor(sc[:, u, :], sc[:, u, :], low[:, u, :], ALU.add))
                    link.wait(dve)
                    link.inc(dve.tensor_reduce(mx[:, u:u + 1], sc[:, u, :], AX_X, ALU.max))
                    link.wait(dve)
                    dve.tensor_scalar(mx[:, u:u + 1], mx[:, u:u + 1], -1.0, None, ALU.mult).then_inc(mx_ready, 1)
                dve.wait_ge(gauss_ready, g + 1)
                for u in range(G):
                    dve.wait_ge(exp_ready, g * G + u + 1)
                    link.inc(dve.reciprocal(den[:, u:u + 1], den[:, u:u + 1]))
                    link.wait(dve)
                    dve.scalar_tensor_tensor(al[:, u, :], sc[:, u, :], den[:, u:u + 1], gauss[:, u, :],
                                             ALU.mult, ALU.mult).then_inc(al_ready, 1)
                for u in range(G):
                    t = g * G + u
                    ring.wait_taken(dve, g, f"y{u}")
                    link.inc(dve.tensor_tensor(new[:, :].rearrange("p (a n) -> p a n", a=1), th[:, u:u + 1, :],
                                               X[:, bass.ds(t, 1), :], ALU.add))
                    finish_rows(dve, keep, link, t, new, bst, mv)
                link.close()


BN_EPS = 1e-5
PK_HEADS = 8
PK_KEYS = 64
PK_TOP = 8
PK_DIM = 128
PK_EXPERTS = PK_KEYS * PK_KEYS
ECH = PK_EXPERTS // P
PICKS = PK_HEADS * PK_TOP
TB = 16
LO_SCALE = 4096.0


def product_key_experts(nc, keep, w):
    tag = "pk"
    with ExitStack() as ctx:
        def sb(name, shape, dt=F32):
            return ctx.enter_context(nc.sbuf_tensor(f"{tag}_{name}", shape, dt))

        def sem(name):
            return keep["semaphore"](f"{tag}_{name}")

        X, MV, ident = keep["X"], keep["MV"], keep["ident"]
        NT = sb("NT", [P, KC, TOKENS])
        wm = sb("wm", [P, KC, 2 * PK_HEADS * PK_KEYS])
        bn = sb("bn", [P, KC, 2])
        rstd = sb("rstd", [P, TILES])
        with ExitStack() as c2:
            def sb2(name, shape, dt=F32):
                return c2.enter_context(nc.sbuf_tensor(f"{tag}1_{name}", shape, dt))

            def sem2(name):
                return keep["semaphore"](f"{tag}_{name}")

            wq = sb2("wq", [P, 2 * PK_HEADS, D])
            keys = sb2("keys", [P, 2 * PK_HEADS, PK_KEYS])
            gamma = sb2("gamma", [P, KC])
            beta = sb2("beta", [P, KC])
            xn = sb2("xn", [P, G, D])
            nT = sb2("nT", [P, KC, GT])
            bst = sb2("bst", [P, KC, GROUPS, 6])
            mvb = sb2("mvb", [P, KC, 2])
            sd = sb2("sd", [P, KC])
            banks = [c2.enter_context(nc.psum_tensor(f"{tag}_p1_{b}", [P, 512], F32)) for b in range(2)]
            ps_w = [c2.enter_context(nc.psum_tensor(f"{tag}_pw_{b}", [P, 512], F32)) for b in range(4)]
            ring = Ring(f"{tag}_ring1", sem2, banks, ["xt0", "xt1"])
            w_loaded = sem2("w1_loaded")
            folded = sem2("folded")
            rstd_sq = sem2("rstd_sq")
            setup = sem2("setup1")
            xn_ready = sem2("xn1_ready")
            stats = sem2("stats")
            sd_sq = sem2("sd_sq")
            block = c2.enter_context(nc.Block())

            @block.sync
            def _(sp):
                sp.dma_start(wq[:, :, :], w["w_q"].rearrange("(c p) n -> p c n", p=P)).then_inc(w_loaded, 16)
                sp.dma_start(keys[:, :, :], w["keys"]).then_inc(w_loaded, 16)
                sp.dma_start(gamma[:, :], w["gamma"]).then_inc(w_loaded, 16)
                sp.dma_start(beta[:, :], w["beta"]).then_inc(w_loaded, 16)

            @block.scalar
            def _(act):
                layer_norm_scale(act, None, keep, rstd, rstd_sq, None)
                act.wait_ge(folded, 1)
                for k in range(KC):
                    for n in range(2):
                        act.activation(wm[:, k, n * 512:(n + 1) * 512], ps_w[2 * k + n][:, :], ACT.Copy)
                with act.Fori(0, GROUPS) as g:
                    for n in range(2):
                        ring.wait_full(act, g, f"xt{n}")
                        ring.take(act.activation(NT[:, :, bass.ds(g * GT + n * 256, 256)],
                                                 ring.bank(f"xt{n}")[:, :].rearrange("p (k n) -> p k n", k=KC),
                                                 ACT.Copy), f"xt{n}")
                act.wait_ge(stats, 2)
                act.activation(sd[:, :], mvb[:, :, 1], ACT.Sqrt, bias=keep["eps"][:, 0:1]).then_inc(sd_sq, 1)

            @block.tensor
            def _(pe):
                ring.start_empty(pe)
                pe.wait_ge(w_loaded, 64)
                for k in range(KC):
                    for c in range(2 * PK_HEADS):
                        at = (c % PK_HEADS) * PK_KEYS
                        ins = pe.matmul(ps_w[2 * k + c // PK_HEADS][:, at:at + PK_KEYS], wq[:, c, k * P:(k + 1) * P],
                                        keys[:, c, :], start=True, stop=True)
                ins.then_inc(folded, 1)
                with pe.Fori(0, GROUPS) as g:
                    for n in range(2):
                        ring.claim(pe, g, f"xt{n}")
                        for u in (2 * n, 2 * n + 1):
                            pe.wait_ge(xn_ready, g * G + u + 1)
                            for k in range(KC):
                                at = k * 256 + (u % 2) * P
                                ins = pe.transpose(ring.bank(f"xt{n}")[:, at:at + P], xn[:, u, k * P:(k + 1) * P],
                                                   ident[:, :])
                        ring.filled(ins)

            @block.vector
            def _(dve):
                layer_norm_scale(None, dve, keep, rstd, rstd_sq, setup)
                for g in range(GROUPS):
                    for u in range(G):
                        t = g * G + u
                        if g:
                            ring.wait_full(dve, g - 1, f"xt{u // 2}")
                        dve.tensor_scalar(xn[:, u, :], X[:, t, :], MV[:, t, 0:1], rstd[:, t:t + 1], ALU.subtract,
                                          ALU.mult).then_inc(xn_ready, 1)
                    if g:
                        for n in range(2):
                            ring.wait_taken(dve, g - 1, f"xt{n}")
                        for k in range(KC):
                            dve.bn_stats(bst[:, k, g - 1, :], NT[:, k, (g - 1) * GT:g * GT])
                for n in range(2):
                    ring.wait_taken(dve, GROUPS - 1, f"xt{n}")
                for k in range(KC):
                    ins = dve.bn_stats(bst[:, k, GROUPS - 1, :], NT[:, k, (GROUPS - 1) * GT:])
                ins.then_inc(setup, 1)
                dve.wait_ge(setup, 2)
                for k in range(KC):
                    dve.bn_aggr(mvb[:, k, :], bst[:, k, :, :].rearrange("p g s -> p (g s)")).then_inc(stats, 1)
                dve.wait_ge(sd_sq, 1)
                dve.wait_ge(w_loaded, 64)
                dve.reciprocal(sd[:, :], sd[:, :]).then_inc(setup, 1)
                dve.wait_ge(setup, 3)
                dve.tensor_tensor(bn[:, :, 0], sd[:, :], gamma[:, :], ALU.mult).then_inc(setup, 1)
                dve.wait_ge(setup, 4)
                dve.tensor_tensor(sd[:, :], mvb[:, :, 0], bn[:, :, 0], ALU.mult).then_inc(setup, 1)
                dve.wait_ge(setup, 5)
                dve.tensor_tensor(bn[:, :, 1], beta[:, :], sd[:, :], ALU.subtract)

        downT = sb("downT", [P, KC, PK_EXPERTS])
        up = sb("up", [P, ECH, D])
        iota_i = sb("iota_i", [P, P], I32)
        iota = sb("iota", [P, P])
        iota_h = sb("iota_h", [P, P], F16)
        iota_w = sb("iota_w", [P, P, TB], F16)
        nt = sb("nt", [P, 2, KC, P])
        xb = sb("xb", [P, 2, KC, P])
        best = sb("best", [P, 2, PK_HEADS, PK_TOP])
        best_i = sb("best_i", [P, 2, PK_HEADS, PK_TOP], U32)
        best_f = sb("best_f", [P, 2, PK_HEADS, PK_TOP])
        pairs = sb("pairs", [P, PK_HEADS, PK_TOP * PK_TOP])
        score = sb("score", [P, PK_HEADS, PK_TOP])
        pick = sb("pick", [P, PK_HEADS, PK_TOP], U32)
        half_i = sb("half_i", [P, 2, PICKS], U32)
        half_f = sb("half_f", [P, 2, PICKS])
        hot = sb("hot", [P, 2, PICKS, PK_TOP])
        key = sb("key", [P, 2, PICKS])
        eid = sb("eid", [P, PICKS])
        eid_i = sb("eid_i", [P, PICKS], I32)
        ehl_i = sb("ehl_i", [P, 2, PICKS], I32)
        sig = sb("sig", [P, PICKS])
        rows = sb("rows", [P, 3, 2, PICKS], F16)
        identh = sb("identh", [P, P], F16)
        cols = sb("cols", [P, 3, P], F16)
        lohot = sb("lohot", [P, 2, P, TB], F16)
        hihot = sb("hihot", [P, 2, ECH, TB], F16)
        hisig = sb("hisig", [P, 2, ECH, TB], F16)
        act_h = sb("act_h", [P, 2, ECH, P])
        new = sb("new", [P, D])
        bst = sb("bst", [P, 6])
        mv = sb("mv", [P, 2])
        NB = P // TB

        def bank(n):
            return ctx.enter_context(nc.psum_tensor(f"{tag}_ps{n}", [P, 512], F32))

        sims = Ring(f"{tag}_sims", sem, [bank(0), bank(1)], ["s0", "s1"])
        tail = Ring(f"{tag}_tail", sem, [bank(2), bank(3)], ["cols", "y"])
        hid = Ring(f"{tag}_hid", sem, [bank(4), bank(5)], [f"h{c}" for c in range(ECH // 4)])
        wts = Ring(f"{tag}_wts", sem, [bank(6), bank(7)], [f"w{b}" for b in range(NB)])
        w_loaded = sem("w2_loaded")
        pool_link = sem("pool_link")
        consts = sem("consts")
        xb_ready = sem("xb_ready")
        score_ready = sem("score_ready")
        sig_ready = sem("sig_ready")
        rows_ready = sem("rows_ready")
        hot_ready = sem("hot_ready")
        hihot_ready = sem("hihot_ready")
        pick_link = sem("pick_link")
        row_link = sem("row_link")
        passed = sem("passed")
        block = ctx.enter_context(nc.Block())

        @block.sync
        def _(sp):
            sp.dma_start(downT[:, :, :], w["downT"][:, 0:PK_EXPERTS].rearrange("(k p) n -> p k n", p=P)).then_inc(
                w_loaded, 16)
            sp.dma_start(up[:, :, :], w["up"][0:PK_EXPERTS, :].rearrange("(c p) n -> p c n", p=P)).then_inc(
                w_loaded, 16)

        @block.gpsimd
        def _(pool):
            pool.iota(iota_i[:, :], [[1, P]], base=0, channel_multiplier=0).then_inc(pool_link, 1)
            pool.wait_ge(pool_link, 1)
            pool.tensor_copy(iota[:, :], iota_i[:, :]).then_inc(consts, 1)
            pool.tensor_copy(iota_h[:, :], iota_i[:, :]).then_inc(consts, 1)
            pool.tensor_copy(identh[:, :], ident[:, :]).then_inc(consts, 1)
            pool.wait_ge(pool_link, 1)
            pool.tensor_copy(iota_w[:, :, :], iota_i[:, :].rearrange("p (n a) -> p n a", a=1).broadcast_to(
                [P, P, TB])).then_inc(consts, 1)

        @block.scalar
        def _(act):
            def hidden(t, s, c):
                hid.wait_full(act, t, f"h{c}")
                hid.take(act.activation(act_h[:, s, 4 * c:4 * c + 4, :], hid.bank(f"h{c}")[:, :].rearrange(
                    "p (c n) -> p c n", c=4), ACT.Gelu), f"h{c}")

            def turn(i, last):
                for s in range(2):
                    t = i * 2 + s
                    act.wait_ge(score_ready, t + 1)
                    act.activation(sig[:, :], score[:, :, :].rearrange("p h k -> p (h k)"),
                                   ACT.Sigmoid).then_inc(sig_ready, 1)
                    tail.wait_full(act, t, "cols")
                    tail.take(act.activation(cols[:, :, :], tail.bank("cols")[:, :].bitcast(F16)[:, 0:3 * P].rearrange(
                        "p (c n) -> p c n", c=3), ACT.Copy), "cols")
                    if not (last and s == 1):
                        for c in range(ECH // 4):
                            hidden(t + 1, 1 - s, c)

            for c in range(ECH // 4):
                hidden(0, 0, c)
            with act.Fori(0, TILES // 2 - 1) as i:
                turn(i, False)
            turn(TILES // 2 - 1, True)

        @block.tensor
        def _(pe):
            for r in (sims, tail, hid, wts):
                r.start_empty(pe)
            pe.wait_ge(w_loaded, 32)
            pe.wait_ge(consts, 4)

            def similarity(t, s):
                pe.wait_ge(xb_ready, t + 1)
                for n in range(2):
                    sims.claim(pe, t, f"s{n}")
                    for k in range(KC):
                        ins = pe.matmul(sims.bank(f"s{n}")[:, :], xb[:, s, k, :], wm[:, k, n * 512:(n + 1) * 512],
                                        start=(k == 0), stop=(k == KC - 1))
                    sims.filled(ins)

            def hidden(t, s, c):
                hid.claim(pe, t, f"h{c}")
                for j in range(4):
                    for k in range(KC):
                        e = 4 * c + j
                        ins = pe.matmul(hid.bank(f"h{c}")[:, j * P:(j + 1) * P], downT[:, k, e * P:(e + 1) * P],
                                        nt[:, s, k, :], start=(k == 0), stop=(k == KC - 1))
                hid.filled(ins)

            def turn(i, last):
                for s in range(2):
                    t = i * 2 + s
                    more = not (last and s == 1)
                    tail.claim(pe, t, "cols")
                    pe.wait_ge(rows_ready, t + 1)
                    for n in range(3):
                        ins = pe.transpose(tail.bank("cols")[:, :].bitcast(F16)[:, n * P:(n + 1) * P],
                                           rows[:, n, :, :].rearrange("p a n -> p (a n)"), identh[:, :])
                    tail.filled(ins)
                    if more:
                        similarity(t + 1, 1 - s)
                    for b in range(NB):
                        wts.claim(pe, t, f"w{b}")
                        pe.wait_ge(hot_ready, t * NB + b + 1)
                        for j in range(TB):
                            ins = pe.matmul(wts.bank(f"w{b}")[:, j * ECH:(j + 1) * ECH], lohot[:, b % 2, :, j],
                                            hisig[:, b % 2, :, j], start=True, stop=True)
                        wts.filled(ins)
                        if more:
                            hidden(t + 1, 1 - s, b)
                    tail.claim(pe, t, "y")
                    for b in (NB - 2, NB - 1):
                        wts.wait_taken(pe, t, f"w{b}")
                    for c in range(ECH):
                        ins = pe.matmul(tail.bank("y")[:, 0:D], act_h[:, s, c, :], up[:, c, :], start=(c == 0),
                                        stop=(c == ECH - 1))
                    tail.filled(ins)

            similarity(0, 0)
            for c in range(ECH // 4):
                hidden(0, 0, c)
            with pe.Fori(0, TILES // 2 - 1) as i:
                turn(i, False)
            turn(TILES // 2 - 1, True)

        @block.vector
        def _(dve):
            dve.wait_ge(consts, 4)
            PICK_LINKS, ROW_LINKS = 16, 2

            def norm(t, s):
                for k in range(KC):
                    dve.tensor_scalar(nt[:, s, k, :], NT[:, k, bass.ds(t * P, P)], 1.0, None, ALU.mult)
                    ins = dve.tensor_scalar(xb[:, s, k, :], NT[:, k, bass.ds(t * P, P)], bn[:, k, 0:1], bn[:, k, 1:2],
                                            ALU.mult, ALU.add)
                ins.then_inc(xb_ready, 1)

            def picks(t):
                link = Tally(pick_link, t, PICK_LINKS)
                for n in range(2):
                    await_apart(dve, sims.full, t * 2 + n + 1, passed)
                    for h in range(PK_HEADS):
                        ins = dve.max(best[:, n, h, :], sims.bank(f"s{n}")[:, h * PK_KEYS:(h + 1) * PK_KEYS])
                    link.inc(ins)
                    await_apart(dve, link.sem, link.base + link.n, passed)
                    for h in range(PK_HEADS):
                        ins = dve.max_index(best_i[:, n, h, :], best[:, n, h, :],
                                            sims.bank(f"s{n}")[:, h * PK_KEYS:(h + 1) * PK_KEYS])
                    sims.take(ins, f"s{n}")
                for n in range(2):
                    sims.wait_taken(dve, t, f"s{n}")
                pair4 = pairs[:, :, :].rearrange("p h (i j) -> p h i j", i=PK_TOP)
                shape4 = [P, PK_HEADS, PK_TOP, PK_TOP]
                link.inc(dve.tensor_tensor(pair4,
                                           best[:, 0, :, :].rearrange("p h (i a) -> p h i a", a=1).broadcast_to(shape4),
                                           best[:, 1, :, :].rearrange("p h (a j) -> p h a j", a=1).broadcast_to(shape4),
                                           ALU.add))
                link.inc(dve.tensor_copy(best_f[:, :, :, :], best_i[:, :, :, :]))
                await_apart(dve, link.sem, link.base + link.n, passed)
                for h in range(PK_HEADS):
                    ins = dve.max(score[:, h, :], pairs[:, h, :])
                ins.then_inc(score_ready, 1)
                await_apart(dve, score_ready, t + 1, passed)
                for h in range(PK_HEADS):
                    ins = dve.max_index(pick[:, h, :], score[:, h, :], pairs[:, h, :])
                link.inc(ins)
                link.wait(dve)
                pk = pick[:, :, :].rearrange("p h k -> p (h k)")
                dve.tensor_scalar(half_i[:, 0, :], pk, 3, None, ALU.logical_shift_right)
                link.inc(dve.tensor_scalar(half_i[:, 1, :], pk, PK_TOP - 1, None, ALU.bitwise_and))
                link.wait(dve)
                link.inc(dve.tensor_copy(half_f[:, :, :], half_i[:, :, :]))
                link.wait(dve)
                wide = [P, 2 * PICKS, PK_TOP]
                link.inc(dve.tensor_tensor(hot[:, :, :, :].rearrange("p n k a -> p (n k) a"),
                                           half_f[:, :, :].rearrange("p n (k a) -> p (n k) a", a=1).broadcast_to(wide),
                                           iota[:, 0:PK_TOP].rearrange("p (a b) -> p a b", a=1).broadcast_to(wide),
                                           ALU.is_equal))
                link.wait(dve)
                for n in range(2):
                    h4 = hot[:, n, :, :].rearrange("p (h k) a -> p h k a", h=PK_HEADS)
                    ins = dve.tensor_tensor(h4, h4, best_f[:, n, :, :].rearrange(
                        "p h (b a) -> p h b a", b=1).broadcast_to([P, PK_HEADS, PK_TOP, PK_TOP]), ALU.mult)
                link.inc(ins)
                link.wait(dve)
                link.inc(dve.tensor_reduce(key[:, :, :], hot[:, :, :, :], AX_X, ALU.add))
                link.wait(dve)
                link.inc(dve.scalar_tensor_tensor(eid[:, :], key[:, 0, :], float(PK_KEYS), key[:, 1, :], ALU.mult,
                                                  ALU.add))
                link.wait(dve)
                link.inc(dve.tensor_copy(eid_i[:, :], eid[:, :]))
                link.wait(dve)
                dve.tensor_scalar(ehl_i[:, 0, :], eid_i[:, :], P - 1, None, ALU.bitwise_and)
                link.inc(dve.tensor_scalar(ehl_i[:, 1, :], eid_i[:, :], 7, None, ALU.logical_shift_right))
                link.wait(dve)
                dve.tensor_copy(rows[:, 0:2, 0, :], ehl_i[:, :, :])
                link.inc(dve.tensor_copy(rows[:, 0:2, 1, :], ehl_i[:, :, :]))
                dve.wait_ge(sig_ready, t + 1)
                link.inc(dve.tensor_scalar(sig[:, :], sig[:, :], LO_SCALE, None, ALU.mult))
                link.wait(dve)
                link.inc(dve.tensor_copy(rows[:, 2, 0, :], sig[:, :]))
                link.wait(dve)
                dve.tensor_tensor(rows[:, 2, 1, :], sig[:, :], rows[:, 2, 0, :], ALU.subtract).then_inc(rows_ready, 1)
                link.close()

            def weigh(t, s, b):
                wts.wait_full(dve, t, f"w{b}")
                hv = act_h[:, s, :, b * TB:(b + 1) * TB]
                wts.take(dve.tensor_tensor(hv, hv, wts.bank(f"w{b}")[:, :].rearrange("p (j c) -> p c j", c=ECH),
                                           ALU.mult), f"w{b}")

            def experts(t, s):
                tail.wait_taken(dve, t, "cols")
                for b in range(NB):
                    if b >= 2:
                        wts.wait_full(dve, t, f"w{b - 2}")
                    blk = slice(b * TB, (b + 1) * TB)

                    def spread(n, width):
                        return cols[:, n, blk].rearrange("p (a j) -> p a j", a=1).broadcast_to([P, width, TB])

                    dve.tensor_tensor(hihot[:, b % 2, :, :], iota_w[:, 0:ECH, :], spread(1, ECH),
                                      ALU.is_equal).then_inc(hihot_ready, 1)
                    dve.tensor_tensor(lohot[:, b % 2, :, :], iota_w[:, :, :], spread(0, P), ALU.is_equal)
                    dve.wait_ge(hihot_ready, t * NB + b + 1)
                    dve.tensor_tensor(hisig[:, b % 2, :, :], hihot[:, b % 2, :, :], spread(2, ECH),
                                      ALU.mult).then_inc(hot_ready, 1)
                    if b == 0:
                        hid.wait_taken(dve, t, f"h{ECH // 4 - 2}")
                        hid.wait_taken(dve, t, f"h{ECH // 4 - 1}")
                    if b:
                        weigh(t, s, b - 1)
                weigh(t, s, NB - 1)

            def finish(t):
                link = Tally(row_link, t, ROW_LINKS)
                tail.wait_full(dve, t, "y")
                tail.take(dve.scalar_tensor_tensor(new[:, :].rearrange("p (a n) -> p a n", a=1),
                                                   tail.bank("y")[:, 0:D].rearrange("p (a n) -> p a n", a=1),
                                                   1.0 / LO_SCALE, X[:, bass.ds(t, 1), :], ALU.mult, ALU.add), "y")
                tail.wait_taken(dve, t, "y")
                finish_rows(dve, keep, link, t, new, bst, mv)
                link.close()

            def turn(i, last):
                for s in range(2):
                    t = i * 2 + s
                    more = not (last and s == 1)
                    if more:
                        norm(t + 1, 1 - s)
                    experts(t, s)
                    if more:
                        picks(t + 1)
                    finish(t)

            norm(0, 0)
            picks(0)
            with dve.Fori(0, TILES // 2 - 1) as i:
                turn(i, False)
            turn(TILES // 2 - 1, True)


MOE = 8


def top2_experts(nc, keep, w, out):
    tag = "mo"
    with ExitStack() as ctx:
        def sb(name, shape, dt=F32):
            return ctx.enter_context(nc.sbuf_tensor(f"{tag}_{name}", shape, dt))

        def sem(name):
            return keep["semaphore"](f"{tag}_{name}")

        X, MV, ident = keep["X"], keep["MV"], keep["ident"]
        we = sb("we", [P, KC, MOE, D])
        gate = sb("gate", [P, KC, MOE])
        iota_i = sb("iota_i", [P, MOE], I32)
        iota = sb("iota", [P, MOE])
        rstd = sb("rstd", [P, TILES])
        xn = sb("xn", [P, G, D])
        xnT = sb("xnT", [P, KC, GT])
        lg = sb("lg", [P, G, MOE])
        top = sb("top", [P, G, 8])
        top_i = sb("top_i", [P, G, 8], U32)
        top_f = sb("top_f", [P, G, 2])
        e2 = sb("e2", [P, G])
        den = sb("den", [P, G])
        pair = sb("pair", [P, 2, G])
        wf = sb("wf", [P, G, MOE])
        wf2 = sb("wf2", [P, G, MOE])
        acc = sb("acc", [P, 2, G, D])
        banks = [ctx.enter_context(nc.psum_tensor(f"{tag}_ps{b}", [P, 512], F32)) for b in range(5)]
        ring = Ring(f"{tag}_ring", sem, banks, ["xt0", "xt1", "lg0", "lg1"]
                    + [f"e{q}_{u}" for u in range(G) for q in range(MOE // 2)])
        w_loaded = sem("w_loaded")
        pool_link = sem("pool_link")
        consts = sem("consts")
        rstd_sq = sem("rstd_sq")
        setup = sem("setup")
        xn_ready = sem("xn_ready")
        diff_ready = sem("diff_ready")
        e2_ready = sem("e2_ready")
        acc_ready = sem("acc_ready")
        stored = sem("stored")
        passed = sem("passed")
        dve_link = sem("dve_link")
        out_v = out.rearrange("t p d -> p t d")
        block = ctx.enter_context(nc.Block())

        @block.sync
        def _(sp):
            sp.dma_start(gate[:, :, :], w["gate"].rearrange("(k p) n -> p k n", p=P)).then_inc(w_loaded, 16)
            sp.dma_start(we[:, :, :, :], w["we"]).then_inc(w_loaded, 16)
            with sp.Fori(0, GROUPS) as g:
                sp.wait_ge(acc_ready, g + 1)
                sp.dma_start(out_v[:, bass.ds(g * G, G), :], acc[:, 1, :, :]).then_inc(stored, 16)
            sp.wait_ge(stored, 16 * (GROUPS + 1))

        @block.gpsimd
        def _(pool):
            pool.iota(iota_i[:, :], [[1, MOE]], base=0, channel_multiplier=0).then_inc(pool_link, 1)
            pool.wait_ge(pool_link, 1)
            pool.tensor_copy(iota[:, :], iota_i[:, :]).then_inc(consts, 1)

        @block.scalar
        def _(act):
            layer_norm_scale(act, None, keep, rstd, rstd_sq, None)
            with act.Fori(0, GROUPS) as g:
                for n in range(2):
                    ring.wait_full(act, g, f"xt{n}")
                    ring.take(act.activation(xnT[:, :, n * 256:(n + 1) * 256],
                                             ring.bank(f"xt{n}")[:, :].rearrange("p (k n) -> p k n", k=KC),
                                             ACT.Copy), f"xt{n}")
                act.wait_ge(diff_ready, g + 1)
                act.activation(e2[:, :], e2[:, :], ACT.Exp).then_inc(e2_ready, 1)

        @block.tensor
        def _(pe):
            ring.start_empty(pe)
            pe.wait_ge(w_loaded, 32)
            with pe.Fori(0, GROUPS) as g:
                for n in range(2):
                    ring.claim(pe, g, f"xt{n}")
                    for u in (2 * n, 2 * n + 1):
                        pe.wait_ge(xn_ready, g * G + u + 1)
                        for k in range(KC):
                            at = k * 256 + (u % 2) * P
                            ins = pe.transpose(ring.bank(f"xt{n}")[:, at:at + P], xn[:, u, k * P:(k + 1) * P],
                                               ident[:, :])
                    ring.filled(ins)
                for n in range(2):
                    ring.wait_taken(pe, g, f"xt{n}")
                for n in range(2):
                    ring.claim(pe, g, f"lg{n}")
                    for u in (2 * n, 2 * n + 1):
                        for k in range(KC):
                            ins = pe.matmul(ring.bank(f"lg{n}")[:, (u % 2) * MOE:(u % 2 + 1) * MOE],
                                            xnT[:, k, u * P:(u + 1) * P], gate[:, k, :], start=(k == 0),
                                            stop=(k == KC - 1))
                    ring.filled(ins)
                for u in range(G):
                    for q in range(MOE // 2):
                        ring.claim(pe, g, f"e{q}_{u}")
                        for k in range(KC):
                            ins = pe.matmul(ring.bank(f"e{q}_{u}")[:, :], xnT[:, k, u * P:(u + 1) * P],
                                            we[:, k, 2 * q:2 * q + 2, :].rearrange("p e n -> p (e n)"),
                                            start=(k == 0), stop=(k == KC - 1))
                        ring.filled(ins)

        @block.vector
        def _(dve):
            layer_norm_scale(None, dve, keep, rstd, rstd_sq, setup)
            dve.wait_ge(consts, 1)
            dve.sem_inc(stored, 16)
            with dve.Fori(0, GROUPS) as g:
                link = Tally(dve_link, g, 11 + 4 * G)
                for u in range(G):
                    t = g * G + u
                    dve.tensor_scalar(xn[:, u:u + 1, :], X[:, bass.ds(t, 1), :], MV[:, bass.ds(t, 1), 0],
                                      rstd[:, bass.ds(t, 1)], ALU.subtract, ALU.mult).then_inc(xn_ready, 1)
                for n in range(2):
                    ring.wait_full(dve, g, f"lg{n}")
                    ring.take(dve.tensor_copy(lg[:, 2 * n:2 * n + 2, :], ring.bank(f"lg{n}")[:, 0:2 * MOE].rearrange(
                        "p (u e) -> p u e", u=2)), f"lg{n}")
                for n in range(2):
                    use = f"lg{n}"
                    m = ring.at[use]
                    await_apart(dve, ring.taken[m % ring.n_banks],
                                g * (ring.per // ring.n_banks) + m // ring.n_banks + 2, passed)
                for u in range(G):
                    ins = dve.max(top[:, u, :], lg[:, u, :])
                link.inc(ins)
                await_apart(dve, link.sem, link.base + link.n, passed)
                for u in range(G):
                    ins = dve.max_index(top_i[:, u, :], top[:, u, :], lg[:, u, :])
                link.inc(ins)
                dve.tensor_tensor(e2[:, :], top[:, :, 1], top[:, :, 0], ALU.subtract).then_inc(diff_ready, 1)
                link.wait(dve)
                link.inc(dve.tensor_copy(top_f[:, :, :], top_i[:, :, 0:2]))
                dve.wait_ge(e2_ready, g + 1)
                link.inc(dve.tensor_scalar(den[:, :], e2[:, :], 1.0, None, ALU.add))
                link.wait(dve)
                link.inc(dve.reciprocal(pair[:, 0, :], den[:, :]))
                link.wait(dve)
                link.inc(dve.tensor_tensor(pair[:, 1, :], e2[:, :], pair[:, 0, :], ALU.mult))
                link.wait(dve)
                shape = [P, G, MOE]
                place = iota[:, :].rearrange("p (a e) -> p a e", a=1).broadcast_to(shape)
                for n, dst in ((0, wf), (1, wf2)):
                    link.inc(dve.tensor_tensor(dst[:, :, :], top_f[:, :, n:n + 1].broadcast_to(shape), place,
                                               ALU.is_equal))
                    link.wait(dve)
                    link.inc(dve.tensor_tensor(dst[:, :, :], dst[:, :, :], pair[:, n, :].rearrange(
                        "p (u a) -> p u a", a=1).broadcast_to(shape), ALU.mult))
                    link.wait(dve)
                link.inc(dve.tensor_tensor(wf[:, :, :], wf[:, :, :], wf2[:, :, :], ALU.add))
                link.wait(dve)
                dve.wait_ge(stored, g * 16 + 16)
                for u in range(G):
                    t = g * G + u
                    for q in range(MOE // 2):
                        ring.wait_full(dve, g, f"e{q}_{u}")
                        for j in range(2):
                            e = 2 * q + j
                            src = ring.bank(f"e{q}_{u}")[:, j * D:(j + 1) * D].rearrange("p (a n) -> p a n", a=1)
                            prev = X[:, bass.ds(t, 1), :] if e == 0 else acc[:, (e + 1) % 2, u:u + 1, :]
                            ins = dve.scalar_tensor_tensor(acc[:, e % 2, u:u + 1, :], src, wf[:, u, e:e + 1], prev,
                                                           ALU.mult, ALU.add)
                            if j == 0:
                                link.inc(ins)
                                link.wait(dve)
                            else:
                                ring.take(ins, f"e{q}_{u}")
                                ring.wait_taken(dve, g, f"e{q}_{u}")
                dve.sem_inc(acc_ready, 1)
                link.close()


def build(nc, a, out, stages):
    with ExitStack() as ctx:
        def sb(name, shape, dt=F32):
            return ctx.enter_context(nc.sbuf_tensor(name, shape, dt))

        keep = {"X": sb("X", [P, TILES, D]), "MV": sb("MV", [P, TILES, 2]), "ident": sb("ident", [P, P]),
                "eps": sb("eps", [P, 1]), "tau": sb("tau", [P, TILES]), "quarter": sb("quarter", [P, 1]),
                "delta_rows": a["delta_rows"]}
        X, MV, ident = keep["X"], keep["MV"], keep["ident"]
        in_use = []

        def semaphore(name):
            in_use.append(nc.alloc_semaphore(name))
            return in_use[-1]

        def clear_semaphores():
            nc.clear_and_free_semaphores(in_use)
            nc.all_engine_barrier()
            in_use.clear()

        keep["semaphore"] = semaphore
        with ExitStack() as c2:
            x_loaded = c2.enter_context(nc.semaphore("x_loaded"))
            c_loaded = c2.enter_context(nc.semaphore("c_loaded"))
            id_zero = c2.enter_context(nc.semaphore("id_zero"))
            start_link = c2.enter_context(nc.semaphore("start_link"))
            bst = c2.enter_context(nc.sbuf_tensor("bst0", [P, TILES, 6], F32))
            block = c2.enter_context(nc.Block())

            @block.sync
            def _(sp):
                sp.dma_start(X[:, :, :], a["x"].rearrange("t p d -> p t d")).then_inc(x_loaded, 16)
                sp.dma_start(keep["tau"][:, :], a["tau"]).then_inc(c_loaded, 16)
                sp.dma_start(keep["quarter"][:, :], a["quarter"]).then_inc(c_loaded, 16)
                sp.wait_ge(c_loaded, 32)

            @block.gpsimd
            def _(pool):
                pool.memset(ident[:, :], 0.0).then_inc(id_zero, 1)
                pool.memset(keep["eps"][:, :], LN_EPS)
                pool.wait_ge(id_zero, 1)
                pool.affine_select(out=ident[:, :], in_=ident[:, :], compare_op=ALU.not_equal, fill=1.0,
                                   base=0, pattern=[[-1, P]], channel_multiplier=1)

            @block.vector
            def _(dve):
                dve.wait_ge(x_loaded, 16)
                for t in range(TILES):
                    ins = dve.bn_stats(bst[:, t, :], X[:, t, :])
                ins.then_inc(start_link, 1)
                dve.wait_ge(start_link, 1)
                for t in range(TILES):
                    dve.bn_aggr(MV[:, t, :], bst[:, t, :])

        def att(n):
            return {k: a[f"L{n}_{k}"] for k in ("wq", "wk", "wv", "wo", "bq", "bk", "bv", "bo")}

        if stages >= 1:
            attention(nc, keep, "a0", att(0), a["ctxT"])
        if stages >= 2:
            row_dram = nc.dram_tensor("row_dram", (TOKENS, ROW), F32, kind="Internal").ap()
            sum_dram = nc.dram_tensor("sum_dram", (TOKENS, D), F32, kind="Internal").ap()
            with ExitStack() as c2:
                idx = c2.enter_context(nc.sbuf_tensor("idx", [P, EXPERTS, SLOTS], U32))
                probs = c2.enter_context(nc.sbuf_tensor("gate_probs", [P, TILES, EXPERTS], F32))
                fw = {k: a[f"L0_{k}"] for k in ("gate", "Ws1", "Ws2", "bs1", "bs2", "W1", "W2", "b1", "b2")}
                shared_ffn(nc, keep, fw, probs, row_dram, sum_dram)
                choose_tokens(nc, keep, probs, idx)
                routed_ffn(nc, keep, fw, idx, row_dram, sum_dram)
        clear_semaphores()
        if stages >= 3:
            attention(nc, keep, "a1", att(1), a["ctxT"])
        if stages >= 4:
            bit_ffn(nc, keep, {n: a[f"L1_{n}"] for n in ("w_gate", "w_up", "w_down")})
        if stages >= 5:
            windowed_attention(nc, keep, {n: a[f"L2_{n}"] for n in ("W_a", "W_c", "pt", "len")}, a["ctxT"], a["ctx"])
        clear_semaphores()
        if stages >= 6:
            product_key_experts(nc, keep, {n: a[f"L2_{n}"] for n in ("w_q", "keys", "gamma", "beta", "downT", "up")})
        if stages >= 7:
            attention(nc, keep, "a3", att(3), a["ctxT"])
        if stages >= 8:
            top2_experts(nc, keep, {n: a[f"L3_{n}"] for n in ("gate", "we")}, out)
            return
        with ExitStack() as c2:
            stored = c2.enter_context(nc.semaphore("stored"))
            block = c2.enter_context(nc.Block())

            @block.sync
            def _(sp):
                sp.dma_start(out.rearrange("t p d -> p t d"), X[:, :, :]).then_inc(stored, 16)
                sp.wait_ge(stored, 16)


STAGES = 8


def lay_out(i):
    import numpy as np

    def rows(v):
        return np.ascontiguousarray(np.broadcast_to(np.asarray(v).reshape(1, -1), (P, np.asarray(v).size)))

    def padded(wt):
        o = np.zeros((wt.shape[0], HC * 4, 32), np.float32)
        o[:, :, 0:DK] = wt.reshape(wt.shape[0], HC * 4, DK)
        return o.reshape(wt.shape[0], HC * P)

    def turned(w):
        return np.ascontiguousarray(np.asarray(w).T)

    a = {"x": np.asarray(i["x"]), "ctxT": turned(np.asarray(i["ctx_1024"]).reshape(TILES * P, D))}
    a["tau"] = rows(i["condB_tau"])
    dr = np.zeros((P, TILES * P), np.float32)
    dr[DK::32, :] = np.asarray(i["fside_BxS2_0"]).reshape(1, -1)
    a["delta_rows"] = dr
    qr = np.zeros((P, 1), np.float32)
    qr[DK::32, :] = 1.0 / DK ** 0.5
    a["quarter"] = qr
    for n in (0, 1, 3):
        for m in "qk":
            a[f"L{n}_w{m}"] = padded(turned(i[f"L{n}_xcond_W{m}"]))
            a[f"L{n}_b{m}"] = turned(padded(np.asarray(i[f"L{n}_xcond_b{m}"]).reshape(1, -1)).reshape(HC, P))
        for m in "vo":
            a[f"L{n}_w{m}"] = turned(i[f"L{n}_xcond_W{m}"])
            a[f"L{n}_b{m}"] = rows(i[f"L{n}_xcond_b{m}"])
    for m in ("gate", "Ws1", "Ws2", "W1", "W2"):
        a[f"L0_{m}"] = np.asarray(i[f"L0_ffn_{m}"])
    a["L0_bs1"] = turned(np.asarray(i["L0_ffn_bs1"]).reshape(HCH, P))
    a["L0_bs2"] = rows(i["L0_ffn_bs2"])
    a["L0_b1"] = np.ascontiguousarray(np.asarray(i["L0_ffn_b1"]).reshape(EXPERTS, HCH, P).transpose(2, 0, 1))
    a["ctx"] = np.asarray(i["ctx_1024"]).reshape(TILES * P, D)
    for m in ("w_gate", "w_up", "w_down"):
        a[f"L1_{m}"] = turned(i[f"L1_ffn_{m}"])
    a["L2_W_a"] = np.asarray(i["L2_xcond_W_a"])
    a["L2_W_c"] = turned(i["L2_xcond_W_c"])
    a["L2_pt"] = rows(i["condB_pt"])
    a["L2_len"] = rows(i["_lenS2"])
    a["L2_w_q"] = np.asarray(i["L2_ffn_w_q"])
    a["L2_keys"] = np.ascontiguousarray(np.asarray(i["L2_ffn_keys_p"]).transpose(3, 2, 0, 1)).reshape(
        PK_DIM, 2 * PK_HEADS, PK_KEYS)
    a["L2_gamma"] = turned(np.asarray(i["L2_ffn_bn_gamma"]).reshape(KC, P))
    a["L2_beta"] = turned(np.asarray(i["L2_ffn_bn_beta"]).reshape(KC, P))
    a["L2_downT"] = turned(i["L2_ffn_down"])
    a["L2_up"] = np.asarray(i["L2_ffn_up"])
    a["L3_gate"] = turned(i["L3_ffn_gate_w"])
    a["L3_we"] = np.ascontiguousarray(np.asarray(i["L3_ffn_expert_w"]).transpose(2, 0, 1).reshape(
        KC, P, MOE, D).transpose(1, 0, 2, 3))
    a["L0_b2"] = np.ascontiguousarray(np.broadcast_to(np.asarray(i["L0_ffn_b2"])[None], (P, EXPERTS, D)))
    return a


def kernel(**inputs):
    import numpy as np
    import concourse.bacc as bacc
    from concourse.bass_utils import run_bass_kernel_spmd

    arrays = lay_out(inputs)
    nc = bacc.Bacc("TRN2", target_bir_lowering=False, num_devices=1)
    a = {n: nc.dram_tensor(f"in_{n}", v.shape, mybir.dt.from_np(v.dtype), kind="ExternalInput").ap()
         for n, v in arrays.items()}
    out = nc.dram_tensor("out_0", (TILES, P, D), F32, kind="ExternalOutput").ap()
    build(nc, a, out, STAGES)
    r = run_bass_kernel_spmd(nc, [{f"in_{n}": v for n, v in arrays.items()}], core_ids=[0])
    return r.results[0]["out_0"]
```

```python
from contextlib import ExitStack

import concourse.bass as bass
from concourse import mybir

ALU = mybir.AluOpType
ACT = mybir.ActivationFunctionType
F32 = mybir.dt.float32
BF16 = mybir.dt.bfloat16
F16 = mybir.dt.float16
I32 = mybir.dt.int32
U32 = mybir.dt.uint32
AX_X = mybir.AxisListType.X

P = 128
TILES = 32
D = 256
KC = D // P
HEADS = 16
DK = D // HEADS
HC = 4
G = 4
GT = G * P
GROUPS = TILES // G
LN_EPS = 1e-5


class Tally:

    def __init__(self, sem, turn, per):
        self.sem, self.base, self.per, self.n = sem, turn * per, per, 0

    def inc(self, ins):
        ins.then_inc(self.sem, 1)
        self.n += 1

    def wait(self, eng):
        eng.wait_ge(self.sem, self.base + self.n)

    def close(self):
        assert self.n == self.per, (self.sem, self.n, self.per)


class Ahead:

    def __init__(self, nc, tag, side, parts):
        self.stack = ExitStack()
        self.loaded = nc.alloc_semaphore(f"{tag}_w_loaded")
        self.at, self.sources = {}, []
        for name, shape, dt, source in parts:
            t = self.stack.enter_context(nc.sbuf_tensor(f"{tag}_{name}", shape, dt, side=side))
            self.at[name] = t
            self.sources.append((t[tuple(slice(None) for _ in shape)], source))

    def load(self, sp):
        for dst, src in self.sources:
            sp.dma_start(dst, src).then_inc(self.loaded, 16)

    def wait(self, eng):
        eng.wait_ge(self.loaded, 16 * len(self.sources))

    def free(self):
        self.stack.close()


def await_apart(eng, sem, value, passed):
    eng.wait_ge(sem, value)
    eng.sem_inc(passed, 1)


class Ring:

    def __init__(self, name, sem, banks, uses):
        assert len(uses) % len(banks) == 0
        self.banks, self.uses = banks, uses
        self.n_banks, self.per = len(banks), len(uses)
        self.full = sem(name + "_full")
        self.taken = [sem(f"{name}_taken{b}") for b in range(len(banks))]
        self.at = {u: n for n, u in enumerate(uses)}

    def bank(self, use):
        return self.banks[self.at[use] % self.n_banks]

    def start_empty(self, eng):
        for s in self.taken:
            eng.sem_inc(s, 1)

    def skip(self, eng, use):
        eng.sem_inc(self.full, 1)
        eng.sem_inc(self.taken[self.at[use] % self.n_banks], 1)

    def claim(self, pe, turn, use):
        n = self.at[use]
        pe.wait_ge(self.taken[n % self.n_banks], turn * (self.per // self.n_banks) + n // self.n_banks + 1)

    def wait_full(self, eng, turn, use):
        eng.wait_ge(self.full, turn * self.per + self.at[use] + 1)

    def filled(self, ins):
        ins.then_inc(self.full, 1)

    def take(self, ins, use):
        ins.then_inc(self.taken[self.at[use] % self.n_banks], 1)

    def wait_taken(self, eng, turn, use):
        n = self.at[use]
        eng.wait_ge(self.taken[n % self.n_banks], turn * (self.per // self.n_banks) + n // self.n_banks + 2)


def slots(eng, slot):
    for t in range(2):
        slot(t, t, None)
    with eng.Fori(1, TILES // 2 - 2) as i:
        for s in range(2):
            slot(i * 2 + s, s, None)
    for t in range(TILES - 4, TILES):
        slot(t, t % 2, TILES - 1 - t)


def turns(eng, turn):
    with eng.Fori(0, GROUPS // 2 - 1) as i:
        for s in range(2):
            turn(i * 2 + s, s, True)
    turn(GROUPS - 2, 0, True)
    turn(GROUPS - 1, 1, False)


def at_start(t, n):
    return isinstance(t, int) and t < n


def finish_rows(dve, keep, link, t, new, bst, mv):
    link.wait(dve)
    link.inc(dve.bn_stats(bst[:, :], new[:, :]))
    link.wait(dve)
    dve.tensor_scalar(keep["X"][:, bass.ds(t, 1), :], new[:, :].rearrange("p (a n) -> p a n", a=1), 1.0, None,
                      ALU.mult)
    link.inc(dve.bn_aggr(mv[:, :], bst[:, :]))
    link.wait(dve)
    dve.tensor_scalar(keep["MV"][:, bass.ds(t, 1), :], mv[:, :].rearrange("p (a n) -> p a n", a=1), 1.0, None,
                      ALU.mult)


def attention(nc, keep, tag, w, ctxT, following, load_first=False):
    with ExitStack() as ctx:
        def sb(name, shape, dt=F32):
            return ctx.enter_context(nc.sbuf_tensor(f"{tag}_{name}", shape, dt))

        def sem(name):
            return keep["semaphore"](f"{tag}_{name}")

        def psum(name, shape):
            return ctx.enter_context(nc.psum_tensor(f"{tag}_ps_{name}", shape, F32))

        X, MV, ident = keep["X"], keep["MV"], keep["ident"]
        wq, wk, wv, wo, bq, bk, bv, bo = (w.at[n] for n in ("wq", "wk", "wv", "wo", "bq", "bk", "bv", "bo"))
        delta = sb("delta", [P, TILES * P])
        tau4 = sb("tau4", [P, TILES])
        rstd = sb("rstd", [P, TILES])
        rstd_tau = sb("rstd_tau", [P, TILES])
        bq_tau = sb("bq_tau", [P, HC, TILES])
        ctx_t = sb("ctx_t", [P, 2, KC, P])
        xn = sb("xn", [P, D])
        xnT = sb("xnT", [P, KC, P])
        vraw = sb("vraw", [P, D])
        qT = sb("qT", [P, HC, P])
        kT = sb("kT", [P, 2, HC, P])
        v32 = sb("v32", [P, D])
        kraw = sb("kraw", [P, HC, P])
        v_parts = sb("v_parts", [P, 2, 2, HEADS, DK + 1], F16)
        probs = sb("probs", [P, 2, HEADS * P])
        pT = sb("pT", [P, 2, HEADS, P], F16)
        mx = sb("mx", [P, HEADS])
        rden = sb("rden", [P, HEADS])
        on = sb("on", [P, D])
        oT = sb("oT", [P, KC, P])
        tmp = sb("tmp", [P, D])
        new = sb("new", [P, D])
        bst = sb("bst", [P, 6])
        mv = sb("mv", [P, 2])

        ps_s = psum("s", [P, 4, HC, P])
        tr = Ring(f"{tag}_tr", sem, [psum("t0", [P, 4, P]), psum("t1", [P, 4, P])], [f"t{j}" for j in range(4)])
        proj = Ring(f"{tag}_proj", sem, [psum("p", [P, 512])], ["v", "x", "k", "q"])
        outs = Ring(f"{tag}_outs", sem, [psum("o", [P, 512])], ["pv", "ot", "y"])

        delta_zero = sem("delta_zero")
        delta_loaded = sem("delta_loaded")
        ctx_loaded = [sem(f"ctx_loaded{s}") for s in range(2)]
        rstd_sq = sem("rstd_sq")
        xn_ready = sem("xn_ready")
        s_ready = sem("s_ready")
        s_taken = sem("s_taken")
        p_ready = sem("p_ready")
        high_ready = sem("high_ready")
        pool_link = sem("pool_link")
        v_ready = sem("v_ready")
        k_ready = sem("k_ready")
        shift_link = sem("shift_link")
        norm_link = sem("norm_link")
        row_link = sem("row_link")
        setup_link = sem("setup_link")

        ctx_v = ctxT.rearrange("(k p) n -> p k n", p=P)
        block = ctx.enter_context(nc.Block())

        @block.sync
        def _(sp):
            for s in range(2):
                sp.dma_start(ctx_t[:, s, :, :], ctx_v[:, :, s * P:(s + 1) * P]).then_inc(ctx_loaded[s], 16)
            if load_first:
                w.load(sp)
            sp.wait_ge(delta_zero, 1)
            for r in range(4):
                row = 32 * r + DK
                sp.dma_start(delta[row:row + 1, :], keep["delta"]).then_inc(delta_loaded, 16)
            following.load(sp)
            with sp.Fori(1, TILES // 2) as i:
                for s in range(2):
                    proj.wait_full(sp, i * 2 + s - 1, "v")
                    sp.dma_start(ctx_t[:, s, :, :], ctx_v[:, :, bass.ds((i * 2 + s) * P, P)]).then_inc(
                        ctx_loaded[s], 16)

        @block.scalar
        def _(act):
            def norm_columns(t):
                proj.wait_full(act, t, "x")
                proj.take(act.activation(xnT[:, :, :], proj.bank("x")[:, 0:D].rearrange("p (k n) -> p k n", k=KC),
                                         ACT.Copy), "x")

            def keys(t):
                proj.wait_full(act, t, "k")
                if not at_start(t, 1):
                    act.wait_ge(k_ready, t)
                for c in range(HC):
                    ins = act.activation(kraw[:, c, :], proj.bank("k")[:, c * P:(c + 1) * P], ACT.Identity,
                                         bias=bk[:, c:c + 1])
                proj.take(ins, "k")

            def values(t):
                proj.wait_full(act, t + 1, "v")
                if not at_start(t, 1):
                    act.wait_ge(v_ready, t)
                proj.take(act.activation(vraw[:, :], proj.bank("v")[:, 0:D], ACT.Copy), "v")

            def exps(t, s, half):
                act.wait_ge(s_taken, 2 * t + half + 3)
                p = probs[:, s, half * 8 * P:(half + 1) * 8 * P]
                act.activation(p, p, ACT.Exp).then_inc(p_ready, 1)

            def turned_outputs(t):
                outs.wait_full(act, t, "ot")
                outs.take(act.activation(oT[:, :, :], outs.bank("ot")[:, 0:D].rearrange("p (k n) -> p k n", k=KC),
                                         ACT.Copy), "ot")

            def high_parts(t, j):
                tr.wait_full(act, t, f"t{j}")
                act.activation(pT[:, 0, 4 * j:4 * j + 4, :], tr.bank(f"t{j}")[:, :, :], ACT.Copy).then_inc(
                    high_ready, 1)

            def slot(t, s, after):
                high_parts(t, 0)
                high_parts(t, 1)
                if not at_start(t, 1):
                    turned_outputs(t - 1)
                if after is None or after >= 1:
                    values(t + 1)
                high_parts(t, 2)
                if after is None or after >= 2:
                    norm_columns(t + 2)
                high_parts(t, 3)
                if after is None or after >= 2:
                    keys(t + 2)
                if after is None or after >= 1:
                    for half in range(2):
                        exps(t + 1, 1 - s, half)

            act.activation(rstd[:, :], MV[:, :, 1], ACT.Sqrt, bias=keep["eps"][:, 0:1]).then_inc(rstd_sq, 1)
            act.wait_ge(setup_link, 5)
            norm_columns(0)
            keys(0)
            values(0)
            norm_columns(1)
            for half in range(2):
                exps(0, 0, half)
            keys(1)
            slots(act, slot)
            turned_outputs(TILES - 1)

        @block.gpsimd
        def _(pool):
            def values(t, s):
                link = Tally(pool_link, t, 2)
                high, low = (v_parts[:, s, n, :, 0:DK] for n in range(2))
                proj.wait_taken(pool, t + 1, "v")
                link.inc(pool.tensor_tensor(v32[:, :], vraw[:, :], bv[:, :], ALU.add))
                link.inc(pool.tensor_tensor(high, vraw[:, :].rearrange("p (h d) -> p h d", h=HEADS),
                                            bv[:, :].rearrange("p (h d) -> p h d", h=HEADS), ALU.add))
                link.wait(pool)
                pool.tensor_tensor(low, v32[:, :].rearrange("p (h d) -> p h d", h=HEADS), high,
                                   ALU.subtract).then_inc(v_ready, 1)
                link.close()

            def keys(t, s):
                proj.wait_taken(pool, t, "k")
                pool.tensor_tensor(kT[:, s, :, :], kraw[:, :, :], delta[:, bass.ds(t * P, P)].rearrange(
                    "p (a n) -> p a n", a=1).broadcast_to([P, HC, P]), ALU.add).then_inc(k_ready, 1)

            w.wait(pool)
            pool.wait_ge(delta_loaded, 64)
            keys(0, 0)
            values(0, 0)
            keys(1, 1)
            values(1, 1)
            with pool.Fori(1, TILES // 2) as i:
                for s in range(2):
                    keys(i * 2 + s, s)
                    values(i * 2 + s, s)

        @block.tensor
        def _(pe):
            for r in (tr, proj, outs):
                r.start_empty(pe)
            pe.sem_inc(s_taken, 2)
            w.wait(pe)

            def norm_columns(t):
                proj.claim(pe, t, "x")
                pe.wait_ge(xn_ready, t + 1)
                for k in range(KC):
                    ins = pe.transpose(proj.bank("x")[:, k * P:(k + 1) * P], xn[:, k * P:(k + 1) * P], ident[:, :])
                proj.filled(ins)

            PRODUCTS = HC * KC

            def project(t, use, wt, rhs, n):
                c, k = divmod(n, KC)
                if n == 0:
                    proj.claim(pe, t, use)
                ins = pe.matmul(proj.bank(use)[:, c * P:(c + 1) * P], wt[:, k, c * P:(c + 1) * P], rhs[:, k, :],
                                start=(k == 0), stop=(k == KC - 1))
                if n == PRODUCTS - 1:
                    proj.filled(ins)

            def queries(t, n):
                project(t, "q", wq, xnT, n)

            def keys(t, s, n):
                if n == 0:
                    pe.wait_ge(ctx_loaded[s], (t - s) * 8 + 16)
                project(t, "k", wk, ctx_t[:, s, :, :], n)

            def values(t, s):
                proj.claim(pe, t + 1, "v")
                for k in range(KC):
                    ins = pe.matmul(proj.bank("v")[:, 0:D], ctx_t[:, s, k, :], wv[:, k, :], start=(k == 0),
                                    stop=(k == KC - 1))
                proj.filled(ins)

            def scores(t, s, half, keys_too):
                pe.wait_ge(s_taken, 2 * t + half + 1)
                if half == 0:
                    pe.wait_ge(k_ready, t + 1)
                for c in range(HC):
                    for r in (2 * half, 2 * half + 1):
                        if c == 0 and r == 0:
                            proj.wait_taken(pe, t, "q")
                        ins = pe.matmul(ps_s[:, r, c, :], qT[32 * r:32 * r + 32, c, :],
                                        kT[32 * r:32 * r + 32, s, c, :], start=True, stop=True, skip_group_check=True)
                        if (c, r) == (HC - 1, 2 * half + 1):
                            ins.then_inc(s_ready, 1)
                        if keys_too:
                            keys(t + 1, 1 - s, 2 * c + r - 2 * half)

            def turn_outputs(t):
                outs.claim(pe, t, "ot")
                for k in range(KC):
                    ins = pe.transpose(outs.bank("ot")[:, k * P:(k + 1) * P], on[:, k * P:(k + 1) * P], ident[:, :])
                outs.filled(ins)

            def output_rows(t):
                outs.claim(pe, t, "y")
                for k in range(KC):
                    ins = pe.matmul(outs.bank("y")[:, 0:D], oT[:, k, :], wo[:, k, :], start=(k == 0),
                                    stop=(k == KC - 1))
                outs.filled(ins)

            def turn_probs(t, s, j):
                if j % 2 == 0:
                    pe.wait_ge(p_ready, 2 * t + j // 2 + 1)
                tr.claim(pe, t, f"t{j}")
                for c in range(4):
                    ins = pe.transpose(tr.bank(f"t{j}")[:, c, :], probs[:, s, (4 * j + c) * P:(4 * j + c + 1) * P],
                                       ident[:, :])
                tr.filled(ins)

            def weighted_values(s, j):
                for c in range(4):
                    h = 4 * c + j
                    for n in range(4):
                        ins = pe.matmul(outs.bank("pv")[:, h * (DK + 1):(h + 1) * (DK + 1)],
                                        pT[:, n // 2, 4 * j + c, :], v_parts[:, s, n % 2, h, :], start=(n == 0),
                                        stop=(n == 3), skip_group_check=True)
                return ins

            def slot(t, s, after):
                turn_probs(t, s, 0)
                turn_probs(t, s, 1)
                if not at_start(t, 1):
                    turn_outputs(t - 1)
                if after is None or after >= 1:
                    values(t + 1, 1 - s)
                turn_probs(t, s, 2)
                more = after is None or after >= 2
                if more:
                    norm_columns(t + 2)
                turn_probs(t, s, 3)
                if after is None or after >= 1:
                    scores(t + 1, 1 - s, 0, more)
                if not at_start(t, 1):
                    output_rows(t - 1)
                if after is None or after >= 1:
                    scores(t + 1, 1 - s, 1, False)
                outs.claim(pe, t, "pv")
                pe.wait_ge(v_ready, t + 1)
                for j in range(4):
                    tr.wait_taken(pe, t, f"t{j}")
                    ins = weighted_values(s, j)
                    if j in (1, 2) and more:
                        for n in range((j - 1) * PRODUCTS // 2, j * PRODUCTS // 2):
                            queries(t + 2, n)
                    if j == 3:
                        outs.filled(ins)

            proj.skip(pe, "v")
            norm_columns(0)
            for n in range(PRODUCTS):
                keys(0, 0, n)
            for n in range(PRODUCTS):
                queries(0, n)
            values(0, 0)
            for half in range(2):
                scores(0, 0, half, False)
            norm_columns(1)
            for n in range(PRODUCTS):
                keys(1, 1, n)
            for n in range(PRODUCTS):
                queries(1, n)
            slots(pe, slot)
            turn_outputs(TILES - 1)
            output_rows(TILES - 1)

        @block.vector
        def _(dve):
            def norm(t):
                if not at_start(t, 1):
                    proj.wait_full(dve, t - 1, "x")
                dve.tensor_scalar(xn[:, :].rearrange("p (a n) -> p a n", a=1), X[:, bass.ds(t, 1), :],
                                  MV[:, bass.ds(t, 1), 0], rstd_tau[:, bass.ds(t, 1)], ALU.subtract,
                                  ALU.mult).then_inc(xn_ready, 1)

            def queries(t):
                proj.wait_full(dve, t, "q")
                proj.take(dve.tensor_tensor(qT[:, :, :], proj.bank("q")[:, :].rearrange("p (c n) -> p c n", c=HC),
                                            bq_tau[:, :, bass.ds(t, 1)].broadcast_to([P, HC, P]), ALU.add), "q")

            def shift(t, s, half):
                link = Tally(shift_link, 2 * t + half, 1)
                dve.wait_ge(s_ready, 2 * t + half + 1)
                sv = ps_s[:, 2 * half:2 * half + 2, :, :].rearrange("p r c n -> p (r c) n")
                m = mx[:, 8 * half:8 * half + 8]
                link.inc(dve.tensor_reduce(m, sv, AX_X, ALU.max))
                link.wait(dve)
                if not at_start(t, 2):
                    tr.wait_full(dve, t - 2, f"t{2 * half + 1}")
                dve.tensor_tensor(probs[:, s, half * 8 * P:(half + 1) * 8 * P].rearrange("p (h n) -> p h n", n=P), sv,
                                  m.rearrange("p (h a) -> p h a", a=1).broadcast_to([P, 8, P]),
                                  ALU.subtract).then_inc(s_taken, 1)
                link.close()

            def divide(t):
                link = Tally(norm_link, t, 1)
                b = outs.bank("pv")[:, 0:HEADS * (DK + 1)].rearrange("p (h d) -> p h d", h=HEADS)
                outs.wait_full(dve, t, "pv")
                link.inc(dve.reciprocal(rden[:, :], b[:, :, DK]))
                link.wait(dve)
                outs.take(dve.tensor_tensor(on[:, :].rearrange("p (h d) -> p h d", h=HEADS), b[:, :, 0:DK],
                                            rden[:, :].rearrange("p (h a) -> p h a", a=1).broadcast_to(
                                                [P, HEADS, DK]), ALU.mult), "pv")
                link.close()

            def read_rows(t):
                outs.wait_full(dve, t, "y")
                outs.take(dve.tensor_tensor(tmp[:, :], outs.bank("y")[:, 0:D], bo[:, :], ALU.add), "y")

            def finish(t):
                link = Tally(row_link, t, 3)
                outs.wait_taken(dve, t, "y")
                link.inc(dve.tensor_tensor(new[:, :].rearrange("p (a n) -> p a n", a=1), X[:, bass.ds(t, 1), :],
                                           tmp[:, :].rearrange("p (a n) -> p a n", a=1), ALU.add))
                finish_rows(dve, keep, link, t, new, bst, mv)
                link.close()

            def low_parts(t, j):
                dve.wait_ge(high_ready, 4 * t + j + 1)
                at = slice(4 * j, 4 * j + 4)
                tr.take(dve.tensor_tensor(pT[:, 1, at, :], tr.bank(f"t{j}")[:, :, :], pT[:, 0, at, :],
                                          ALU.subtract), f"t{j}")

            def slot(t, s, after):
                for j in range(4):
                    low_parts(t, j)
                if not at_start(t, 2):
                    finish(t - 2)
                if after is None or after >= 3:
                    norm(t + 3)
                if not at_start(t, 1):
                    read_rows(t - 1)
                if after is None or after >= 1:
                    for half in range(2):
                        shift(t + 1, 1 - s, half)
                divide(t)
                if after is None or after >= 2:
                    queries(t + 2)

            dve.memset(delta[:, :], 0.0).then_inc(delta_zero, 1)
            dve.memset(v_parts[:, :, 0, :, DK:DK + 1], 1.0)
            dve.memset(v_parts[:, :, 1, :, DK:DK + 1], 0.0).then_inc(setup_link, 1)
            dve.wait_ge(rstd_sq, 1)
            dve.reciprocal(rstd[:, :], rstd[:, :]).then_inc(setup_link, 1)
            dve.tensor_scalar(tau4[:, :], keep["tau"][:, :], 1.0 / DK ** 0.5, None, ALU.mult).then_inc(setup_link, 1)
            dve.wait_ge(setup_link, 3)
            dve.tensor_tensor(rstd_tau[:, :], rstd[:, :], tau4[:, :], ALU.mult).then_inc(setup_link, 1)
            w.wait(dve)
            for c in range(HC):
                ins = dve.tensor_scalar(bq_tau[:, c, :], tau4[:, :], bq[:, c:c + 1], keep["quarter"][:, 0:1],
                                        ALU.mult, ALU.add)
            ins.then_inc(setup_link, 1)
            dve.wait_ge(setup_link, 5)
            norm(0)
            norm(1)
            queries(0)
            for half in range(2):
                shift(0, 0, half)
            norm(2)
            queries(1)
            slots(dve, slot)
            finish(TILES - 2)
            read_rows(TILES - 1)
            finish(TILES - 1)


TOKENS = TILES * P
EXPERTS = 8
CAPACITY = TOKENS // EXPERTS
SLOTS = CAPACITY // P
HID = 1024
HCH = HID // P
ROW = D + EXPERTS


def layer_norm_scale(act, dve, keep, rstd, sq, done):
    if act is not None:
        act.activation(rstd[:, :], keep["MV"][:, :, 1], ACT.Sqrt, bias=keep["eps"][:, 0:1]).then_inc(sq, 1)
    if dve is not None:
        dve.wait_ge(sq, 1)
        dve.reciprocal(rstd[:, :], rstd[:, :]).then_inc(done, 1)
        dve.wait_ge(done, 1)


def shared_ffn(nc, keep, w, probs, row_dram, sum_dram, following):
    tag = "sh"
    with ExitStack() as ctx:
        def sb(name, shape, dt=F32):
            return ctx.enter_context(nc.sbuf_tensor(f"{tag}_{name}", shape, dt))

        def sem(name):
            return keep["semaphore"](f"{tag}_{name}")

        X, MV, ident = keep["X"], keep["MV"], keep["ident"]
        w1, w2, gate, b1, b2 = (w.at[n] for n in ("w1", "w2", "gate", "b1", "b2"))
        rstd = sb("rstd", [P, TILES])
        row = sb("row", [P, G, ROW])
        xnT = sb("xnT", [P, KC, GT])
        hT = sb("hT", [P, HCH, GT])
        tmp = sb("tmp", [P, G, D])
        new = sb("new", [P, G, D])
        lg = sb("lg", [P, G, EXPERTS])
        lmx = sb("lmx", [P, G])
        lsum = sb("lsum", [P, G])
        banks = [ctx.enter_context(nc.psum_tensor(f"{tag}_ps{b}", [P, 512], F32)) for b in range(7)]
        first = Ring(f"{tag}_first", sem, banks[0:3], ["xt0", "xt1", "lg"])
        main = Ring(f"{tag}_main", sem, banks[3:7], [f"up{c}" for c in range(HCH)] + [f"y{u}" for u in range(G)])
        rstd_sq = sem("rstd_sq")
        rstd_done = sem("rstd_done")
        xn_ready = sem("xn_ready")
        lg_shifted = sem("lg_shifted")
        lg_exp = sem("lg_exp")
        row_ready = sem("row_ready")
        row_stored = sem("row_stored")
        sum_ready = sem("sum_ready")
        sum_stored = sem("sum_stored")
        gate_link = sem("gate_link")
        sum_link = sem("sum_link")
        row_v = row_dram.rearrange("(t p) n -> p t n", p=P)
        sum_v = sum_dram.rearrange("(t p) n -> p t n", p=P)
        block = ctx.enter_context(nc.Block())

        @block.sync
        def _(sp):
            following.load(sp)
            def rows_out(g):
                sp.wait_ge(row_ready, g + 1)
                sp.dma_start(row_v[:, bass.ds(g * G, G), :], row[:, :, :]).then_inc(row_stored, 16)

            def sums_out(g):
                sp.wait_ge(sum_ready, g + 1)
                sp.dma_start(sum_v[:, bass.ds(g * G, G), :], new[:, :, :]).then_inc(sum_stored, 16)

            rows_out(0)
            with sp.Fori(0, GROUPS - 1) as g:
                rows_out(g + 1)
                sums_out(g)
            sums_out(GROUPS - 1)
            sp.wait_ge(row_stored, 16 * (GROUPS + 1))
            sp.wait_ge(sum_stored, 16 * (GROUPS + 1))

        @block.scalar
        def _(act):
            layer_norm_scale(act, None, keep, rstd, rstd_sq, rstd_done)
            w.wait(act)

            def columns_and_gate(g):
                for i in range(2):
                    first.wait_full(act, g, f"xt{i}")
                    first.take(act.activation(xnT[:, :, i * 256:(i + 1) * 256],
                                              first.bank(f"xt{i}")[:, :].rearrange("p (k n) -> p k n", k=KC),
                                              ACT.Copy), f"xt{i}")
                act.wait_ge(lg_shifted, g + 1)
                act.activation(lg[:, :, :], lg[:, :, :], ACT.Exp).then_inc(lg_exp, 1)

            def turn(g, more):
                for c in range(HCH):
                    main.wait_full(act, g, f"up{c}")
                    main.take(act.activation(hT[:, c, :], main.bank(f"up{c}")[:, :], ACT.Gelu_apprx_tanh,
                                             bias=b1[:, c:c + 1]), f"up{c}")
                if more:
                    columns_and_gate(g + 1)

            columns_and_gate(0)
            with act.Fori(0, GROUPS - 1) as g:
                turn(g, True)
            turn(GROUPS - 1, False)

        @block.tensor
        def _(pe):
            for r in (first, main):
                r.start_empty(pe)
            w.wait(pe)

            def columns_and_gate(g):
                for i in range(2):
                    first.claim(pe, g, f"xt{i}")
                    for u in (2 * i, 2 * i + 1):
                        pe.wait_ge(xn_ready, g * G + u + 1)
                        for k in range(KC):
                            at = k * 256 + (u % 2) * P
                            ins = pe.transpose(first.bank(f"xt{i}")[:, at:at + P], row[:, u, k * P:(k + 1) * P],
                                               ident[:, :])
                    first.filled(ins)

            def gate_logits(g):
                for i in range(2):
                    first.wait_taken(pe, g, f"xt{i}")
                first.claim(pe, g, "lg")
                for u in range(G):
                    for k in range(KC):
                        ins = pe.matmul(first.bank("lg")[:, u * EXPERTS:(u + 1) * EXPERTS],
                                        xnT[:, k, u * P:(u + 1) * P], gate[:, k, :], start=(k == 0),
                                        stop=(k == KC - 1))
                first.filled(ins)

            def turn(g, more):
                for c in range(HCH):
                    main.claim(pe, g, f"up{c}")
                    for k in range(KC):
                        ins = pe.matmul(main.bank(f"up{c}")[:, :], w1[:, k, c * P:(c + 1) * P], xnT[:, k, :],
                                        start=(k == 0), stop=(k == KC - 1))
                    main.filled(ins)
                if more:
                    columns_and_gate(g + 1)
                for u in range(G):
                    main.claim(pe, g, f"y{u}")
                    for c in range(HCH):
                        if u == 0:
                            main.wait_taken(pe, g, f"up{c}")
                        ins = pe.matmul(main.bank(f"y{u}")[:, 0:D], hT[:, c, u * P:(u + 1) * P], w2[:, c, :],
                                        start=(c == 0), stop=(c == HCH - 1))
                    main.filled(ins)
                    if u == 0 and more:
                        gate_logits(g + 1)

            columns_and_gate(0)
            gate_logits(0)
            with pe.Fori(0, GROUPS - 1) as g:
                turn(g, True)
            turn(GROUPS - 1, False)

        @block.vector
        def _(dve):
            layer_norm_scale(None, dve, keep, rstd, rstd_sq, rstd_done)
            w.wait(dve)
            dve.sem_inc(row_stored, 16)
            dve.sem_inc(sum_stored, 16)

            def norm(g):
                dve.wait_ge(row_stored, g * 16 + 16)
                for u in range(G):
                    t = g * G + u
                    dve.tensor_scalar(row[:, u:u + 1, 0:D], X[:, bass.ds(t, 1), :], MV[:, bass.ds(t, 1), 0],
                                      rstd[:, bass.ds(t, 1)], ALU.subtract, ALU.mult).then_inc(xn_ready, 1)

            def gate_softmax(g):
                link = Tally(gate_link, g, 3)
                first.wait_full(dve, g, "lg")
                lv = first.bank("lg")[:, 0:G * EXPERTS].rearrange("p (u e) -> p u e", u=G)
                link.inc(dve.tensor_reduce(lmx[:, :], lv, AX_X, ALU.max))
                link.wait(dve)
                first.take(dve.tensor_tensor(lg[:, :, :], lv, lmx[:, :].rearrange(
                    "p (u a) -> p u a", a=1).broadcast_to([P, G, EXPERTS]), ALU.subtract), "lg")
                first.wait_taken(dve, g, "lg")
                dve.sem_inc(lg_shifted, 1)
                dve.wait_ge(lg_exp, g + 1)
                link.inc(dve.tensor_reduce(lsum[:, :], lg[:, :, :], AX_X, ALU.add))
                link.wait(dve)
                link.inc(dve.reciprocal(lsum[:, :], lsum[:, :]))
                link.wait(dve)
                lb = lsum[:, :].rearrange("p (u a) -> p u a", a=1).broadcast_to([P, G, EXPERTS])
                dve.tensor_tensor(probs[:, bass.ds(g * G, G), :], lg[:, :, :], lb, ALU.mult)
                dve.tensor_tensor(row[:, :, D:ROW], lg[:, :, :], lb, ALU.mult).then_inc(row_ready, 1)
                link.close()

            def turn(g, more):
                link = Tally(sum_link, g, G)
                if more:
                    norm(g + 1)
                dve.wait_ge(sum_stored, g * 16 + 16)
                for u in range(G):
                    t = g * G + u
                    main.wait_full(dve, g, f"y{u}")
                    main.take(dve.tensor_tensor(tmp[:, u, :], main.bank(f"y{u}")[:, 0:D], b2[:, :], ALU.add), f"y{u}")
                    main.wait_taken(dve, g, f"y{u}")
                    link.inc(dve.tensor_tensor(new[:, u:u + 1, :], X[:, bass.ds(t, 1), :],
                                               tmp[:, u:u + 1, :], ALU.add))
                    if u == 1 and more:
                        gate_softmax(g + 1)
                link.wait(dve)
                dve.sem_inc(sum_ready, 1)
                link.close()

            norm(0)
            gate_softmax(0)
            with dve.Fori(0, GROUPS - 1) as g:
                turn(g, True)
            turn(GROUPS - 1, False)


def choose_tokens(nc, keep, probs, idx, first_loads):
    tag = "ch"
    ROUNDS = 15
    ET = EXPERTS * TILES
    with ExitStack() as ctx:
        def sb(name, shape, dt=F32):
            return ctx.enter_context(nc.sbuf_tensor(f"{tag}_{name}", shape, dt))

        def sem(name):
            return keep["semaphore"](f"{tag}_{name}")

        ones = sb("ones", [P, P])
        before = sb("before", [P, P])
        iota_i = sb("iota_i", [P, P], I32)
        iota = sb("iota", [P, P])
        part_i = sb("part_i", [P, 1], I32)
        part = sb("part", [P, 1])
        tile_i = sb("tile_i", [P, ET], I32)
        tile_f = sb("tile_f", [P, ET])
        thr = sb("thr", [P, EXPERTS], I32)
        low_bit = sb("low_bit", [P, EXPERTS])
        bits = sb("bits", [P, 3, EXPERTS], I32)
        cand = sb("cand", [P, 3, EXPERTS], I32)
        flags = sb("flags", [P, 3, EXPERTS, TILES])
        counts = sb("counts", [P, 3, EXPERTS])
        hit = sb("hit", [P, 3, EXPERTS])
        reached = sb("reached", [P, EXPERTS])
        more_bits = sb("more_bits", [P, EXPERTS], I32)
        pe_t = sb("pe_t", [P, EXPERTS, TILES])
        flag = sb("flag", [P, EXPERTS, TILES])
        over = sb("over", [P, EXPERTS, TILES])
        count = sb("count", [P, EXPERTS])
        need = sb("need", [P, EXPERTS])
        carry = sb("carry", [P, ET])
        tot = sb("tot", [P, ET])
        inc_s = sb("inc_s", [P, ET])
        pos = sb("pos", [P, ET])
        pos_i = sb("pos_i", [P, ET], I32)
        hi_i = sb("hi_i", [P, ET], I32)
        hi = sb("hi", [P, ET])
        lo = sb("lo", [P, ET], BF16)
        iota_w = sb("iota_w", [P, P, TILES], BF16)
        chosen = sb("chosen", [P, ET])
        oh = sb("oh", [P, ET, SLOTS])
        rhs = sb("rhs", [P, ET, 2 * SLOTS], BF16)
        lohot = sb("lohot", [P, 2, P, TILES], BF16)
        half = sb("half", [P, EXPERTS, SLOTS])
        ps_c = ctx.enter_context(nc.psum_tensor(f"{tag}_ps_c", [P, 3, EXPERTS], F32))
        ps_a = ctx.enter_context(nc.psum_tensor(f"{tag}_ps_a", [P, ET], F32))
        ps_b = ctx.enter_context(nc.psum_tensor(f"{tag}_ps_b", [P, ET], F32))
        ps_i = ctx.enter_context(nc.psum_tensor(f"{tag}_ps_i", [P, EXPERTS, 2 * SLOTS], F32))
        consts = sem("consts")
        pool_link = sem("pool_link")
        bit_link = sem("bit_link")
        part_ready = sem("part_ready")
        counted = sem("counted")
        flags_ready = sem("flags_ready")
        summed = sem("summed")
        dl = sem("dl")
        lohot_ready = sem("lohot_ready")
        placed = sem("placed")
        wide_ready = sem("wide_ready")
        block = ctx.enter_context(nc.Block())

        @block.sync
        def _(sp):
            first_loads(sp)

        @block.gpsimd
        def _(pool):
            pool.memset(ones[:, :], 1.0).then_inc(pool_link, 1)
            pool.memset(carry[:, :], 1.0).then_inc(pool_link, 1)
            pool.wait_ge(pool_link, 2)
            pool.affine_select(out=before[:, :], in_=ones[:, :], compare_op=ALU.is_gt, fill=0.0, base=0,
                               pattern=[[1, P]], channel_multiplier=-1).then_inc(consts, 1)
            pool.memset(carry[:, :].rearrange("p (e t) -> p e t", e=EXPERTS)[:, :, 0:1], 0.0).then_inc(consts, 1)
            pool.iota(iota_i[:, :], [[1, P]], base=0, channel_multiplier=0).then_inc(pool_link, 1)
            pool.iota(part_i[:, :], [[0, 1]], base=0, channel_multiplier=1).then_inc(pool_link, 1)
            pool.iota(tile_i[:, :], [[0, EXPERTS], [1, TILES]], base=0, channel_multiplier=0).then_inc(pool_link, 1)
            pool.wait_ge(pool_link, 5)
            pool.tensor_copy(iota[:, :], iota_i[:, :]).then_inc(consts, 1)
            pool.tensor_copy(part[:, :], part_i[:, :]).then_inc(consts, 1)
            pool.tensor_copy(tile_f[:, :], tile_i[:, :]).then_inc(consts, 1)
            pool.tensor_copy(iota_w[:, :, :], iota_i[:, :].rearrange("p (n a) -> p n a", a=1).broadcast_to(
                [P, P, TILES])).then_inc(wide_ready, 1)

        @block.tensor
        def _(pe):
            pe.wait_ge(consts, 5)
            with pe.Fori(0, ROUNDS) as b:
                pe.wait_ge(part_ready, b + 1)
                pe.matmul(ps_c[:, :, :], ones[:, :], counts[:, :, :], start=True, stop=True).then_inc(counted, 1)
            pe.wait_ge(part_ready, ROUNDS + 1)
            pe.matmul(ps_c[:, 0, :], ones[:, :], count[:, :], start=True, stop=True).then_inc(counted, 1)
            for n in range(2):
                pe.wait_ge(flags_ready, n + 1)
                src = over[:, :, :].rearrange("p e t -> p (e t)") if n == 0 else chosen[:, :]
                pe.matmul(ps_a[:, :], before[:, :], src, start=True, stop=True)
                pe.matmul(ps_b[:, :], ones[:, :], src, start=True, stop=True).then_inc(summed, 1)
            with pe.Fori(0, EXPERTS // 2) as i:
                for s in range(2):
                    e = i * 2 + s
                    pe.wait_ge(lohot_ready, e + 1)
                    for t in range(TILES):
                        ins = pe.matmul(ps_i[:, bass.ds(e, 1), :], lohot[:, s, :, t],
                                        rhs[:, bass.ds(e * TILES + t, 1), :], start=(t == 0), stop=(t == TILES - 1))
                    ins.then_inc(placed, 1)

        @block.vector
        def _(dve):
            dve.memset(thr[:, :], 0)
            top = 1 << (2 * ROUNDS - 2)
            dve.memset(low_bit[:, :], float(top))
            for n in range(3):
                ins = dve.memset(bits[:, n, :], (n + 1) * top)
            ins.then_inc(dl, 1)
            dve.tensor_copy(pe_t[:, :, :], probs[:, :, :].rearrange("p t e -> p e t")).then_inc(dl, 1)
            dve.wait_ge(dl, 2)

            def wide(v):
                return v.rearrange("p (e a) -> p e a", a=1).broadcast_to([P, EXPERTS, TILES])

            three = [P, 3, EXPERTS, TILES]
            with dve.Fori(0, ROUNDS) as b:
                link = Tally(bit_link, b, 8)
                link.inc(dve.tensor_tensor(cand[:, :, :], bits[:, :, :], thr[:, :].rearrange(
                    "p (a e) -> p a e", a=1).broadcast_to([P, 3, EXPERTS]), ALU.bitwise_or))
                link.wait(dve)
                link.inc(dve.tensor_tensor(
                    flags[:, :, :, :], pe_t[:, :, :].rearrange("p (a e) t -> p a e t", a=1).broadcast_to(three),
                    cand[:, :, :].bitcast(F32).rearrange("p n (e a) -> p n e a", a=1).broadcast_to(three), ALU.is_ge))
                link.wait(dve)
                dve.tensor_reduce(counts[:, :, :], flags[:, :, :, :], AX_X, ALU.add).then_inc(part_ready, 1)
                dve.wait_ge(counted, b + 1)
                link.inc(dve.tensor_scalar(hit[:, :, :], ps_c[:, :, :], float(CAPACITY), None, ALU.is_ge))
                link.wait(dve)
                link.inc(dve.tensor_reduce(reached[:, :], hit[:, :, :].rearrange("p n e -> p e n"), AX_X, ALU.add))
                link.wait(dve)
                link.inc(dve.tensor_tensor(more_bits[:, :], reached[:, :], low_bit[:, :], ALU.mult))
                link.wait(dve)
                link.inc(dve.tensor_tensor(thr[:, :], thr[:, :], more_bits[:, :], ALU.bitwise_or))
                link.inc(dve.tensor_scalar(bits[:, :, :], bits[:, :, :], 2, None, ALU.logical_shift_right))
                link.inc(dve.tensor_scalar(low_bit[:, :], low_bit[:, :], 0.25, None, ALU.mult))
                link.wait(dve)
                link.close()
            steps = [2]

            def step(ins):
                ins.then_inc(dl, 1)
                steps[0] += 1
                dve.wait_ge(dl, steps[0])

            T = wide(thr[:, :].bitcast(F32))
            step(dve.tensor_tensor(flag[:, :, :], pe_t[:, :, :], T, ALU.is_gt))
            dve.tensor_tensor(over[:, :, :], pe_t[:, :, :], T, ALU.is_equal).then_inc(flags_ready, 1)
            dve.tensor_reduce(count[:, :], flag[:, :, :], AX_X, ALU.add).then_inc(part_ready, 1)
            dve.wait_ge(counted, ROUNDS + 1)
            step(dve.tensor_scalar(need[:, :], ps_c[:, 0, :], -1.0, float(CAPACITY), ALU.mult, ALU.add))

            def rank(n):
                dve.wait_ge(summed, n)
                step(dve.tensor_copy(tot[:, :], ps_b[:, :]))
                step(dve.tensor_tensor_scan(inc_s[:, :], carry[:, :], tot[:, :], 0.0, ALU.mult, ALU.add))
                step(dve.tensor_tensor(inc_s[:, :], inc_s[:, :], tot[:, :], ALU.subtract))
                step(dve.tensor_tensor(pos[:, :], ps_a[:, :], inc_s[:, :], ALU.add))

            dve.wait_ge(consts, 5)
            rank(1)
            step(dve.tensor_tensor(pos[:, :].rearrange("p (e t) -> p e t", e=EXPERTS),
                                   pos[:, :].rearrange("p (e t) -> p e t", e=EXPERTS), wide(need[:, :]), ALU.is_lt))
            step(dve.tensor_tensor(pos[:, :], pos[:, :], over[:, :, :].rearrange("p e t -> p (e t)"), ALU.mult))
            step(dve.tensor_tensor(chosen[:, :], pos[:, :], flag[:, :, :].rearrange("p e t -> p (e t)"), ALU.add))
            dve.sem_inc(flags_ready, 1)
            rank(2)
            step(dve.tensor_copy(pos_i[:, :], pos[:, :]))
            step(dve.tensor_scalar(hi_i[:, :], pos_i[:, :], 7, None, ALU.logical_shift_right))
            step(dve.tensor_copy(hi[:, :], hi_i[:, :]))
            step(dve.tensor_scalar(pos_i[:, :], pos_i[:, :], P - 1, None, ALU.bitwise_and))
            step(dve.tensor_copy(lo[:, :], pos_i[:, :]))
            four = [P, ET, SLOTS]
            step(dve.tensor_tensor(oh[:, :, :], hi[:, :].rearrange("p (n a) -> p n a", a=1).broadcast_to(four),
                                   iota[:, 0:SLOTS].rearrange("p (a c) -> p a c", a=1).broadcast_to(four),
                                   ALU.is_equal))
            step(dve.tensor_tensor(oh[:, :, :], oh[:, :, :],
                                   chosen[:, :].rearrange("p (n a) -> p n a", a=1).broadcast_to(four), ALU.mult))
            step(dve.tensor_scalar(rhs[:, :, 0:SLOTS], oh[:, :, :], part[:, 0:1], None, ALU.mult))
            step(dve.tensor_tensor(rhs[:, :, SLOTS:2 * SLOTS], oh[:, :, :],
                                   tile_f[:, :].rearrange("p (n a) -> p n a", a=1).broadcast_to(four), ALU.mult))
            dve.sem_inc(placed, 2)
            dve.wait_ge(wide_ready, 1)
            with dve.Fori(0, EXPERTS // 2) as i:
                for s in range(2):
                    e = i * 2 + s
                    dve.wait_ge(placed, e + 1)
                    dve.tensor_tensor(lohot[:, s, :, :], iota_w[:, :, :],
                                      lo[:, bass.ds(e * TILES, TILES)].rearrange("p (a t) -> p a t", a=1).broadcast_to(
                                          [P, P, TILES]), ALU.is_equal).then_inc(lohot_ready, 1)
            dve.wait_ge(placed, EXPERTS + 2)
            step(dve.tensor_copy(half[:, :, :], ps_i[:, :, 0:SLOTS]))
            step(dve.scalar_tensor_tensor(idx[:, :, :], ps_i[:, :, SLOTS:2 * SLOTS], float(P), half[:, :, :],
                                          ALU.mult, ALU.add))


def load_expert(sp, w, held, s, e):
    one = bass.ds(e, 1)
    for name, src in (("w1", w["W1"].rearrange("e (k p) n -> p e k n", p=P)[:, one, :, :]),
                      ("w2", w["W2"].rearrange("e (k p) n -> p e k n", p=P)[:, one, :, :]),
                      ("b1", w["b1"][:, one, :]), ("b2", w["b2"][:, one, :])):
        dst = held[name][:, s:s + 1, :, :] if name[0] == "w" else held[name][:, s:s + 1, :]
        sp.dma_start(dst, src).then_inc(held["loaded"][s], 16)


def routed_ffn(nc, keep, w, held, idx, row_dram, sum_dram):
    tag = "ro"
    with ExitStack() as ctx:
        def sb(name, shape, dt=F32):
            return ctx.enter_context(nc.sbuf_tensor(f"{tag}_{name}", shape, dt))

        def sem(name):
            return keep["semaphore"](f"{tag}_{name}")

        X, MV, ident = keep["X"], keep["MV"], keep["ident"]
        w1, w2, b1, b2, w_loaded = held["w1"], held["w2"], held["b1"], held["b2"], held["loaded"]
        row = sb("row", [P, 2, SLOTS, ROW])
        score = sb("score", [P, 2, SLOTS])
        xnT = sb("xnT", [P, KC, CAPACITY])
        hT = sb("hT", [P, HCH, CAPACITY])
        tmp = sb("tmp", [P, SLOTS, D])
        y = sb("y", [P, 2, SLOTS, D])
        tok = sb("tok", [P, 2, SLOTS], U32)
        bst = sb("bst", [P, TILES, 6])
        banks = [ctx.enter_context(nc.psum_tensor(f"{tag}_ps{b}", [P, 512], F32)) for b in range(6)]
        first = Ring(f"{tag}_first", sem, banks[0:2], ["xt0", "xt1"])
        main = Ring(f"{tag}_main", sem, banks[2:6], [f"up{c}" for c in range(HCH)] + [f"y{u}" for u in range(SLOTS)])
        gathered = [sem(f"gathered{s}") for s in range(2)]
        scattered = sem("scattered")
        tok_ready = sem("tok_ready")
        scores_out = sem("scores_out")
        pool_passed = sem("pool_passed")
        y_stored = sem("y_stored")
        y_ready = sem("y_ready")
        x_loaded = [sem(f"x_loaded{q}") for q in range(4)]
        bn_link = sem("bn_link")
        sum_v = sum_dram.rearrange("(t p) n -> p t n", p=P)
        block = ctx.enter_context(nc.Block())

        @block.sync
        def _(sp):
            with sp.Fori(1, EXPERTS // 2) as i:
                for s in range(2):
                    sp.wait_ge(y_ready, (i - 1) * 2 + s + 2)
                    load_expert(sp, w, held, s, i * 2 + s)
            sp.wait_ge(scattered, 16 * SLOTS * EXPERTS)
            for q in range(4):
                part = slice(q * TILES // 4, (q + 1) * TILES // 4)
                sp.dma_start(X[:, part, :], sum_v[:, part, :]).then_inc(x_loaded[q], 16)

        @block.gpsimd
        def _(pool):
            def gather(s, e):
                pool.tensor_copy(tok[:, s:s + 1, :], idx[:, bass.ds(e, 1), :]).then_inc(tok_ready, 1)
                await_apart(pool, tok_ready, e + 1, pool_passed)
                for c in range(SLOTS):
                    pool.indirect_dma_start(out=row[:, s, c, :], out_offset=None, in_=row_dram[:, :],
                                            in_offset=bass.IndirectOffsetOnAxis(ap=tok[:, s, c:c + 1], axis=0),
                                            ).then_inc(gathered[s], 16)

            gather(0, 0)
            def turn(i, last):
                for s in range(2):
                    e = i * 2 + s
                    if not (last and s == 1):
                        gather(1 - s, e + 1)
                    await_apart(pool, y_ready, e + 2, pool_passed)
                    for c in range(SLOTS):
                        pool.indirect_dma_start(out=sum_dram[:, :], in_=y[:, s, c, :], in_offset=None,
                                                out_offset=bass.IndirectOffsetOnAxis(ap=tok[:, s, c:c + 1], axis=0),
                                                compute_op=ALU.add).then_inc(scattered, 16)
                    await_apart(pool, scattered, (e + 1) * 16 * SLOTS, y_stored)

            with pool.Fori(0, EXPERTS // 2 - 1) as i:
                turn(i, False)
            turn(EXPERTS // 2 - 1, True)

        @block.scalar
        def _(act):
            def columns(e):
                for n in range(2):
                    first.wait_full(act, e, f"xt{n}")
                    first.take(act.activation(xnT[:, :, n * 256:(n + 1) * 256],
                                              first.bank(f"xt{n}")[:, :].rearrange("p (k n) -> p k n", k=KC),
                                              ACT.Copy), f"xt{n}")

            def turn(i, last):
                for s in range(2):
                    e = i * 2 + s
                    act.wait_ge(w_loaded[s], i * 64 + 64)
                    for c in range(HCH):
                        main.wait_full(act, e, f"up{c}")
                        main.take(act.activation(hT[:, c, :], main.bank(f"up{c}")[:, :], ACT.Gelu_apprx_tanh,
                                                 bias=b1[:, s, c:c + 1]), f"up{c}")
                    if not (last and s == 1):
                        columns(e + 1)

            columns(0)
            with act.Fori(0, EXPERTS // 2 - 1) as i:
                turn(i, False)
            turn(EXPERTS // 2 - 1, True)

        @block.tensor
        def _(pe):
            for r in (first, main):
                r.start_empty(pe)

            def columns(e, s, arrived):
                pe.wait_ge(gathered[s], arrived)
                for n in range(2):
                    first.claim(pe, e, f"xt{n}")
                    for u in (2 * n, 2 * n + 1):
                        for k in range(KC):
                            at = k * 256 + (u % 2) * P
                            ins = pe.transpose(first.bank(f"xt{n}")[:, at:at + P],
                                               row[:, s, u, k * P:(k + 1) * P], ident[:, :])
                    first.filled(ins)

            def turn(i, last):
                for s in range(2):
                    e = i * 2 + s
                    for n in range(2):
                        first.wait_taken(pe, e, f"xt{n}")
                    pe.wait_ge(w_loaded[s], i * 64 + 64)
                    for c in range(HCH):
                        main.claim(pe, e, f"up{c}")
                        for k in range(KC):
                            ins = pe.matmul(main.bank(f"up{c}")[:, :], w1[:, s, k, c * P:(c + 1) * P], xnT[:, k, :],
                                            start=(k == 0), stop=(k == KC - 1))
                        main.filled(ins)
                    for u in range(SLOTS):
                        main.claim(pe, e, f"y{u}")
                        for c in range(HCH):
                            if u == 0:
                                main.wait_taken(pe, e, f"up{c}")
                            ins = pe.matmul(main.bank(f"y{u}")[:, 0:D], hT[:, c, u * P:(u + 1) * P], w2[:, s, c, :],
                                            start=(c == 0), stop=(c == HCH - 1))
                        main.filled(ins)
                        if u == 1 and not (last and s == 1):
                            columns(e + 1, 1 - s, (i + s + 1) * 16 * SLOTS)

            columns(0, 0, 16 * SLOTS)
            with pe.Fori(0, EXPERTS // 2 - 1) as i:
                turn(i, False)
            turn(EXPERTS // 2 - 1, True)

        @block.vector
        def _(dve):
            dve.sem_inc(scores_out, 1)
            dve.sem_inc(y_ready, 1)
            dve.sem_inc(y_stored, 2)
            with dve.Fori(0, EXPERTS // 2) as i:
                for s in range(2):
                    e = i * 2 + s
                    dve.wait_ge(gathered[s], (i + 1) * 16 * SLOTS)
                    dve.tensor_scalar(score[:, s, :].rearrange("p (c a) -> p c a", a=1),
                                      row[:, s, :, bass.ds(D + e, 1)], 1.0, None, ALU.mult).then_inc(scores_out, 1)
                    dve.wait_ge(w_loaded[s], i * 64 + 64)
                    dve.wait_ge(y_ready, e + 1)
                    dve.wait_ge(y_stored, e + 1)
                    for u in range(SLOTS):
                        main.wait_full(dve, e, f"y{u}")
                        main.take(dve.tensor_tensor(tmp[:, u, :], main.bank(f"y{u}")[:, 0:D], b2[:, s, :], ALU.add),
                                  f"y{u}")
                    dve.wait_ge(scores_out, e + 2)
                    for u in range(SLOTS):
                        main.wait_taken(dve, e, f"y{u}")
                        ins = dve.tensor_scalar(y[:, s, u, :], tmp[:, u, :], score[:, s, u:u + 1], None, ALU.mult)
                    ins.then_inc(y_ready, 1)
            for t in range(TILES):
                if t % (TILES // 4) == 0:
                    dve.wait_ge(x_loaded[t // (TILES // 4)], 16)
                ins = dve.bn_stats(bst[:, t, :], X[:, t, :])
            ins.then_inc(bn_link, 1)
            dve.wait_ge(bn_link, 1)
            for t in range(TILES):
                dve.bn_aggr(MV[:, t, :], bst[:, t, :])


INNER = 1024
ROUND = 12582912.0


def bit_ffn(nc, keep, w, following):
    tag = "bf"
    with ExitStack() as ctx:
        def sb(name, shape, dt=F32):
            return ctx.enter_context(nc.sbuf_tensor(f"{tag}_{name}", shape, dt))

        def sem(name):
            return keep["semaphore"](f"{tag}_{name}")

        X, MV = keep["X"], keep["MV"]
        names = ("gate", "up", "down")
        raw = {n: w.at[n] for n in names}
        wb = {n: sb("wb_" + n, [P, KC * INNER], BF16) for n in names}
        wg = wb["gate"][:, :].rearrange("p (k n) -> p k n", k=KC)
        wu = wb["up"][:, :].rearrange("p (k n) -> p k n", k=KC)
        wd = wb["down"][:, :].rearrange("p (k n) -> p k n", k=INNER // P)
        ones = sb("ones", [P, P])
        identb = sb("identb", [P, P], BF16)
        neg_round = sb("neg_round", [P, 1])
        asum = sb("asum", [P, 3])
        wmean = sb("wmean", [P, 3])
        wscale = sb("wscale", [P, 3])
        wq127 = sb("wq127", [P, 3])
        rstd = sb("rstd", [P, TILES])
        xn = sb("xn", [P, D])
        xq = sb("xq", [P, D], BF16)
        xqT = sb("xqT", [P, KC, P], BF16)
        amx = sb("amx", [P, 2, 2])
        asc = sb("asc", [P, 2, 2])
        dq = sb("dq", [P, 2, 3])
        gt = sb("gt", [P, 2, INNER])
        h = sb("h", [P, INNER])
        hq = sb("hq", [P, INNER], BF16)
        hqT = sb("hqT", [P, INNER // P, P], BF16)
        new = sb("new", [P, D])
        bst = sb("bst", [P, 6])
        mv = sb("mv", [P, 2])
        banks = [ctx.enter_context(nc.psum_tensor(f"{tag}_ps{b}", [P, 512], F32)) for b in range(7)]
        ps_w = ctx.enter_context(nc.psum_tensor(f"{tag}_ps_w", [P, 3], F32))
        gu = Ring(f"{tag}_gu", sem, banks[0:4], ["g0", "g1", "u0", "u1"])
        xt = Ring(f"{tag}_xt", sem, banks[4:5], ["xt"])
        ht = Ring(f"{tag}_ht", sem, banks[5:6], ["ht"])
        ys = Ring(f"{tag}_ys", sem, banks[6:7], ["y"])
        consts = sem("consts")
        rstd_sq = sem("rstd_sq")
        sums_ready = sem("sums_ready")
        summed = sem("summed")
        setup = sem("setup")
        xq_ready = sem("xq_ready")
        dq_ready = sem("dq_ready")
        h_ready = sem("h_ready")
        hq_ready = sem("hq_ready")
        x_link = sem("x_link")
        h_link = sem("h_link")
        row_link = sem("row_link")
        block = ctx.enter_context(nc.Block())

        @block.sync
        def _(sp):
            following.load(sp)

        @block.gpsimd
        def _(pool):
            pool.memset(ones[:, :], 1.0).then_inc(consts, 1)
            pool.memset(neg_round[:, :], -ROUND).then_inc(consts, 1)
            pool.tensor_copy(identb[:, :], keep["ident"][:, :]).then_inc(consts, 1)

        @block.scalar
        def _(act):
            def x_columns(t):
                xt.wait_full(act, t, "xt")
                xt.take(act.activation(xqT[:, :, :], xt.bank("xt")[:, :].bitcast(BF16)[:, 0:D].rearrange(
                    "p (k n) -> p k n", k=KC), ACT.Copy), "xt")

            def gates(t, s):
                act.wait_ge(dq_ready, t + 1)
                for n in range(2):
                    gu.wait_full(act, t, f"g{n}")
                    gu.take(act.activation(gt[:, s, n * 512:(n + 1) * 512], gu.bank(f"g{n}")[:, :], ACT.Silu,
                                           scale=dq[:, s, 0:1]), f"g{n}")

            def slot(t, s, after):
                if after is None or after >= 1:
                    gates(t + 1, 1 - s)
                act.wait_ge(h_ready, t + 1)
                act.activation(hq[:, :], h[:, :], ACT.Identity, bias=neg_round[:, 0:1]).then_inc(hq_ready, 1)
                ht.wait_full(act, t, "ht")
                ht.take(act.activation(hqT[:, :, :], ht.bank("ht")[:, :].bitcast(BF16).rearrange(
                    "p (k n) -> p k n", n=P), ACT.Copy), "ht")
                if after is None or after >= 2:
                    x_columns(t + 2)

            layer_norm_scale(act, None, keep, rstd, rstd_sq, None)
            act.wait_ge(consts, 3)
            x_columns(0)
            gates(0, 0)
            x_columns(1)
            slots(act, slot)

        @block.tensor
        def _(pe):
            for r in (gu, xt, ht, ys):
                r.start_empty(pe)
            pe.wait_ge(consts, 3)
            pe.wait_ge(sums_ready, 3)
            pe.matmul(ps_w[:, :], ones[:, :], asum[:, :], start=True, stop=True).then_inc(summed, 1)

            def x_columns(t):
                xt.claim(pe, t, "xt")
                pe.wait_ge(xq_ready, t + 1)
                for k in range(KC):
                    ins = pe.transpose(xt.bank("xt")[:, :].bitcast(BF16)[:, k * P:(k + 1) * P],
                                       xq[:, k * P:(k + 1) * P], identb[:, :])
                xt.filled(ins)

            def gates_and_ups(t):
                xt.wait_taken(pe, t, "xt")
                for a, wt in (("g", wg), ("u", wu)):
                    for n in range(2):
                        gu.claim(pe, t, f"{a}{n}")
                        for k in range(KC):
                            ins = pe.matmul(gu.bank(f"{a}{n}")[:, :], xqT[:, k, :], wt[:, k, n * 512:(n + 1) * 512],
                                            start=(k == 0), stop=(k == KC - 1))
                        gu.filled(ins)

            def slot(t, s, after):
                if after is None or after >= 1:
                    gates_and_ups(t + 1)
                ht.claim(pe, t, "ht")
                pe.wait_ge(hq_ready, t + 1)
                for k in range(INNER // P):
                    ins = pe.transpose(ht.bank("ht")[:, :].bitcast(BF16)[:, k * P:(k + 1) * P],
                                       hq[:, k * P:(k + 1) * P], identb[:, :])
                ht.filled(ins)
                if after is None or after >= 2:
                    x_columns(t + 2)
                ys.claim(pe, t, "y")
                ht.wait_taken(pe, t, "ht")
                for k in range(INNER // P):
                    ins = pe.matmul(ys.bank("y")[:, 0:D], hqT[:, k, :], wd[:, k, :], start=(k == 0),
                                    stop=(k == INNER // P - 1))
                ys.filled(ins)

            x_columns(0)
            gates_and_ups(0)
            x_columns(1)
            slots(pe, slot)

        @block.vector
        def _(dve):
            layer_norm_scale(None, dve, keep, rstd, rstd_sq, setup)
            done = [1]

            def step(ins):
                ins.then_inc(setup, 1)
                done[0] += 1
                dve.wait_ge(setup, done[0])

            w.wait(dve)
            for n in range(3):
                dve.tensor_reduce(asum[:, n:n + 1], raw[names[n]][:, :], AX_X, ALU.add,
                                  apply_absolute_value=True).then_inc(sums_ready, 1)
            dve.wait_ge(summed, 1)
            step(dve.tensor_scalar(wmean[:, :], ps_w[:, :], 1.0 / (D * INNER), 1e-5, ALU.mult, ALU.max))
            step(dve.reciprocal(wscale[:, :], wmean[:, :]))
            step(dve.tensor_scalar(wq127[:, :], wmean[:, :], 1.0 / 127.0, None, ALU.mult))
            for n in range(3):
                r = raw[names[n]]
                step(dve.tensor_scalar(r[:, :], r[:, :], wscale[:, n:n + 1], ROUND, ALU.mult, ALU.add))
                step(dve.tensor_scalar(r[:, :], r[:, :], ROUND, 1.0, ALU.subtract, ALU.min))
                step(dve.tensor_scalar(wb[names[n]][:, :], r[:, :], -1.0, None, ALU.max))

            def norm(t):
                return dve.tensor_scalar(xn[:, :].rearrange("p (a n) -> p a n", a=1), X[:, bass.ds(t, 1), :],
                                         MV[:, bass.ds(t, 1), 0], rstd[:, bass.ds(t, 1)], ALU.subtract, ALU.mult)

            def largest(src, s, a):
                return dve.tensor_reduce(amx[:, s, a:a + 1], src, AX_X, ALU.max, apply_absolute_value=True)

            def factor(s, at, inc, wait):
                inc(dve.tensor_scalar(amx[:, s, at], amx[:, s, at], 1e-5, None, ALU.max))
                wait()
                inc(dve.reciprocal(asc[:, s, at], amx[:, s, at]))
                wait()
                inc(dve.tensor_scalar(asc[:, s, at], asc[:, s, at], 127.0, None, ALU.mult))
                wait()

            def scaled(v, s, a):
                return dve.tensor_scalar(v, v, asc[:, s, a:a + 1], -128.0, ALU.mult, ALU.max)

            def rounded(v):
                return dve.tensor_scalar(v, v, 127.0, ROUND, ALU.min, ALU.add)

            def x_integers():
                return dve.tensor_scalar(xq[:, :], xn[:, :], ROUND, None, ALU.subtract)

            def scales_of_x(s):
                dve.tensor_scalar(dq[:, s, 0:2], wq127[:, 0:2], amx[:, s, 0:1], None, ALU.mult).then_inc(dq_ready, 1)

            for t in range(2):
                if t:
                    dve.wait_ge(xq_ready, t)
                step(norm(t))
                step(largest(xn[:, :], t, 0))
                factor(t, slice(0, 1), lambda ins: ins.then_inc(setup, 1), lambda: (
                    done.__setitem__(0, done[0] + 1), dve.wait_ge(setup, done[0])))
                step(scaled(xn[:, :], t, 0))
                step(rounded(xn[:, :]))
                if t:
                    xt.wait_full(dve, t - 1, "xt")
                x_integers().then_inc(xq_ready, 1)
                scales_of_x(t)

            def slot(t, s, after):
                more = after is None or after >= 2
                x_tally = Tally(x_link, t, 4)
                h_tally = Tally(h_link, t, 6)
                for n in range(2):
                    gu.wait_taken(dve, t, f"g{n}")
                    gu.wait_full(dve, t, f"u{n}")
                    if n == 0 and not at_start(t, 1):
                        dve.wait_ge(hq_ready, t)
                    gu.take(dve.scalar_tensor_tensor(h[:, n * 512:(n + 1) * 512], gu.bank(f"u{n}")[:, :],
                                                     dq[:, s, 1:2], gt[:, s, n * 512:(n + 1) * 512], ALU.mult,
                                                     ALU.mult), f"u{n}")
                if more:
                    dve.wait_ge(xq_ready, t + 2)
                    x_tally.inc(norm(t + 2))
                    x_tally.wait(dve)
                    x_tally.inc(largest(xn[:, :], s, 0))
                for n in range(2):
                    gu.wait_taken(dve, t, f"u{n}")
                h_tally.inc(largest(h[:, :], s, 1))
                if more:
                    x_tally.wait(dve)
                h_tally.wait(dve)
                factor(s, slice(0, 2), h_tally.inc, lambda: h_tally.wait(dve))
                if more:
                    x_tally.inc(scaled(xn[:, :], s, 0))
                h_tally.inc(scaled(h[:, :], s, 1))
                if more:
                    x_tally.wait(dve)
                    x_tally.inc(rounded(xn[:, :]))
                h_tally.wait(dve)
                rounded(h[:, :]).then_inc(h_ready, 1)
                if more:
                    x_tally.wait(dve)
                    xt.wait_full(dve, t + 1, "xt")
                    x_integers().then_inc(xq_ready, 1)
                    scales_of_x(s)
                    x_tally.close()
                h_tally.inc(dve.tensor_scalar(dq[:, s, 2:3], wq127[:, 2:3], amx[:, s, 1:2], None, ALU.mult))
                h_tally.close()
                if not at_start(t, 1):
                    finish(t - 1, 1 - s)

            def finish(t, s):
                link = Tally(row_link, t, 2)
                ys.wait_full(dve, t, "y")
                ys.take(dve.scalar_tensor_tensor(new[:, :].rearrange("p (a n) -> p a n", a=1),
                                                 ys.bank("y")[:, 0:D].rearrange("p (a n) -> p a n", a=1),
                                                 dq[:, s, 2:3], X[:, bass.ds(t, 1), :], ALU.mult, ALU.add), "y")
                ys.wait_taken(dve, t, "y")
                finish_rows(dve, keep, link, t, new, bst, mv)
                link.close()

            slots(dve, slot)
            dve.wait_ge(h_link, 6 * TILES)
            finish(TILES - 1, (TILES - 1) % 2)


WINDOW = 16.0
DEV_POW = 128.0
MASKED = 1e9


def windowed_attention(nc, keep, w, ctxT, ctx_n, following):
    tag = "wa"
    with ExitStack() as ctx:
        def sb(name, shape, dt=F32):
            return ctx.enter_context(nc.sbuf_tensor(f"{tag}_{name}", shape, dt))

        def sem(name):
            return keep["semaphore"](f"{tag}_{name}")

        X, MV, ident = keep["X"], keep["MV"], keep["ident"]
        wa, wc, pt, len_i = (w.at[n] for n in ("wa", "wc", "pt", "len"))
        first_key = sb("first_key", [P, TILES])
        last = sb("last", [P, TILES])
        neg_pt = sb("neg_pt", [P, TILES])
        iota_i = sb("iota_i", [P, P], I32)
        iota = sb("iota", [P, P])
        rstd = sb("rstd", [P, TILES])
        ctx_t = sb("ctx_t", [P, KC, GT])
        ctx_r = sb("ctx_r", [P, G, D])
        xn = sb("xn", [P, G, D])
        xnT = sb("xnT", [P, 2, KC, GT])
        aT = sb("aT", [P, KC, GT])
        inside = sb("inside", [P, G, P])
        low = sb("low", [P, G, P])
        gauss = sb("gauss", [P, G, P])
        sc = sb("sc", [P, G, P])
        mx = sb("mx", [P, G])
        den = sb("den", [P, G])
        al = sb("al", [P, G, P])
        alT = sb("alT", [P, G, P])
        cxT = sb("cxT", [P, G, KC, P])
        th = sb("th", [P, 2, G, D])
        new = sb("new", [P, D])
        bst = sb("bst", [P, 6])
        mv = sb("mv", [P, 2])
        banks = [ctx.enter_context(nc.psum_tensor(f"{tag}_ps{b}", [P, 512], F32)) for b in range(8)]
        first = Ring(f"{tag}_first", sem, banks[0:4], ["xt0", "xt1", "a0", "a1"] + [f"sc{u}" for u in range(G)])
        second = Ring(f"{tag}_second", sem, banks[4:8], [f"{n}{u}" for n in ("al", "cx", "y") for u in range(G)])
        ctx_t_loaded = sem("ctx_t_loaded")
        ctx_r_loaded = sem("ctx_r_loaded")
        pool_link = sem("pool_link")
        consts = sem("consts")
        rstd_sq = sem("rstd_sq")
        setup = sem("setup")
        xn_ready = sem("xn_ready")
        gauss_sq = sem("gauss_sq")
        gauss_ready = sem("gauss_ready")
        mx_ready = sem("mx_ready")
        exp_ready = sem("exp_ready")
        al_ready = sem("al_ready")
        mask_link = sem("mask_link")
        weight_link = sem("weight_link")
        row_link = sem("row_link")
        ctxT_v = ctxT.rearrange("(k p) n -> p k n", p=P)
        ctx_v = ctx_n.rearrange("(t p) d -> p t d", p=P)
        block = ctx.enter_context(nc.Block())

        @block.sync
        def _(sp):
            sp.dma_start(ctx_t[:, :, :], ctxT_v[:, :, 0:GT]).then_inc(ctx_t_loaded, 16)
            sp.dma_start(ctx_r[:, :, :], ctx_v[:, 0:G, :]).then_inc(ctx_r_loaded, 16)
            following.load(sp)
            with sp.Fori(1, GROUPS) as g:
                first.wait_full(sp, g - 1, f"sc{G - 1}")
                sp.dma_start(ctx_t[:, :, :], ctxT_v[:, :, bass.ds(g * GT, GT)]).then_inc(ctx_t_loaded, 16)
                second.wait_full(sp, g - 1, f"cx{G - 1}")
                sp.dma_start(ctx_r[:, :, :], ctx_v[:, bass.ds(g * G, G), :]).then_inc(ctx_r_loaded, 16)

        @block.gpsimd
        def _(pool):
            pool.iota(iota_i[:, :], [[1, P]], base=0, channel_multiplier=0).then_inc(pool_link, 1)
            pool.wait_ge(pool_link, 1)
            pool.tensor_copy(iota[:, :], iota_i[:, :]).then_inc(consts, 1)

        @block.scalar
        def _(act):
            layer_norm_scale(act, None, keep, rstd, rstd_sq, None)
            act.wait_ge(consts, 1)
            act.wait_ge(setup, 6)

            def columns(g, s):
                for n in range(2):
                    first.wait_full(act, g, f"xt{n}")
                    first.take(act.activation(xnT[:, s, :, n * 256:(n + 1) * 256],
                                              first.bank(f"xt{n}")[:, :].rearrange("p (k n) -> p k n", k=KC),
                                              ACT.Copy), f"xt{n}")

            def distances(g):
                for u in range(G):
                    act.activation(gauss[:, u, :], iota[:, :], ACT.Square,
                                   bias=neg_pt[:, bass.ds(g * G + u, 1)]).then_inc(gauss_sq, 1)
                act.wait_ge(gauss_sq, g * G + G)
                act.activation(gauss[:, :, :], gauss[:, :, :], ACT.Exp, scale=-1.0 / DEV_POW).then_inc(gauss_ready, 1)

            def queries(g):
                for k in range(KC):
                    first.wait_full(act, g, f"a{k}")
                    first.take(act.activation(aT[:, k, :], first.bank(f"a{k}")[:, :], ACT.Copy), f"a{k}")

            def exps(g):
                for u in range(G):
                    act.wait_ge(mx_ready, g * G + u + 1)
                    act.activation(sc[:, u, :], sc[:, u, :], ACT.Exp, bias=mx[:, u:u + 1],
                                   accum_out=den[:, u:u + 1]).then_inc(exp_ready, 1)

            def turn(g, s, more):
                for u in range(G):
                    second.wait_full(act, g, f"al{u}")
                    second.take(act.activation(alT[:, u, :], second.bank(f"al{u}")[:, 0:P], ACT.Copy), f"al{u}")
                if more:
                    columns(g + 1, 1 - s)
                for u in range(G):
                    second.wait_full(act, g, f"cx{u}")
                    second.take(act.activation(cxT[:, u, :, :], second.bank(f"cx{u}")[:, 0:D].rearrange(
                        "p (k n) -> p k n", k=KC), ACT.Copy), f"cx{u}")
                if more:
                    queries(g + 1)
                for u in range(G):
                    second.wait_full(act, g, f"y{u}")
                    second.take(act.activation(th[:, s, u, :], second.bank(f"y{u}")[:, 0:D], ACT.Tanh), f"y{u}")
                if more:
                    distances(g + 1)
                    exps(g + 1)

            columns(0, 0)
            distances(0)
            queries(0)
            exps(0)
            turns(act, turn)

        @block.tensor
        def _(pe):
            for r in (first, second):
                r.start_empty(pe)
            w.wait(pe)

            def columns(g):
                for n in range(2):
                    first.claim(pe, g, f"xt{n}")
                    for u in (2 * n, 2 * n + 1):
                        pe.wait_ge(xn_ready, g * G + u + 1)
                        for k in range(KC):
                            at = k * 256 + (u % 2) * P
                            ins = pe.transpose(first.bank(f"xt{n}")[:, at:at + P], xn[:, u, k * P:(k + 1) * P],
                                               ident[:, :])
                    first.filled(ins)

            def queries(g, s):
                for n in range(2):
                    first.wait_taken(pe, g, f"xt{n}")
                for c in range(KC):
                    first.claim(pe, g, f"a{c}")
                    for k in range(KC):
                        ins = pe.matmul(first.bank(f"a{c}")[:, :], wa[:, k, c * P:(c + 1) * P], xnT[:, s, k, :],
                                        start=(k == 0), stop=(k == KC - 1))
                    first.filled(ins)

            def scores(g):
                pe.wait_ge(ctx_t_loaded, g * 16 + 16)
                for c in range(KC):
                    first.wait_taken(pe, g, f"a{c}")
                for u in range(G):
                    first.claim(pe, g, f"sc{u}")
                    for k in range(KC):
                        ins = pe.matmul(first.bank(f"sc{u}")[:, 0:P], aT[:, k, u * P:(u + 1) * P],
                                        ctx_t[:, k, u * P:(u + 1) * P], start=(k == 0), stop=(k == KC - 1))
                    first.filled(ins)

            def turn(g, s, more):
                for u in range(G):
                    second.claim(pe, g, f"al{u}")
                    pe.wait_ge(al_ready, g * G + u + 1)
                    second.filled(pe.transpose(second.bank(f"al{u}")[:, 0:P], al[:, u, :], ident[:, :]))
                if more:
                    columns(g + 1)
                pe.wait_ge(ctx_r_loaded, g * 16 + 16)
                for u in range(G):
                    second.claim(pe, g, f"cx{u}")
                    second.wait_taken(pe, g, f"al{u}")
                    for c in range(KC):
                        ins = pe.matmul(second.bank(f"cx{u}")[:, c * P:(c + 1) * P], ctx_r[:, u, c * P:(c + 1) * P],
                                        alT[:, u, :], start=True, stop=True)
                    second.filled(ins)
                if more:
                    queries(g + 1, 1 - s)
                for u in range(G):
                    second.claim(pe, g, f"y{u}")
                    second.wait_taken(pe, g, f"cx{u}")
                    for k in range(2 * KC):
                        lhs = cxT[:, u, k, :] if k < KC else xnT[:, s, k - KC, u * P:(u + 1) * P]
                        ins = pe.matmul(second.bank(f"y{u}")[:, 0:D], lhs, wc[:, k, :], start=(k == 0),
                                        stop=(k == 2 * KC - 1))
                    second.filled(ins)
                    if u == 1 and more:
                        scores(g + 1)

            columns(0)
            queries(0, 0)
            scores(0)
            turns(pe, turn)

        @block.vector
        def _(dve):
            layer_norm_scale(None, dve, keep, rstd, rstd_sq, setup)
            w.wait(dve)
            dve.tensor_copy(last[:, :], len_i[:, :]).then_inc(setup, 1)
            dve.tensor_scalar(first_key[:, :], pt[:, :], WINDOW, 0.0, ALU.subtract, ALU.max).then_inc(setup, 1)
            dve.tensor_scalar(neg_pt[:, :], pt[:, :], -1.0, None, ALU.mult).then_inc(setup, 1)
            dve.wait_ge(setup, 4)
            dve.scalar_tensor_tensor(last[:, :], pt[:, :], WINDOW, last[:, :], ALU.add, ALU.min).then_inc(setup, 1)
            dve.memset(mv[:, :], 0.0).then_inc(setup, 1)
            dve.wait_ge(setup, 6)
            dve.wait_ge(consts, 1)

            def norm(g):
                if not (isinstance(g, int) and g == 0):
                    first.wait_full(dve, g - 1, "xt1")
                for u in range(G):
                    t = g * G + u
                    dve.tensor_scalar(xn[:, u:u + 1, :], X[:, bass.ds(t, 1), :], MV[:, bass.ds(t, 1), 0],
                                      rstd[:, bass.ds(t, 1)], ALU.subtract, ALU.mult).then_inc(xn_ready, 1)

            def masks(g):
                link = Tally(mask_link, g, 3)
                for u in range(G):
                    t = g * G + u
                    ins = dve.tensor_scalar(low[:, u, :], iota[:, :], first_key[:, bass.ds(t, 1)], None, ALU.is_ge)
                link.inc(ins)
                link.wait(dve)
                for u in range(G):
                    t = g * G + u
                    ins = dve.scalar_tensor_tensor(inside[:, u, :], iota[:, :], last[:, bass.ds(t, 1)], low[:, u, :],
                                                   ALU.is_le, ALU.mult)
                link.inc(ins)
                link.wait(dve)
                link.inc(dve.tensor_scalar(low[:, :, :], inside[:, :, :], MASKED, MASKED, ALU.mult, ALU.subtract))
                link.wait(dve)
                link.close()

            def weights(g):
                link = Tally(weight_link, g, 2 + G)
                for u in range(G):
                    first.wait_full(dve, g, f"sc{u}")
                    first.take(dve.tensor_tensor(sc[:, u, :], first.bank(f"sc{u}")[:, 0:P], inside[:, u, :],
                                                 ALU.mult), f"sc{u}")
                for u in range(G):
                    first.wait_taken(dve, g, f"sc{u}")
                link.inc(dve.tensor_tensor(sc[:, :, :], sc[:, :, :], low[:, :, :], ALU.add))
                link.wait(dve)
                link.inc(dve.tensor_reduce(mx[:, :], sc[:, :, :], AX_X, ALU.max))
                link.wait(dve)
                dve.tensor_scalar(mx[:, :], mx[:, :], -1.0, None, ALU.mult).then_inc(mx_ready, G)
                dve.wait_ge(gauss_ready, g + 1)
                for u in range(G):
                    dve.wait_ge(exp_ready, g * G + u + 1)
                    link.inc(dve.reciprocal(den[:, u:u + 1], den[:, u:u + 1]))
                for u in range(G):
                    if u == 0:
                        link.wait(dve)
                    dve.scalar_tensor_tensor(al[:, u, :], sc[:, u, :], den[:, u:u + 1], gauss[:, u, :],
                                             ALU.mult, ALU.mult).then_inc(al_ready, 1)
                link.close()

            def turn(g, s, more):
                ahead = not (isinstance(g, int) and g + 2 >= GROUPS)
                rows = Tally(row_link, g, 3 * G)
                for u in range(G):
                    t = g * G + u
                    second.wait_taken(dve, g, f"y{u}")
                    rows.inc(dve.tensor_tensor(new[:, :].rearrange("p (a n) -> p a n", a=1), th[:, s, u:u + 1, :],
                                               X[:, bass.ds(t, 1), :], ALU.add))
                    finish_rows(dve, keep, rows, t, new, bst, mv)
                    if u == 1 and more:
                        weights(g + 1)
                        if ahead:
                            norm(g + 2)
                rows.close()
                if ahead:
                    masks(g + 2)

            norm(0)
            masks(0)
            weights(0)
            norm(1)
            masks(1)
            turns(dve, turn)


BN_EPS = 1e-5
PK_HEADS = 8
PK_KEYS = 64
PK_TOP = 8
PK_DIM = 128
PK_EXPERTS = PK_KEYS * PK_KEYS
ECH = PK_EXPERTS // P
PICKS = PK_HEADS * PK_TOP
TB = 16
LO_SCALE = 4096.0


def product_key_experts(nc, keep, w, experts_w):
    tag = "pk"
    with ExitStack() as ctx:
        def sb(name, shape, dt=F32):
            return ctx.enter_context(nc.sbuf_tensor(f"{tag}_{name}", shape, dt))

        def sem(name):
            return keep["semaphore"](f"{tag}_{name}")

        X, MV, ident = keep["X"], keep["MV"], keep["ident"]
        NT = sb("NT", [P, KC, TOKENS])
        wm = sb("wm", [P, KC, 2 * PK_HEADS * PK_KEYS])
        bn = sb("bn", [P, KC, 2])
        rstd = sb("rstd", [P, TILES])
        with ExitStack() as c2:
            def sb2(name, shape, dt=F32):
                return c2.enter_context(nc.sbuf_tensor(f"{tag}1_{name}", shape, dt))

            def sem2(name):
                return keep["semaphore"](f"{tag}_{name}")

            wq, keys, gamma, beta = (w.at[n] for n in ("wq", "keys", "gamma", "beta"))
            xn = sb2("xn", [P, G, D])
            nT = sb2("nT", [P, KC, GT])
            bst = sb2("bst", [P, KC, GROUPS, 6])
            mvb = sb2("mvb", [P, KC, 2])
            sd = sb2("sd", [P, KC])
            banks = [c2.enter_context(nc.psum_tensor(f"{tag}_p1_{b}", [P, 512], F32)) for b in range(2)]
            ps_w = [c2.enter_context(nc.psum_tensor(f"{tag}_pw_{b}", [P, 512], F32)) for b in range(4)]
            ring = Ring(f"{tag}_ring1", sem2, banks, ["xt0", "xt1"])
            folded = sem2("folded")
            rstd_sq = sem2("rstd_sq")
            setup = sem2("setup1")
            xn_ready = sem2("xn1_ready")
            stats = sem2("stats")
            sd_sq = sem2("sd_sq")
            block = c2.enter_context(nc.Block())

            @block.sync
            def _(sp):
                experts_w.load(sp)

            @block.scalar
            def _(act):
                layer_norm_scale(act, None, keep, rstd, rstd_sq, None)
                act.wait_ge(folded, 1)
                for k in range(KC):
                    for n in range(2):
                        act.activation(wm[:, k, n * 512:(n + 1) * 512], ps_w[2 * k + n][:, :], ACT.Copy)
                with act.Fori(0, GROUPS) as g:
                    for n in range(2):
                        ring.wait_full(act, g, f"xt{n}")
                        ring.take(act.activation(NT[:, :, bass.ds(g * GT + n * 256, 256)],
                                                 ring.bank(f"xt{n}")[:, :].rearrange("p (k n) -> p k n", k=KC),
                                                 ACT.Copy), f"xt{n}")
                act.wait_ge(stats, 2)
                act.activation(sd[:, :], mvb[:, :, 1], ACT.Sqrt, bias=keep["eps"][:, 0:1]).then_inc(sd_sq, 1)

            @block.tensor
            def _(pe):
                ring.start_empty(pe)
                w.wait(pe)
                for k in range(KC):
                    for c in range(2 * PK_HEADS):
                        at = (c % PK_HEADS) * PK_KEYS
                        ins = pe.matmul(ps_w[2 * k + c // PK_HEADS][:, at:at + PK_KEYS], wq[:, c, k * P:(k + 1) * P],
                                        keys[:, c, :], start=True, stop=True)
                ins.then_inc(folded, 1)
                with pe.Fori(0, GROUPS) as g:
                    for n in range(2):
                        ring.claim(pe, g, f"xt{n}")
                        for u in (2 * n, 2 * n + 1):
                            pe.wait_ge(xn_ready, g * G + u + 1)
                            for k in range(KC):
                                at = k * 256 + (u % 2) * P
                                ins = pe.transpose(ring.bank(f"xt{n}")[:, at:at + P], xn[:, u, k * P:(k + 1) * P],
                                                   ident[:, :])
                        ring.filled(ins)

            @block.vector
            def _(dve):
                layer_norm_scale(None, dve, keep, rstd, rstd_sq, setup)
                for g in range(GROUPS):
                    for u in range(G):
                        t = g * G + u
                        if g:
                            ring.wait_full(dve, g - 1, f"xt{u // 2}")
                        dve.tensor_scalar(xn[:, u, :], X[:, t, :], MV[:, t, 0:1], rstd[:, t:t + 1], ALU.subtract,
                                          ALU.mult).then_inc(xn_ready, 1)
                    if g:
                        for n in range(2):
                            ring.wait_taken(dve, g - 1, f"xt{n}")
                        for k in range(KC):
                            dve.bn_stats(bst[:, k, g - 1, :], NT[:, k, (g - 1) * GT:g * GT])
                for n in range(2):
                    ring.wait_taken(dve, GROUPS - 1, f"xt{n}")
                for k in range(KC):
                    ins = dve.bn_stats(bst[:, k, GROUPS - 1, :], NT[:, k, (GROUPS - 1) * GT:])
                ins.then_inc(setup, 1)
                dve.wait_ge(setup, 2)
                for k in range(KC):
                    dve.bn_aggr(mvb[:, k, :], bst[:, k, :, :].rearrange("p g s -> p (g s)")).then_inc(stats, 1)
                dve.wait_ge(sd_sq, 1)
                w.wait(dve)
                dve.reciprocal(sd[:, :], sd[:, :]).then_inc(setup, 1)
                dve.wait_ge(setup, 3)
                dve.tensor_tensor(bn[:, :, 0], sd[:, :], gamma[:, :], ALU.mult).then_inc(setup, 1)
                dve.wait_ge(setup, 4)
                dve.tensor_tensor(sd[:, :], mvb[:, :, 0], bn[:, :, 0], ALU.mult).then_inc(setup, 1)
                dve.wait_ge(setup, 5)
                dve.tensor_tensor(bn[:, :, 1], beta[:, :], sd[:, :], ALU.subtract)

        w.free()
        downT, up = experts_w.at["downT"], experts_w.at["up"]
        iota_i = sb("iota_i", [P, P], I32)
        iota = sb("iota", [P, P])
        iota_h = sb("iota_h", [P, P], F16)
        iota_w = sb("iota_w", [P, P, TB], F16)
        nt = sb("nt", [P, 2, KC, P])
        xb = sb("xb", [P, 2, KC, P])
        best = sb("best", [P, 2, PK_HEADS, PK_TOP])
        best_i = sb("best_i", [P, 2, PK_HEADS, PK_TOP], U32)
        best_f = sb("best_f", [P, 2, PK_HEADS, PK_TOP])
        pairs = sb("pairs", [P, PK_HEADS, PK_TOP * PK_TOP])
        score = sb("score", [P, PK_HEADS, PK_TOP])
        pick = sb("pick", [P, PK_HEADS, PK_TOP], U32)
        half_i = sb("half_i", [P, 2, PICKS], U32)
        half_f = sb("half_f", [P, 2, PICKS])
        hot = sb("hot", [P, 2, PICKS, PK_TOP])
        key = sb("key", [P, 2, PICKS])
        eid = sb("eid", [P, PICKS])
        eid_i = sb("eid_i", [P, PICKS], I32)
        ehl_i = sb("ehl_i", [P, 2, PICKS], I32)
        sig = sb("sig", [P, PICKS])
        rows = sb("rows", [P, 3, 2, PICKS], F16)
        identh = sb("identh", [P, P], F16)
        cols = sb("cols", [P, 3, P], F16)
        lohot = sb("lohot", [P, 2, P, TB], F16)
        hihot = sb("hihot", [P, 2, ECH, TB], F16)
        hisig = sb("hisig", [P, 2, ECH, TB], F16)
        act_h = sb("act_h", [P, 2, ECH, P])
        new = sb("new", [P, D])
        bst = sb("bst", [P, 6])
        mv = sb("mv", [P, 2])
        NB = P // TB

        def bank(n):
            return ctx.enter_context(nc.psum_tensor(f"{tag}_ps{n}", [P, 512], F32))

        sims = Ring(f"{tag}_sims", sem, [bank(0), bank(1)], ["s0", "s1"])
        tail = Ring(f"{tag}_tail", sem, [bank(2), bank(3)], ["cols", "y"])
        hid = Ring(f"{tag}_hid", sem, [bank(4), bank(5)], [f"h{c}" for c in range(ECH // 4)])
        wts = Ring(f"{tag}_wts", sem, [bank(6), bank(7)], [f"w{b}" for b in range(NB)])
        pool_link = sem("pool_link")
        consts = sem("consts")
        xb_ready = sem("xb_ready")
        score_ready = sem("score_ready")
        sig_ready = sem("sig_ready")
        rows_ready = sem("rows_ready")
        hot_ready = sem("hot_ready")
        hihot_ready = sem("hihot_ready")
        pick_link = sem("pick_link")
        row_link = sem("row_link")
        passed = sem("passed")
        block = ctx.enter_context(nc.Block())

        @block.gpsimd
        def _(pool):
            pool.iota(iota_i[:, :], [[1, P]], base=0, channel_multiplier=0).then_inc(pool_link, 1)
            pool.wait_ge(pool_link, 1)
            pool.tensor_copy(iota[:, :], iota_i[:, :]).then_inc(consts, 1)
            pool.tensor_copy(iota_h[:, :], iota_i[:, :]).then_inc(consts, 1)
            pool.tensor_copy(identh[:, :], ident[:, :]).then_inc(consts, 1)
            pool.wait_ge(pool_link, 1)
            pool.tensor_copy(iota_w[:, :, :], iota_i[:, :].rearrange("p (n a) -> p n a", a=1).broadcast_to(
                [P, P, TB])).then_inc(consts, 1)
            with pool.Fori(0, TILES) as t:
                for b in range(NB):
                    pool.wait_ge(hihot_ready, t * NB + b + 1)
                    sigs = cols[:, 2, b * TB:(b + 1) * TB].rearrange("p (a j) -> p a j", a=1)
                    pool.tensor_tensor(hisig[:, b % 2, :, :], hihot[:, b % 2, :, :],
                                       sigs.broadcast_to([P, ECH, TB]), ALU.mult).then_inc(hot_ready, 1)

        @block.scalar
        def _(act):
            def hidden(t, s, c):
                hid.wait_full(act, t, f"h{c}")
                hid.take(act.activation(act_h[:, s, 4 * c:4 * c + 4, :], hid.bank(f"h{c}")[:, :].rearrange(
                    "p (c n) -> p c n", c=4), ACT.Gelu), f"h{c}")

            def norm(t, s):
                act.activation(nt[:, s, :, :], NT[:, :, bass.ds(t * P, P)], ACT.Copy)
                for k in range(KC):
                    ins = act.activation(xb[:, s, k, :], NT[:, k, bass.ds(t * P, P)], ACT.Identity,
                                         scale=bn[:, k, 0:1], bias=bn[:, k, 1:2])
                ins.then_inc(xb_ready, 1)

            def turn(i, last):
                for s in range(2):
                    t = i * 2 + s
                    if not (last and s == 1):
                        norm(t + 1, 1 - s)
                    act.wait_ge(score_ready, t + 1)
                    act.activation(sig[:, :], score[:, :, :].rearrange("p h k -> p (h k)"),
                                   ACT.Sigmoid).then_inc(sig_ready, 1)
                    tail.wait_full(act, t, "cols")
                    tail.take(act.activation(cols[:, :, :], tail.bank("cols")[:, :].bitcast(F16)[:, 0:3 * P].rearrange(
                        "p (c n) -> p c n", c=3), ACT.Copy), "cols")
                    if not (last and s == 1):
                        for c in range(ECH // 4):
                            hidden(t + 1, 1 - s, c)

            norm(0, 0)
            for c in range(ECH // 4):
                hidden(0, 0, c)
            with act.Fori(0, TILES // 2 - 1) as i:
                turn(i, False)
            turn(TILES // 2 - 1, True)

        @block.tensor
        def _(pe):
            for r in (sims, tail, hid, wts):
                r.start_empty(pe)
            experts_w.wait(pe)
            pe.wait_ge(consts, 4)

            def similarity(t, s):
                pe.wait_ge(xb_ready, t + 1)
                for n in range(2):
                    sims.claim(pe, t, f"s{n}")
                    for k in range(KC):
                        ins = pe.matmul(sims.bank(f"s{n}")[:, :], xb[:, s, k, :], wm[:, k, n * 512:(n + 1) * 512],
                                        start=(k == 0), stop=(k == KC - 1))
                    sims.filled(ins)

            def hidden(t, s, c):
                hid.claim(pe, t, f"h{c}")
                for j in range(4):
                    for k in range(KC):
                        e = 4 * c + j
                        ins = pe.matmul(hid.bank(f"h{c}")[:, j * P:(j + 1) * P], downT[:, k, e * P:(e + 1) * P],
                                        nt[:, s, k, :], start=(k == 0), stop=(k == KC - 1))
                hid.filled(ins)

            def turn(i, last):
                for s in range(2):
                    t = i * 2 + s
                    more = not (last and s == 1)
                    tail.claim(pe, t, "cols")
                    pe.wait_ge(rows_ready, t + 1)
                    for n in range(3):
                        ins = pe.transpose(tail.bank("cols")[:, :].bitcast(F16)[:, n * P:(n + 1) * P],
                                           rows[:, n, :, :].rearrange("p a n -> p (a n)"), identh[:, :])
                    tail.filled(ins)
                    if more:
                        similarity(t + 1, 1 - s)
                    for b in range(NB):
                        wts.claim(pe, t, f"w{b}")
                        pe.wait_ge(hot_ready, t * NB + b + 1)
                        for j in range(TB):
                            ins = pe.matmul(wts.bank(f"w{b}")[:, j * ECH:(j + 1) * ECH], lohot[:, b % 2, :, j],
                                            hisig[:, b % 2, :, j], start=True, stop=True)
                        wts.filled(ins)
                        if more:
                            hidden(t + 1, 1 - s, b)
                    tail.claim(pe, t, "y")
                    for b in (NB - 2, NB - 1):
                        wts.wait_taken(pe, t, f"w{b}")
                    for c in range(ECH):
                        ins = pe.matmul(tail.bank("y")[:, 0:D], act_h[:, s, c, :], up[:, c, :], start=(c == 0),
                                        stop=(c == ECH - 1))
                    tail.filled(ins)

            similarity(0, 0)
            for c in range(ECH // 4):
                hidden(0, 0, c)
            with pe.Fori(0, TILES // 2 - 1) as i:
                turn(i, False)
            turn(TILES // 2 - 1, True)

        @block.vector
        def _(dve):
            dve.wait_ge(consts, 4)
            PICK_LINKS, ROW_LINKS = 16, 2

            def picks(t):
                link = Tally(pick_link, t, PICK_LINKS)
                for n in range(2):
                    await_apart(dve, sims.full, t * 2 + n + 1, passed)
                    for h in range(PK_HEADS):
                        ins = dve.max(best[:, n, h, :], sims.bank(f"s{n}")[:, h * PK_KEYS:(h + 1) * PK_KEYS])
                    link.inc(ins)
                    await_apart(dve, link.sem, link.base + link.n, passed)
                    for h in range(PK_HEADS):
                        ins = dve.max_index(best_i[:, n, h, :], best[:, n, h, :],
                                            sims.bank(f"s{n}")[:, h * PK_KEYS:(h + 1) * PK_KEYS])
                    sims.take(ins, f"s{n}")
                for n in range(2):
                    sims.wait_taken(dve, t, f"s{n}")
                pair4 = pairs[:, :, :].rearrange("p h (i j) -> p h i j", i=PK_TOP)
                shape4 = [P, PK_HEADS, PK_TOP, PK_TOP]
                link.inc(dve.tensor_tensor(pair4,
                                           best[:, 0, :, :].rearrange("p h (i a) -> p h i a", a=1).broadcast_to(shape4),
                                           best[:, 1, :, :].rearrange("p h (a j) -> p h a j", a=1).broadcast_to(shape4),
                                           ALU.add))
                link.inc(dve.tensor_copy(best_f[:, :, :, :], best_i[:, :, :, :]))
                await_apart(dve, link.sem, link.base + link.n, passed)
                for h in range(PK_HEADS):
                    ins = dve.max(score[:, h, :], pairs[:, h, :])
                ins.then_inc(score_ready, 1)
                await_apart(dve, score_ready, t + 1, passed)
                for h in range(PK_HEADS):
                    ins = dve.max_index(pick[:, h, :], score[:, h, :], pairs[:, h, :])
                link.inc(ins)
                link.wait(dve)
                pk = pick[:, :, :].rearrange("p h k -> p (h k)")
                dve.tensor_scalar(half_i[:, 0, :], pk, 3, None, ALU.logical_shift_right)
                link.inc(dve.tensor_scalar(half_i[:, 1, :], pk, PK_TOP - 1, None, ALU.bitwise_and))
                link.wait(dve)
                link.inc(dve.tensor_copy(half_f[:, :, :], half_i[:, :, :]))
                link.wait(dve)
                wide = [P, 2 * PICKS, PK_TOP]
                link.inc(dve.tensor_tensor(hot[:, :, :, :].rearrange("p n k a -> p (n k) a"),
                                           half_f[:, :, :].rearrange("p n (k a) -> p (n k) a", a=1).broadcast_to(wide),
                                           iota[:, 0:PK_TOP].rearrange("p (a b) -> p a b", a=1).broadcast_to(wide),
                                           ALU.is_equal))
                link.wait(dve)
                for n in range(2):
                    h4 = hot[:, n, :, :].rearrange("p (h k) a -> p h k a", h=PK_HEADS)
                    ins = dve.tensor_tensor(h4, h4, best_f[:, n, :, :].rearrange(
                        "p h (b a) -> p h b a", b=1).broadcast_to([P, PK_HEADS, PK_TOP, PK_TOP]), ALU.mult)
                link.inc(ins)
                link.wait(dve)
                link.inc(dve.tensor_reduce(key[:, :, :], hot[:, :, :, :], AX_X, ALU.add))
                link.wait(dve)
                link.inc(dve.scalar_tensor_tensor(eid[:, :], key[:, 0, :], float(PK_KEYS), key[:, 1, :], ALU.mult,
                                                  ALU.add))
                link.wait(dve)
                link.inc(dve.tensor_copy(eid_i[:, :], eid[:, :]))
                link.wait(dve)
                dve.tensor_scalar(ehl_i[:, 0, :], eid_i[:, :], P - 1, None, ALU.bitwise_and)
                link.inc(dve.tensor_scalar(ehl_i[:, 1, :], eid_i[:, :], 7, None, ALU.logical_shift_right))
                link.wait(dve)
                dve.tensor_copy(rows[:, 0:2, 0, :], ehl_i[:, :, :])
                link.inc(dve.tensor_copy(rows[:, 0:2, 1, :], ehl_i[:, :, :]))
                dve.wait_ge(sig_ready, t + 1)
                link.inc(dve.tensor_scalar(sig[:, :], sig[:, :], LO_SCALE, None, ALU.mult))
                link.wait(dve)
                link.inc(dve.tensor_copy(rows[:, 2, 0, :], sig[:, :]))
                link.wait(dve)
                dve.tensor_tensor(rows[:, 2, 1, :], sig[:, :], rows[:, 2, 0, :], ALU.subtract).then_inc(rows_ready, 1)
                link.close()

            def weigh(t, s, b):
                wts.wait_full(dve, t, f"w{b}")
                hv = act_h[:, s, :, b * TB:(b + 1) * TB]
                wts.take(dve.tensor_tensor(hv, hv, wts.bank(f"w{b}")[:, :].rearrange("p (j c) -> p c j", c=ECH),
                                           ALU.mult), f"w{b}")

            def experts(t, s):
                tail.wait_taken(dve, t, "cols")
                for b in range(NB):
                    if b == 2 and not at_start(t, 1):
                        read_sums(t - 1)
                    if b >= 2:
                        wts.wait_full(dve, t, f"w{b - 2}")
                    blk = slice(b * TB, (b + 1) * TB)

                    def spread(n, width):
                        return cols[:, n, blk].rearrange("p (a j) -> p a j", a=1).broadcast_to([P, width, TB])

                    dve.tensor_tensor(lohot[:, b % 2, :, :], iota_w[:, :, :], spread(0, P), ALU.is_equal)
                    dve.tensor_tensor(hihot[:, b % 2, :, :], iota_w[:, 0:ECH, :], spread(1, ECH),
                                      ALU.is_equal).then_inc(hihot_ready, 1)
                    if b == 0:
                        hid.wait_taken(dve, t, f"h{ECH // 4 - 2}")
                        hid.wait_taken(dve, t, f"h{ECH // 4 - 1}")
                    if b:
                        weigh(t, s, b - 1)
                weigh(t, s, NB - 1)

            def read_sums(t):
                tail.wait_full(dve, t, "y")
                tail.take(dve.scalar_tensor_tensor(new[:, :].rearrange("p (a n) -> p a n", a=1),
                                                   tail.bank("y")[:, 0:D].rearrange("p (a n) -> p a n", a=1),
                                                   1.0 / LO_SCALE, X[:, bass.ds(t, 1), :], ALU.mult, ALU.add), "y")

            def finish(t):
                link = Tally(row_link, t, ROW_LINKS)
                tail.wait_taken(dve, t, "y")
                finish_rows(dve, keep, link, t, new, bst, mv)
                link.close()

            def turn(i, last):
                for s in range(2):
                    t = i * 2 + s
                    experts(t, s)
                    if not (last and s == 1):
                        picks(t + 1)
                    if not at_start(t, 1):
                        finish(t - 1)

            picks(0)
            turn(0, False)
            with dve.Fori(1, TILES // 2 - 1) as i:
                turn(i, False)
            turn(TILES // 2 - 1, True)
            read_sums(TILES - 1)
            finish(TILES - 1)


MOE = 8


def top2_experts(nc, keep, w, out):
    tag = "mo"
    with ExitStack() as ctx:
        def sb(name, shape, dt=F32):
            return ctx.enter_context(nc.sbuf_tensor(f"{tag}_{name}", shape, dt))

        def sem(name):
            return keep["semaphore"](f"{tag}_{name}")

        X, MV, ident = keep["X"], keep["MV"], keep["ident"]
        we, gate = w.at["we"], w.at["gate"]
        iota_i = sb("iota_i", [P, MOE], I32)
        iota = sb("iota", [P, MOE])
        rstd = sb("rstd", [P, TILES])
        xn = sb("xn", [P, G, D])
        xnT = sb("xnT", [P, 2, KC, GT])
        lg = sb("lg", [P, G, MOE])
        top = sb("top", [P, G, 8])
        top_i = sb("top_i", [P, G, 8], U32)
        top_f = sb("top_f", [P, G, 2])
        e2 = sb("e2", [P, G])
        den = sb("den", [P, G])
        pair = sb("pair", [P, 2, G])
        wf = sb("wf", [P, 2, G, MOE])
        wf2 = sb("wf2", [P, G, MOE])
        acc = sb("acc", [P, 2, G, D])
        banks = [ctx.enter_context(nc.psum_tensor(f"{tag}_ps{b}", [P, 512], F32)) for b in range(8)]
        first = Ring(f"{tag}_first", sem, banks[0:4], ["xt0", "xt1", "lg0", "lg1"])
        main = Ring(f"{tag}_main", sem, banks[4:8], [f"e{q}_{u}" for u in range(G) for q in range(MOE // 2)])
        pool_link = sem("pool_link")
        consts = sem("consts")
        rstd_sq = sem("rstd_sq")
        setup = sem("setup")
        xn_ready = sem("xn_ready")
        diff_ready = sem("diff_ready")
        e2_ready = sem("e2_ready")
        acc_ready = sem("acc_ready")
        stored = sem("stored")
        passed = sem("passed")
        gate_link = sem("gate_link")
        sum_link = sem("sum_link")
        out_v = out.rearrange("t p d -> p t d")
        block = ctx.enter_context(nc.Block())

        @block.sync
        def _(sp):
            with sp.Fori(0, GROUPS) as g:
                sp.wait_ge(acc_ready, g + 1)
                sp.dma_start(out_v[:, bass.ds(g * G, G), :], acc[:, 1, :, :]).then_inc(stored, 16)
            sp.wait_ge(stored, 16 * (GROUPS + 1))

        @block.gpsimd
        def _(pool):
            pool.iota(iota_i[:, :], [[1, MOE]], base=0, channel_multiplier=0).then_inc(pool_link, 1)
            pool.wait_ge(pool_link, 1)
            pool.tensor_copy(iota[:, :], iota_i[:, :]).then_inc(consts, 1)

        @block.scalar
        def _(act):
            def columns_and_gate(g, s):
                for n in range(2):
                    first.wait_full(act, g, f"xt{n}")
                    first.take(act.activation(xnT[:, s, :, n * 256:(n + 1) * 256],
                                              first.bank(f"xt{n}")[:, :].rearrange("p (k n) -> p k n", k=KC),
                                              ACT.Copy), f"xt{n}")
                act.wait_ge(diff_ready, g + 1)
                act.activation(e2[:, :], e2[:, :], ACT.Exp).then_inc(e2_ready, 1)

            def turn(g, s, more):
                if more:
                    columns_and_gate(g + 1, 1 - s)

            layer_norm_scale(act, None, keep, rstd, rstd_sq, None)
            columns_and_gate(0, 0)
            turns(act, turn)

        @block.tensor
        def _(pe):
            for r in (first, main):
                r.start_empty(pe)
            w.wait(pe)

            def columns(g):
                for n in range(2):
                    first.claim(pe, g, f"xt{n}")
                    for u in (2 * n, 2 * n + 1):
                        pe.wait_ge(xn_ready, g * G + u + 1)
                        for k in range(KC):
                            at = k * 256 + (u % 2) * P
                            ins = pe.transpose(first.bank(f"xt{n}")[:, at:at + P], xn[:, u, k * P:(k + 1) * P],
                                               ident[:, :])
                    first.filled(ins)

            def gate_logits(g, s):
                for n in range(2):
                    first.wait_taken(pe, g, f"xt{n}")
                for n in range(2):
                    first.claim(pe, g, f"lg{n}")
                    for u in (2 * n, 2 * n + 1):
                        for k in range(KC):
                            ins = pe.matmul(first.bank(f"lg{n}")[:, (u % 2) * MOE:(u % 2 + 1) * MOE],
                                            xnT[:, s, k, u * P:(u + 1) * P], gate[:, k, :], start=(k == 0),
                                            stop=(k == KC - 1))
                    first.filled(ins)

            def turn(g, s, more):
                for u in range(G):
                    if u == 1 and more:
                        columns(g + 1)
                    if u == 2 and more:
                        gate_logits(g + 1, 1 - s)
                    for q in range(MOE // 2):
                        main.claim(pe, g, f"e{q}_{u}")
                        for k in range(KC):
                            ins = pe.matmul(main.bank(f"e{q}_{u}")[:, :], xnT[:, s, k, u * P:(u + 1) * P],
                                            we[:, k, 2 * q:2 * q + 2, :].rearrange("p e n -> p (e n)"),
                                            start=(k == 0), stop=(k == KC - 1))
                        main.filled(ins)

            columns(0)
            gate_logits(0, 0)
            turns(pe, turn)

        @block.vector
        def _(dve):
            layer_norm_scale(None, dve, keep, rstd, rstd_sq, setup)
            dve.wait_ge(consts, 1)
            dve.sem_inc(stored, 16)

            def norm(g):
                if not (isinstance(g, int) and g == 0):
                    first.wait_full(dve, g - 1, "xt1")
                for u in range(G):
                    t = g * G + u
                    dve.tensor_scalar(xn[:, u:u + 1, :], X[:, bass.ds(t, 1), :], MV[:, bass.ds(t, 1), 0],
                                      rstd[:, bass.ds(t, 1)], ALU.subtract, ALU.mult).then_inc(xn_ready, 1)

            def weights(g, s):
                link = Tally(gate_link, g, 11)
                for n in range(2):
                    first.wait_full(dve, g, f"lg{n}")
                    first.take(dve.tensor_copy(lg[:, 2 * n:2 * n + 2, :], first.bank(f"lg{n}")[:, 0:2 * MOE].rearrange(
                        "p (u e) -> p u e", u=2)), f"lg{n}")
                for n in range(2):
                    use = f"lg{n}"
                    m = first.at[use]
                    await_apart(dve, first.taken[m % first.n_banks],
                                g * (first.per // first.n_banks) + m // first.n_banks + 2, passed)
                for u in range(G):
                    ins = dve.max(top[:, u, :], lg[:, u, :])
                link.inc(ins)
                await_apart(dve, link.sem, link.base + link.n, passed)
                for u in range(G):
                    ins = dve.max_index(top_i[:, u, :], top[:, u, :], lg[:, u, :])
                link.inc(ins)
                dve.tensor_tensor(e2[:, :], top[:, :, 1], top[:, :, 0], ALU.subtract).then_inc(diff_ready, 1)
                link.wait(dve)
                link.inc(dve.tensor_copy(top_f[:, :, :], top_i[:, :, 0:2]))
                dve.wait_ge(e2_ready, g + 1)
                link.inc(dve.tensor_scalar(den[:, :], e2[:, :], 1.0, None, ALU.add))
                link.wait(dve)
                link.inc(dve.reciprocal(pair[:, 0, :], den[:, :]))
                link.wait(dve)
                link.inc(dve.tensor_tensor(pair[:, 1, :], e2[:, :], pair[:, 0, :], ALU.mult))
                link.wait(dve)
                shape = [P, G, MOE]
                place = iota[:, :].rearrange("p (a e) -> p a e", a=1).broadcast_to(shape)
                for n, dst in ((0, wf[:, s, :, :]), (1, wf2[:, :, :])):
                    link.inc(dve.tensor_tensor(dst, top_f[:, :, n:n + 1].broadcast_to(shape), place,
                                               ALU.is_equal))
                    link.wait(dve)
                    link.inc(dve.tensor_tensor(dst, dst, pair[:, n, :].rearrange(
                        "p (u a) -> p u a", a=1).broadcast_to(shape), ALU.mult))
                    link.wait(dve)
                link.inc(dve.tensor_tensor(wf[:, s, :, :], wf[:, s, :, :], wf2[:, :, :], ALU.add))
                link.wait(dve)
                link.close()

            def turn(g, s, more):
                link = Tally(sum_link, g, 4 * G)
                if more:
                    norm(g + 1)
                dve.wait_ge(stored, g * 16 + 16)
                for u in range(G):
                    t = g * G + u
                    if u == 2 and more:
                        weights(g + 1, 1 - s)
                    for q in range(MOE // 2):
                        main.wait_full(dve, g, f"e{q}_{u}")
                        for j in range(2):
                            e = 2 * q + j
                            src = main.bank(f"e{q}_{u}")[:, j * D:(j + 1) * D].rearrange("p (a n) -> p a n", a=1)
                            prev = X[:, bass.ds(t, 1), :] if e == 0 else acc[:, (e + 1) % 2, u:u + 1, :]
                            ins = dve.scalar_tensor_tensor(acc[:, e % 2, u:u + 1, :], src, wf[:, s, u, e:e + 1], prev,
                                                           ALU.mult, ALU.add)
                            if j == 0:
                                link.inc(ins)
                                link.wait(dve)
                            else:
                                main.take(ins, f"e{q}_{u}")
                                main.wait_taken(dve, g, f"e{q}_{u}")
                dve.sem_inc(acc_ready, 1)
                link.close()

            norm(0)
            weights(0, 0)
            turns(dve, turn)


def build(nc, a, out):
    with ExitStack() as ctx:
        def sb(name, shape, dt=F32):
            return ctx.enter_context(nc.sbuf_tensor(name, shape, dt))

        keep = {"X": sb("X", [P, TILES, D]), "MV": sb("MV", [P, TILES, 2]), "ident": sb("ident", [P, P]),
                "eps": sb("eps", [P, 1]), "tau": sb("tau", [P, TILES]), "quarter": sb("quarter", [P, 1]),
                "delta": a["delta"]}
        X, MV, ident = keep["X"], keep["MV"], keep["ident"]
        in_use = []

        def semaphore(name):
            in_use.append(nc.alloc_semaphore(name))
            return in_use[-1]

        def clear_semaphores():
            nc.clear_and_free_semaphores(in_use)
            nc.all_engine_barrier()
            in_use.clear()

        keep["semaphore"] = semaphore
        def chunked(v):
            return v.rearrange("(k p) n -> p k n", p=P)

        def attention_weights(n):
            w = {k: a[f"L{n}_{k}"] for k in ("wq", "wk", "wv", "wo", "bq", "bk", "bv", "bo")}
            return Ahead(nc, f"a{n}", "left", [
                ("wq", [P, KC, HC * P], F32, chunked(w["wq"])), ("wk", [P, KC, HC * P], F32, chunked(w["wk"])),
                ("wv", [P, KC, D], F32, chunked(w["wv"])), ("bq", [P, HC], F32, w["bq"]), ("bk", [P, HC], F32, w["bk"]),
                ("bv", [P, D], F32, w["bv"]), ("wo", [P, KC, D], F32, chunked(w["wo"])), ("bo", [P, D], F32, w["bo"])])

        att_w = attention_weights(0)
        with ExitStack() as c2:
            x_loaded = [c2.enter_context(nc.semaphore(f"x_loaded{q}")) for q in range(4)]
            c_loaded = c2.enter_context(nc.semaphore("c_loaded"))
            id_zero = c2.enter_context(nc.semaphore("id_zero"))
            start_link = c2.enter_context(nc.semaphore("start_link"))
            bst = c2.enter_context(nc.sbuf_tensor("bst0", [P, TILES, 6], F32))
            block = c2.enter_context(nc.Block())

            @block.sync
            def _(sp):
                for q in range(4):
                    part = slice(q * TILES // 4, (q + 1) * TILES // 4)
                    sp.dma_start(X[:, part, :], a["x"].rearrange("t p d -> p t d")[:, part, :]).then_inc(
                        x_loaded[q], 16)
                att_w.load(sp)
                sp.dma_start(keep["tau"][:, :], a["tau"]).then_inc(c_loaded, 16)
                sp.dma_start(keep["quarter"][:, :], a["quarter"]).then_inc(c_loaded, 16)
                sp.wait_ge(c_loaded, 32)

            @block.gpsimd
            def _(pool):
                pool.memset(ident[:, :], 0.0).then_inc(id_zero, 1)
                pool.memset(keep["eps"][:, :], LN_EPS)
                pool.wait_ge(id_zero, 1)
                pool.affine_select(out=ident[:, :], in_=ident[:, :], compare_op=ALU.not_equal, fill=1.0,
                                   base=0, pattern=[[-1, P]], channel_multiplier=1)

            @block.vector
            def _(dve):
                for t in range(TILES):
                    if t % (TILES // 4) == 0:
                        dve.wait_ge(x_loaded[t // (TILES // 4)], 16)
                    ins = dve.bn_stats(bst[:, t, :], X[:, t, :])
                ins.then_inc(start_link, 1)
                dve.wait_ge(start_link, 1)
                for t in range(TILES):
                    dve.bn_aggr(MV[:, t, :], bst[:, t, :])

        ffn_w = Ahead(nc, "sh", "right", [
            ("gate", [P, KC, EXPERTS], F32, chunked(a["L0_gate"])), ("w1", [P, KC, HID], F32, chunked(a["L0_Ws1"])),
            ("b1", [P, HCH], F32, a["L0_bs1"]), ("w2", [P, HCH, D], F32, chunked(a["L0_Ws2"])),
            ("b2", [P, D], F32, a["L0_bs2"])])
        attention(nc, keep, "a0", att_w, a["ctxT"], ffn_w)
        att_w.free()

        row_dram = nc.dram_tensor("row_dram", (TOKENS, ROW), F32, kind="Internal").ap()
        sum_dram = nc.dram_tensor("sum_dram", (TOKENS, D), F32, kind="Internal").ap()
        att_w = attention_weights(1)
        with ExitStack() as c2:
            idx = c2.enter_context(nc.sbuf_tensor("idx", [P, EXPERTS, SLOTS], U32))
            probs = c2.enter_context(nc.sbuf_tensor("gate_probs", [P, TILES, EXPERTS], F32))
            shared_ffn(nc, keep, ffn_w, probs, row_dram, sum_dram, att_w)
            ffn_w.free()
            expert_w = {k: a[f"L0_{k}"] for k in ("W1", "W2", "b1", "b2")}
            held = {n: c2.enter_context(nc.sbuf_tensor(f"ro_{n}", shape, F32)) for n, shape in (
                ("w1", [P, 2, KC, HID]), ("w2", [P, 2, HCH, D]), ("b1", [P, 2, HCH]), ("b2", [P, 2, D]))}
            held["loaded"] = [semaphore(f"ro_w_loaded{s}") for s in range(2)]

            def first_loads(sp):
                for s in range(2):
                    load_expert(sp, expert_w, held, s, s)

            choose_tokens(nc, keep, probs, idx, first_loads)
            routed_ffn(nc, keep, expert_w, held, idx, row_dram, sum_dram)
        clear_semaphores()

        bit_w = Ahead(nc, "bw", "right", [
            (n, [P, KC * INNER], F32, a[f"L1_w_{n}"].rearrange("(k p) n -> p k n", p=P))
            for n in ("gate", "up", "down")])
        attention(nc, keep, "a1", att_w, a["ctxT"], bit_w)
        att_w.free()
        win_w = Ahead(nc, "ww", "left", [
            ("wa", [P, KC, D], F32, chunked(a["L2_W_a"])), ("wc", [P, 2 * KC, D], F32, chunked(a["L2_W_c"])),
            ("pt", [P, TILES], F32, a["L2_pt"]), ("len", [P, TILES], I32, a["L2_len"])])
        bit_ffn(nc, keep, bit_w, win_w)
        bit_w.free()
        keys_w = Ahead(nc, "kw", "right", [
            ("wq", [P, 2 * PK_HEADS, D], F32, a["L2_w_q"].rearrange("(c p) n -> p c n", p=P)),
            ("keys", [P, 2 * PK_HEADS, PK_KEYS], F32, a["L2_keys"]), ("gamma", [P, KC], F32, a["L2_gamma"]),
            ("beta", [P, KC], F32, a["L2_beta"])])
        windowed_attention(nc, keep, win_w, a["ctxT"], a["ctx"], keys_w)
        win_w.free()
        clear_semaphores()

        experts_w = Ahead(nc, "ew", "left", [
            ("downT", [P, KC, PK_EXPERTS], F32, chunked(a["L2_downT"][:, 0:PK_EXPERTS])),
            ("up", [P, ECH, D], F32, a["L2_up"][0:PK_EXPERTS, :].rearrange("(c p) n -> p c n", p=P))])
        product_key_experts(nc, keep, keys_w, experts_w)
        experts_w.free()
        att_w = attention_weights(3)
        moe_w = Ahead(nc, "mw", "right", [("gate", [P, KC, MOE], F32, chunked(a["L3_gate"])),
                                 ("we", [P, KC, MOE, D], F32, a["L3_we"])])
        attention(nc, keep, "a3", att_w, a["ctxT"], moe_w, load_first=True)
        att_w.free()
        top2_experts(nc, keep, moe_w, out)


def lay_out(i):
    import numpy as np

    def rows(v):
        return np.ascontiguousarray(np.broadcast_to(np.asarray(v).reshape(1, -1), (P, np.asarray(v).size)))

    def padded(wt):
        o = np.zeros((wt.shape[0], HC * 4, 32), np.float32)
        o[:, :, 0:DK] = wt.reshape(wt.shape[0], HC * 4, DK)
        return o.reshape(wt.shape[0], HC * P)

    def turned(w):
        return np.ascontiguousarray(np.asarray(w).T)

    a = {"x": np.asarray(i["x"]), "ctxT": turned(np.asarray(i["ctx_1024"]).reshape(TILES * P, D))}
    a["tau"] = rows(i["condB_tau"])
    a["delta"] = np.asarray(i["fside_BxS2_0"]).reshape(1, -1)
    qr = np.zeros((P, 1), np.float32)
    qr[DK::32, :] = 1.0 / DK ** 0.5
    a["quarter"] = qr
    for n in (0, 1, 3):
        for m in "qk":
            a[f"L{n}_w{m}"] = padded(turned(i[f"L{n}_xcond_W{m}"]))
            a[f"L{n}_b{m}"] = turned(padded(np.asarray(i[f"L{n}_xcond_b{m}"]).reshape(1, -1)).reshape(HC, P))
        for m in "vo":
            a[f"L{n}_w{m}"] = turned(i[f"L{n}_xcond_W{m}"])
            a[f"L{n}_b{m}"] = rows(i[f"L{n}_xcond_b{m}"])
    for m in ("gate", "Ws1", "Ws2", "W1", "W2"):
        a[f"L0_{m}"] = np.asarray(i[f"L0_ffn_{m}"])
    a["L0_bs1"] = turned(np.asarray(i["L0_ffn_bs1"]).reshape(HCH, P))
    a["L0_bs2"] = rows(i["L0_ffn_bs2"])
    a["L0_b1"] = np.ascontiguousarray(np.asarray(i["L0_ffn_b1"]).reshape(EXPERTS, HCH, P).transpose(2, 0, 1))
    a["ctx"] = np.asarray(i["ctx_1024"]).reshape(TILES * P, D)
    for m in ("w_gate", "w_up", "w_down"):
        a[f"L1_{m}"] = turned(i[f"L1_ffn_{m}"])
    a["L2_W_a"] = np.asarray(i["L2_xcond_W_a"])
    a["L2_W_c"] = turned(i["L2_xcond_W_c"])
    a["L2_pt"] = rows(i["condB_pt"])
    a["L2_len"] = rows(i["_lenS2"])
    a["L2_w_q"] = np.asarray(i["L2_ffn_w_q"])
    a["L2_keys"] = np.ascontiguousarray(np.asarray(i["L2_ffn_keys_p"]).transpose(3, 2, 0, 1)).reshape(
        PK_DIM, 2 * PK_HEADS, PK_KEYS)
    a["L2_gamma"] = turned(np.asarray(i["L2_ffn_bn_gamma"]).reshape(KC, P))
    a["L2_beta"] = turned(np.asarray(i["L2_ffn_bn_beta"]).reshape(KC, P))
    a["L2_downT"] = turned(i["L2_ffn_down"])
    a["L2_up"] = np.asarray(i["L2_ffn_up"])
    a["L3_gate"] = turned(i["L3_ffn_gate_w"])
    a["L3_we"] = np.ascontiguousarray(np.asarray(i["L3_ffn_expert_w"]).transpose(2, 0, 1).reshape(
        KC, P, MOE, D).transpose(1, 0, 2, 3))
    a["L0_b2"] = np.ascontiguousarray(np.broadcast_to(np.asarray(i["L0_ffn_b2"])[None], (P, EXPERTS, D)))
    return a


def kernel(**inputs):
    import numpy as np
    import concourse.bacc as bacc
    from concourse.bass_utils import run_bass_kernel_spmd

    arrays = lay_out(inputs)
    nc = bacc.Bacc("TRN2", target_bir_lowering=False, num_devices=1)
    a = {n: nc.dram_tensor(f"in_{n}", v.shape, mybir.dt.from_np(v.dtype), kind="ExternalInput").ap()
         for n, v in arrays.items()}
    out = nc.dram_tensor("out_0", (TILES, P, D), F32, kind="ExternalOutput").ap()
    build(nc, a, out)
    r = run_bass_kernel_spmd(nc, [{f"in_{n}": v for n, v in arrays.items()}], core_ids=[0])
    return r.results[0]["out_0"]
```
